# Optimizing a Trainium2 kernel written in Bass

```python
import numpy as np
import jax
import jax.numpy as jnp

def _softmax(x, axis=-1):
    return jax.nn.softmax(x, axis=axis)

def _gelu(x):
    return jax.nn.gelu(x, approximate=True)

def _silu(x):
    return jax.nn.silu(x)

def _sigmoid(x):
    return jax.nn.sigmoid(x)

def _layernorm(x, axis=-1, eps=1e-05):
    m = jnp.mean(x, axis=axis, keepdims=True)
    v = jnp.var(x, axis=axis, keepdims=True)
    return (x - m) / jnp.sqrt(v + eps)

def _scatter_add(tgt, idx, src, axis=0):
    return tgt.at[idx].add(src)

def _segment_sum(src, seg, n):
    return jax.ops.segment_sum(src, seg, n)
kernel_name = 'mk_flamingo_gated_d1_seqx_r4_42ddb7'

def setup_inputs(seed: int=0):
    np.random.seed(seed)
    _w = jnp.asarray

    def _rec_inputs():
        import jax
        import jax.numpy as jnp
        _rk = jax.random.key(seed)
        x = 7.22e-05 + 1 * jax.random.normal(jax.random.fold_in(_rk, 1), (2, 512, 1024), jnp.float32)
        _lenS = 512 - jax.random.randint(jax.random.fold_in(_rk, 7), (2,), 0, max(1, 512 // 4) + 1, jnp.int32)
        _lenS2 = 1024 - jax.random.randint(jax.random.fold_in(_rk, 8), (2,), 0, max(1, 1024 // 4) + 1, jnp.int32)
        _ctx_4096P = jax.random.normal(jax.random.fold_in(_rk, 11), (2, 16, 1024), jnp.float32)
        _ctx_4096c = jax.random.dirichlet(jax.random.fold_in(_rk, 511), 0.3 * jnp.ones((16,), jnp.float32), (2, 1024))
        _ctx_4096t = jnp.einsum('bsk,bkd->bsd', _ctx_4096c, _ctx_4096P)
        _ctx_4096t = _ctx_4096t * jax.lax.rsqrt(jnp.mean(jnp.square(_ctx_4096t)) + 1e-12) * 0.953939
        ctx_4096 = 4.13588e-05 + 0.999923 * (_ctx_4096t + 0.3 * jax.random.normal(jax.random.fold_in(_rk, 611), (2, 1024, 1024), jnp.float32))
        fside_Bx32xSxS2_0 = 1.74963e-06 + 0.0200011 * jax.random.normal(jax.random.fold_in(_rk, 13), (2, 32, 512, 1024), jnp.float32)
        _validS = jnp.arange(512)[None, :] < _lenS[:, None]
        _validS2 = jnp.arange(1024)[None, :] < _lenS2[:, None]
        _causal = jnp.tril(jnp.ones((512, 512), dtype=bool))
        mask_BxSxS2_bk0 = jnp.logical_not(jnp.broadcast_to(_validS2[:, None, :], (2, 512, 1024)))
        _g = jax.random.normal(jax.random.fold_in(_rk, 9001), (2, 1), jnp.float32)
        _g = jnp.sign(_g) * jnp.maximum(jnp.abs(_g), 1.0) + (_g == 0) * 1.0
        g_xattn = _g[0]
        g_ffn = _g[1]
        return (x, ctx_4096, fside_Bx32xSxS2_0, mask_BxSxS2_bk0, g_xattn, g_ffn)
    x, ctx_4096, fside_Bx32xSxS2_0, mask_BxSxS2_bk0, g_xattn, g_ffn = _rec_inputs()

    def _L0_xattn_setup():
        import jax, jax.numpy as jnp
        import numpy as np
        B, S, D, H, DH = (2, 256, 1024, 32, 128)
        key = jax.random.key(seed)
        ks = jax.random.split(key, 7)
        hidden_q = jax.random.normal(ks[0], (B, S, D), dtype=jnp.float32)
        hidden_kv = jax.random.normal(ks[1], (B, S, D), dtype=jnp.float32)
        attention_mask = jnp.tril(jnp.ones((B, S, S), dtype=bool))
        position_bias = jax.random.normal(ks[2], (B, H, S, S), dtype=jnp.float32) * 0.02
        Wq = jax.random.normal(ks[3], (D, H * DH), dtype=jnp.float32) * 0.02
        Wk = jax.random.normal(ks[4], (D, H * DH), dtype=jnp.float32) * 0.02
        Wv = jax.random.normal(ks[5], (D, H * DH), dtype=jnp.float32) * 0.02
        Wo = jax.random.normal(ks[6], (H * DH, D), dtype=jnp.float32) * 0.02
        return {'hidden_q': hidden_q, 'hidden_kv': hidden_kv, 'attention_mask': attention_mask, 'position_bias': position_bias, 'Wq': Wq, 'Wk': Wk, 'Wv': Wv, 'Wo': Wo}
    _L0_xattn_all = _L0_xattn_setup()
    _L0_xattn_in = {k: v for k, v in _L0_xattn_all.items() if k in ('Wq', 'Wk', 'Wv', 'Wo')}
    del _L0_xattn_all

    def _L0_ffn_setup():
        import jax, jax.numpy as jnp
        import numpy as np
        HID, BOT, RDIM, NSLOT, K, VB = (1024, 64, 48, 256, 8, 64)
        TAU_LOW, TAU_HIGH, EARLY_EXIT = (0.5, 2.0, 0.05)

        def _uncertainty(h, Wu1, bu1, Wu2, bu2):
            var = jnp.var(h, axis=-1)
            log_var = jnp.log1p(var)
            norm_var = log_var / (jnp.mean(log_var) + 1e-06)
            learned = (jax.nn.gelu(h @ Wu1.T + bu1) @ Wu2.T + bu2)[..., 0]
            return jnp.clip(norm_var * 0.5 + jax.nn.sigmoid(learned) * 2.5, 0.0, 5.0)
        key = jax.random.key(seed)
        ks = jax.random.split(key, 12)
        B, S = (2, 512)
        return {'hidden_states': jax.random.normal(ks[0], (B, S, HID), dtype=jnp.float32), 'Wq': jax.random.normal(ks[1], (BOT, HID), dtype=jnp.float32) / np.sqrt(HID), 'Wr': jax.random.normal(ks[2], (RDIM, BOT), dtype=jnp.float32) / np.sqrt(BOT), 'aux_keys': jax.random.normal(ks[3], (NSLOT, BOT), dtype=jnp.float32) * 0.01, 'aux_values': jax.random.normal(ks[4], (NSLOT, HID), dtype=jnp.float32) * 0.02, 'Wvd': jax.random.normal(ks[5], (VB, HID), dtype=jnp.float32) * 0.1 / np.sqrt(HID), 'Wvu': jax.random.normal(ks[6], (HID, VB), dtype=jnp.float32) * 0.1 / np.sqrt(VB), 'Wu1': jax.random.normal(ks[7], (HID // 4, HID), dtype=jnp.float32) / np.sqrt(HID), 'bu1': jnp.zeros((HID // 4,), dtype=jnp.float32), 'Wu2': jax.random.normal(ks[8], (1, HID // 4), dtype=jnp.float32) * 0.01, 'bu2': jnp.zeros((1,), dtype=jnp.float32), 'gate_w1': jnp.float32(0.5), 'gate_bias': jnp.float32(-1.0), 'log_rel': jnp.zeros((NSLOT,), dtype=jnp.float32)}
    _L0_ffn_all = _L0_ffn_setup()
    _L0_ffn_in = {k: v for k, v in _L0_ffn_all.items() if k in ('Wq', 'Wr', 'aux_keys', 'aux_values', 'Wvd', 'Wvu', 'Wu1', 'bu1', 'Wu2', 'bu2', 'gate_w1', 'gate_bias', 'log_rel')}
    del _L0_ffn_all
    return {'x': x, 'ctx_4096': ctx_4096, 'fside_Bx32xSxS2_0': fside_Bx32xSxS2_0, 'mask_BxSxS2_bk0': mask_BxSxS2_bk0, 'g_xattn': g_xattn, 'g_ffn': g_ffn, 'L0_xattn_Wq': _L0_xattn_in['Wq'], 'L0_xattn_Wk': _L0_xattn_in['Wk'], 'L0_xattn_Wv': _L0_xattn_in['Wv'], 'L0_xattn_Wo': _L0_xattn_in['Wo'], 'L0_ffn_Wq': _L0_ffn_in['Wq'], 'L0_ffn_Wr': _L0_ffn_in['Wr'], 'L0_ffn_aux_keys': _L0_ffn_in['aux_keys'], 'L0_ffn_aux_values': _L0_ffn_in['aux_values'], 'L0_ffn_Wvd': _L0_ffn_in['Wvd'], 'L0_ffn_Wvu': _L0_ffn_in['Wvu'], 'L0_ffn_Wu1': _L0_ffn_in['Wu1'], 'L0_ffn_bu1': _L0_ffn_in['bu1'], 'L0_ffn_Wu2': _L0_ffn_in['Wu2'], 'L0_ffn_bu2': _L0_ffn_in['bu2'], 'L0_ffn_gate_w1': _L0_ffn_in['gate_w1'], 'L0_ffn_gate_bias': _L0_ffn_in['gate_bias'], 'L0_ffn_log_rel': _L0_ffn_in['log_rel']}

def reference(x, ctx_4096, fside_Bx32xSxS2_0, mask_BxSxS2_bk0, g_xattn, g_ffn, L0_xattn_Wq, L0_xattn_Wk, L0_xattn_Wv, L0_xattn_Wo, L0_ffn_Wq, L0_ffn_Wr, L0_ffn_aux_keys, L0_ffn_aux_values, L0_ffn_Wvd, L0_ffn_Wvu, L0_ffn_Wu1, L0_ffn_bu1, L0_ffn_Wu2, L0_ffn_bu2, L0_ffn_gate_w1, L0_ffn_gate_bias, L0_ffn_log_rel):
    import jax
    import jax.numpy as jnp

    def _L0_xattn_ref(hidden_q, hidden_kv, attention_mask, position_bias, Wq, Wk, Wv, Wo):
        import jax, jax.numpy as jnp
        import numpy as np
        B, S, D, H, DH = (2, 256, 1024, 32, 128)
        b, lq, _ = hidden_q.shape
        lk = hidden_kv.shape[1]
        h, dh = (H, DH)
        q = (hidden_q @ Wq).reshape(b, lq, h, dh)
        k = (hidden_kv @ Wk).reshape(b, lk, h, dh)
        v = (hidden_kv @ Wv).reshape(b, lk, h, dh)
        scale = 1.0 / jnp.sqrt(jnp.asarray(dh, dtype=q.dtype))
        score = jnp.einsum('bqhd,bkhd->bhqk', q, k) * scale + position_bias
        mask = attention_mask[:, None, :, :]
        neg_inf = jnp.asarray(-jnp.inf, dtype=score.dtype)
        score = jnp.where(mask, score, neg_inf)
        probs = jax.nn.softmax(score, axis=-1)
        probs = jnp.where(mask, probs, jnp.asarray(0, dtype=probs.dtype))
        ctx = jnp.einsum('bhqk,bkhd->bqhd', probs, v).reshape(b, lq, h * dh)
        return ctx @ Wo

    def _L0_ffn_ref(hidden_states, Wq, Wr, aux_keys, aux_values, Wvd, Wvu, Wu1, bu1, Wu2, bu2, gate_w1, gate_bias, log_rel):
        import jax, jax.numpy as jnp
        import numpy as np
        HID, BOT, RDIM, NSLOT, K, VB = (1024, 64, 48, 256, 8, 64)
        TAU_LOW, TAU_HIGH, EARLY_EXIT = (0.5, 2.0, 0.05)

        def _uncertainty(h, Wu1, bu1, Wu2, bu2):
            var = jnp.var(h, axis=-1)
            log_var = jnp.log1p(var)
            norm_var = log_var / (jnp.mean(log_var) + 1e-06)
            learned = (jax.nn.gelu(h @ Wu1.T + bu1) @ Wu2.T + bu2)[..., 0]
            return jnp.clip(norm_var * 0.5 + jax.nn.sigmoid(learned) * 2.5, 0.0, 5.0)
        query = hidden_states @ Wq.T
        rq = query @ Wr.T
        rk = aux_keys @ Wr.T
        router_scores = jnp.einsum('bsr,nr->bsn', rq, rk) / np.sqrt(RDIM) + log_rel
        top_scores, top_idx = jax.lax.top_k(router_scores, K)
        sel_keys = aux_keys[top_idx]
        attn = jnp.einsum('bsd,bskd->bsk', query, sel_keys) / np.sqrt(BOT) + log_rel[top_idx]
        w = jax.nn.softmax(attn, axis=-1)
        sel_vals = aux_values[top_idx]
        aux_out = jnp.einsum('bsk,bskh->bsh', w, sel_vals)
        aux_out = aux_out @ Wvd.T @ Wvu.T
        u = _uncertainty(hidden_states, Wu1, bu1, Wu2, bu2)
        u_norm = jnp.clip((u - TAU_LOW) / (TAU_HIGH - TAU_LOW), 0.0, 1.0)
        gate = jax.nn.sigmoid(gate_w1 * u_norm + gate_bias)
        gate = jnp.where(gate < EARLY_EXIT, 0.0, gate)
        return hidden_states + gate[..., None] * aux_out
    x = x + jnp.tanh(g_xattn[0]) * _L0_xattn_ref(_layernorm(x, axis=-1), ctx_4096, mask_BxSxS2_bk0, fside_Bx32xSxS2_0, L0_xattn_Wq, L0_xattn_Wk, L0_xattn_Wv, L0_xattn_Wo)
    x = x + jnp.tanh(g_ffn[0]) * _L0_ffn_ref(_layernorm(x, axis=-1), L0_ffn_Wq, L0_ffn_Wr, L0_ffn_aux_keys, L0_ffn_aux_values, L0_ffn_Wvd, L0_ffn_Wvu, L0_ffn_Wu1, L0_ffn_bu1, L0_ffn_Wu2, L0_ffn_bu2, L0_ffn_gate_w1, L0_ffn_gate_bias, L0_ffn_log_rel)
    return x

_drawn_inputs = setup_inputs


def setup_inputs(seed=0):
    import zlib

    import numpy as np

    out = dict(_drawn_inputs(seed))
    spreads = {'L0_ffn_bu1': (0.0, 2.0), 'L0_ffn_log_rel': (0.0, 0.8)}
    factors = {'fside_Bx32xSxS2_0': 30.562,
     'L0_ffn_Wq': 8.0,
     'L0_ffn_Wr': 8.0,
     'L0_ffn_aux_keys': 8.0,
     'L0_ffn_aux_values': 8.0,
     'L0_ffn_Wvd': 8.0,
     'L0_ffn_Wvu': 8.0,
     'L0_ffn_Wu1': 22.553,
     'L0_ffn_Wu2': 22.87}
    for name, (base, spread) in spreads.items():
        noise = np.random.default_rng([zlib.crc32(name.encode()), seed]).standard_normal(out[name].shape)
        drawn = base * np.exp(spread * noise) if base else spread * noise
        out[name] = jnp.asarray(drawn.astype(out[name].dtype))
    for name, factor in factors.items():
        out[name] = (out[name] * factor).astype(out[name].dtype)
    return out
```

```python
from contextlib import ExitStack

import concourse.bass as bass
from concourse import mybir

ALU = mybir.AluOpType
ACT = mybir.ActivationFunctionType
F32 = mybir.dt.float32
F32R = mybir.dt.float32r
BF16 = mybir.dt.bfloat16
U8 = mybir.dt.uint8

P = 128
BANK = 512
ONE = 1
DMA = 16
EPS = 1e-5
MASKED = -3e38
NO_SCORE = 1.5e38
LEAST_SUM = 1e-30
HI, LO = 0, 1
PASSES = ((HI, HI), (HI, LO), (LO, HI))
HEADS_PER_TURN = 2


def attention(nc, x, ctx_in, bias, mask, g_xattn, Wq, Wk, Wv, Wo, x1, ident):
    B, S, D = x.shape
    SK = ctx_in.shape[1]
    H = bias.shape[1]
    DH = Wq.shape[1] // H
    NC = D // P
    QT = S // P
    KT = SK // P
    KH = SK // BANK
    YG = QT * (D // BANK)
    SCALE = float(DH) ** -0.5
    TURNS = (H - 2) // HEADS_PER_TURN
    assert DH == P and S == BANK and KH == 2 and QT == 4 and NC == 8 and KT == 8
    assert (H - 2) % HEADS_PER_TURN == 0
    GROUPS = 2 * (KT + QT)

    x_t = x.rearrange("b (t p) d -> b p t d", p=P)
    x1_t = x1.rearrange("b (t p) d -> b p t d", p=P)
    ctx_t = ctx_in.rearrange("b (t p) d -> (b t) p d", p=P)
    mask_t = mask.rearrange("b (t p) k -> b p t k", p=P)
    bias_t = bias.rearrange("b h (t p) k -> (b h t) p k", p=P)
    w_dram = {m: w.rearrange("(c p) n -> p c n", p=P) for m, w in (("q", Wq), ("k", Wk), ("v", Wv))}

    with ExitStack() as stack:
        def sb(name, shape, dt):
            return stack.enter_context(nc.sbuf_tensor(name, shape, dt))

        def sem(name):
            return stack.enter_context(nc.semaphore(name))

        ctxT = sb("ctxT", [P, 2, NC, SK], F32R)
        xnT = sb("xnT", [P, 2, NC, S], F32R)
        y = sb("y", [P, QT, D], F32)
        hide = sb("hide", [P, QT, SK], BF16)
        raw = sb("raw", [P, 2, D], F32)
        w = {m: sb("w" + m, [P, 2, D], F32R) for m in "qkvo"}
        kT = sb("kT", [P, 2, SK], F32R)
        qT = sb("qT", [P, 2, S], F32R)
        vT = sb("vT", [P, BANK], F32)
        v = sb("v", [P, 2, KT, DH], F32R)
        bias_sb = sb("bias_sb", [P, 2, SK], F32)
        probs = sb("probs", [P, QT, SK], F32)
        pT = sb("pT", [P, 2, 2, S], F32R)
        oT = sb("oT", [P, 2, S], F32R)
        negmax = sb("negmax", [P, QT], F32)
        rowsum = sb("rowsum", [P, QT], F32)
        safe_sum = sb("safe_sum", [P, QT], F32)
        recip = sb("recip", [P, QT], F32)
        coef = sb("coef", [P, QT], F32)
        gate = sb("gate", [P, 2], F32)
        eps = sb("eps", [P, 1], F32)
        stats = sb("stats", [P, QT, 2, 6], F32)
        moments = sb("moments", [P, QT, 2], F32)
        std = sb("std", [P, QT], F32)
        rstd = sb("rstd", [P, QT], F32)

        def bank(name, n=1):
            return stack.enter_context(nc.psum_tensor(name, [P, n * BANK], F32))

        score_ps = bank("score_ps", 2)
        proj_ps = [bank("proj_ps0"), bank("proj_ps1")]
        turn_ps = [bank("turn_ps0"), bank("turn_ps1")]
        head_ps = bank("head_ps")
        out_ps = bank("out_ps")
        K_BANK = proj_ps
        Q_BANK = proj_ps[0]
        V_BANK = [proj_ps[1], head_ps]
        START_BANKS = [turn_ps[0][:], turn_ps[1][:], score_ps[:, 0:BANK], score_ps[:, BANK:]]

        weight_in = {m: sem("weight_in_" + m) for m in "qkvo"}
        weight_hi = {m: sem("weight_hi_" + m) for m in "qkvo"}
        weight_lo = {m: sem("weight_lo_" + m) for m in "qkvo"}
        bias_in = [sem("bias_in0"), sem("bias_in1")]
        bias_masked = sem("bias_masked")
        stage_in = [sem(f"stage_in{i}") for i in range(4)]
        x_in = sem("x_in")
        g_in = sem("g_in")
        y_out = sem("y_out")
        ident_done = sem("ident_done")
        gate_done = sem("gate_done")
        eps_done = sem("eps_done")
        hide_done = sem("hide_done")
        stats_done = sem("stats_done")
        moments_done = sem("moments_done")
        std_done = sem("std_done")
        rstd_done = sem("rstd_done")
        xn_done = sem("xn_done")
        start_ps = sem("start_ps")
        start_hi = sem("start_hi")
        start_lo = sem("start_lo")
        kq_ps = sem("kq_ps")
        kq_hi = sem("kq_hi")
        kq_lo = sem("kq_lo")
        v_ps = sem("v_ps")
        vT_sb = sem("vT_sb")
        v_turned = sem("v_turned")
        v_hi = sem("v_hi")
        v_lo = sem("v_lo")
        score_done = sem("score_done")
        score_sb = sem("score_sb")
        exp_done = sem("exp_done")
        coef_step = sem("coef_step")
        p_turned = sem("p_turned")
        pT_hi = sem("pT_hi")
        pT_lo = sem("pT_lo")
        pv_done = sem("pv_done")
        oT_hi = sem("oT_hi")
        oT_lo = sem("oT_lo")
        y_ps = sem("y_ps")
        y_sb = sem("y_sb")

        WSLOT = {"k": 0, "v": 0, "q": 1, "o": 1}

        def heads(eng, begin, head, end):
            with eng.Fori(0, B) as b:
                begin(b, b * H)
                head(b * H, True, False)
                with eng.Fori(0, TURNS) as turn:
                    for u in range(HEADS_PER_TURN):
                        head(b * H + turn * HEADS_PER_TURN + (u + 1), False, False)
                head(b * H + (H - 1), False, True)
                end(b, b * H + (H - 1))

        def head_in_batch(b_g, g):
            return g - b_g

        went_on = {"sp": sem("went_on_sp"), "dve": sem("went_on_dve")}
        started_by = {
            "pe": (start_ps, kq_ps, v_ps, v_turned, score_done, p_turned, pv_done, y_ps),
            "act": (start_hi, kq_hi, vT_sb, v_hi, exp_done, pT_hi, oT_hi, std_done, *weight_hi.values()),
            "dve": (start_lo, kq_lo, v_lo, score_sb, coef_step, pT_lo, oT_lo, y_sb, hide_done, stats_done,
                    moments_done, rstd_done, xn_done, *weight_lo.values()),
            "pool": (bias_masked,),
        }

        def start_counts(eng, name):
            for s in started_by[name]:
                eng.sem_inc(s, ONE)

        block = stack.enter_context(nc.Block())

        @block.sync
        def _(sp):
            sp.dma_start(gate[:, 0:1], g_xattn.rearrange("(a n) -> a n", a=1).to_broadcast((P, 1))).then_inc(g_in, DMA)
            sp.dma_start(y[0:1, 0, 0:1], g_xattn.rearrange("(a n) -> a n", a=1)).then_inc(y_out, DMA)

            def load_weight(m, h, *split):
                for before, count in split:
                    sp.wait_ge(weight_lo[before], ONE + count)
                    sp.sem_inc(went_on["sp"], 1)
                dst = raw[:, WSLOT[m], :]
                if m == "o":
                    src = Wo[bass.ds(h * DH, DH), :]
                else:
                    src = w_dram[m][:, :, bass.ds(h * DH, DH)]
                    dst = dst.rearrange("p (c n) -> p c n", n=DH)
                sp.dma_start(dst, src).then_inc(weight_in[m], DMA)

            def load_bias(g, qt):
                sp.dma_start(bias_sb[:, qt % 2, :],
                             bias_t[bass.ds(g * QT + qt, 1), :, :].rearrange("a p k -> p (a k)")).then_inc(bias_in[qt % 2], DMA)

            def begin(b, g):
                load_weight("k", 0, ("v", g))
                for j in range(KT + 1):
                    if j < 4:
                        sp.wait_ge(p_turned, ONE + KT * g)
                    elif j == 4:
                        sp.wait_ge(hide_done, ONE + b + 1)
                    else:
                        sp.wait_ge(start_ps, ONE + GROUPS * b + 2 * (j - 4))
                    if j == 0:
                        sp.sem_inc(went_on["sp"], 1)
                        sp.dma_start(probs[:, 0, :].bitcast(U8).rearrange("p (t k) -> p t k", t=QT),
                                     mask_t[bass.ds(b, 1), :, :, :].rearrange("a p t k -> p (a t) k")).then_inc(stage_in[0], DMA)
                    else:
                        sp.dma_start(probs[:, j % 4, :],
                                     ctx_t[bass.ds(b * KT + (j - 1), 1), :, :].rearrange("a p d -> p (a d)")).then_inc(stage_in[j % 4], DMA)
                    if j == 3:
                        sp.wait_ge(y_out, DMA * b + DMA)
                        sp.sem_inc(went_on["sp"], 1)
                        sp.dma_start(y[:, :, :], x_t[bass.ds(b, 1), :, :, :].rearrange("a p t d -> p (a t) d")).then_inc(x_in, DMA)
                load_weight("q", 0, ("o", g))
                load_weight("v", 0, ("k", g + 1))
                sp.wait_ge(score_sb, ONE + QT * g)
                for qt in range(2):
                    load_bias(g, qt)

            def head(g, h, last):
                if not last:
                    load_weight("k", h + 1, ("v", g + 1))
                    load_weight("q", h + 1, ("q", g + 1), ("o", g))
                for qt in range(2, QT):
                    sp.wait_ge(score_sb, ONE + QT * g + qt - 1)
                    load_bias(g, qt)
                if not last:
                    load_weight("v", h + 1, ("k", g + 2))
                load_weight("o", h, ("q", g + 1 if last else g + 2), ("o", g))
                if not last:
                    for qt in range(2):
                        sp.wait_ge(score_sb, ONE + QT * g + QT - 1 + qt)
                        load_bias(g + 1, qt)

            with sp.Fori(0, B) as b:
                begin(b, b * H)
                head(b * H, 0, False)
                with sp.Fori(0, TURNS) as turn:
                    for u in range(HEADS_PER_TURN):
                        h = turn * HEADS_PER_TURN + (u + 1)
                        head(b * H + h, h, False)
                head(b * H + (H - 1), H - 1, True)
                sp.wait_ge(y_sb, ONE + YG * H * b + YG * H)
                sp.dma_start(x1_t[bass.ds(b, 1), :, :, :].rearrange("a p t d -> p (a t) d"), y[:, :, :]).then_inc(y_out, DMA)
            sp.wait_ge(y_out, DMA * B + DMA)

        @block.gpsimd
        def _(pool):
            start_counts(pool, "pool")
            nc.gpsimd.memset(ident[:], 0.0).then_inc(ident_done, 1)
            pool.wait_ge(ident_done, 1)
            nc.gpsimd.affine_select(out=ident[:], in_=ident[:], compare_op=ALU.not_equal, fill=1.0,
                                    base=0, pattern=[[-1, P]], channel_multiplier=1).then_inc(ident_done, 1)

            def begin(b, g):
                pool.wait_ge(hide_done, ONE + b + 1)

            def head(g, first, last):
                for qt in range(QT):
                    pool.wait_ge(bias_in[qt % 2], DMA * 2 * g + DMA * (qt // 2 + 1))
                    nc.gpsimd.tensor_tensor(bias_sb[:, qt % 2, :], bias_sb[:, qt % 2, :], hide[:, qt, :],
                                            ALU.add).then_inc(bias_masked, 1)

            heads(pool, begin, head, lambda b, g: None)

        @block.tensor
        def _(pe):
            start_counts(pe, "pe")

            def turn_blocks(out, blocks):
                for n, blk in enumerate(blocks):
                    last = pe.transpose(out[:, n * P:(n + 1) * P], blk, ident[:])
                return last

            def project(out, m, src, cols, n):
                c, (a, b) = n // 3, PASSES[n % 3]
                return pe.matmul(out[:, 0:BANK], w[m][:, a, c * DH:(c + 1) * DH], src[:, b, c, cols],
                                 start=(n == 0), stop=(n == 3 * NC - 1))

            def next_kq(g, n):
                part, n = n // (3 * NC), n % (3 * NC)
                if n == 0 and part == 0:
                    pe.wait_ge(weight_lo["k"], ONE + g + 2)
                    pe.wait_ge(kq_lo, ONE + 3 * g + 3)
                if n == 0 and part == 1:
                    pe.wait_ge(vT_sb, ONE + 2 * g + 1)
                if n == 0 and part == 2:
                    pe.wait_ge(weight_lo["q"], ONE + g + 2)
                    pe.wait_ge(kq_lo, ONE + 3 * g + 4)
                if part < 2:
                    mm = project(K_BANK[part], "k", ctxT, slice(part * BANK, (part + 1) * BANK), n)
                else:
                    mm = project(Q_BANK, "q", xnT, slice(0, S), n)
                if n == 3 * NC - 1:
                    mm.then_inc(kq_ps, 1)

            def begin(b, g):
                def group(k):
                    tile, half = k // 2, k % 2
                    if k < 2:
                        pe.wait_ge(pT_lo, ONE + KT * g)
                    elif k < 4:
                        pe.wait_ge(score_sb, ONE + QT * g)
                    else:
                        pe.wait_ge(start_lo, ONE + GROUPS * b + k - 3)
                    slot = (tile + 1) % 4
                    if tile < KT:
                        loads = 3 if slot == 0 else 2
                        pe.wait_ge(stage_in[slot], DMA * loads * b + DMA * ((tile + 1) // 4 + 1))
                    else:
                        pe.wait_ge(xn_done, ONE + QT * b + tile - KT + 1)
                    turn_blocks(START_BANKS[k % 4], [probs[:, slot, (4 * half + c) * P:(4 * half + c + 1) * P]
                                                     for c in range(4)]).then_inc(start_ps, 1)

                def k_chunk(part, c):
                    if c == 0:
                        pe.wait_ge(start_lo, ONE + GROUPS * b + 8 * (part + 1))
                        if part == 0:
                            pe.wait_ge(weight_lo["k"], ONE + g + 1)
                            pe.wait_ge(kq_lo, ONE + 3 * g)
                        else:
                            pe.wait_ge(vT_sb, ONE + 2 * g)
                    for n in range(3 * c, 3 * c + 3):
                        mm = project(K_BANK[part], "k", ctxT, slice(part * BANK, (part + 1) * BANK), n)
                    if c == NC - 1:
                        mm.then_inc(kq_ps, 1)

                for k in range(8):
                    group(k)
                for n in range(8):
                    group(8 + n)
                    k_chunk(0, n)
                for n in range(8):
                    group(16 + n)
                    k_chunk(1, n)
                pe.wait_ge(start_lo, ONE + GROUPS * b + GROUPS)
                pe.wait_ge(weight_lo["q"], ONE + g + 1)
                pe.wait_ge(kq_lo, ONE + 3 * g + 1)
                for n in range(3 * NC):
                    mm = project(Q_BANK, "q", xnT, slice(0, S), n)
                mm.then_inc(kq_ps, 1)

            def out_group(g, i):
                if i == 0:
                    pe.wait_ge(oT_lo, ONE + g + 1)
                    pe.wait_ge(weight_lo["o"], ONE + g + 1)
                pe.wait_ge(y_sb, ONE + YG * g + i)
                qt, n = i // 2, i % 2
                for a, b in PASSES:
                    mm = pe.matmul(out_ps[:, :], oT[:, a, qt * P:(qt + 1) * P],
                                   w["o"][:, b, n * BANK:(n + 1) * BANK], start=(a, b) == PASSES[0], stop=(a, b) == PASSES[-1])
                mm.then_inc(y_ps, 1)

            def turn_v(g, half):
                pe.wait_ge(vT_sb, ONE + 2 * g + half + 1)
                pe.wait_ge(pT_lo, ONE + KT * g)
                turn_blocks(turn_ps[half], [vT[:, k * P:(k + 1) * P] for k in range(4)]).then_inc(v_turned, 1)

            def turn_p(g, kt):
                if kt == 0:
                    pe.wait_ge(exp_done, ONE + QT * g + QT)
                if kt < 2:
                    pe.wait_ge(v_lo, ONE + 2 * g + kt + 1)
                else:
                    pe.wait_ge(pT_lo, ONE + KT * g + kt - 1)
                turn_blocks(turn_ps[kt % 2], [probs[:, qt, kt * P:(kt + 1) * P] for qt in range(QT)]).then_inc(p_turned, 1)

            def pv(g, kt):
                pe.wait_ge(pT_lo, ONE + KT * g + kt + 1)
                if kt == 0:
                    pe.wait_ge(v_lo, ONE + 2 * g + 2)
                    pe.wait_ge(vT_sb, ONE + 2 * g + 2)
                for a, b in PASSES:
                    mm = pe.matmul(head_ps[:, :], v[:, a, kt, :], pT[:, kt % 2, b, :],
                                   start=(kt == 0 and (a, b) == PASSES[0]), stop=(kt == KT - 1 and (a, b) == PASSES[-1]))
                mm.then_inc(pv_done, 1)

            def head(g, first, last):
                for i in range(8):
                    half, qt, sh = i // 4, i // 2, i % 2
                    if i == 0:
                        pe.wait_ge(weight_lo["v"], ONE + g + 1)
                        pe.wait_ge(kq_lo, ONE + 3 * g + 2)
                    if i == 4:
                        pe.wait_ge(oT_lo, ONE + g)
                    for n in range(6 * (i % 4), 6 * (i % 4) + 6):
                        mm = project(V_BANK[half], "v", ctxT, slice(half * BANK, (half + 1) * BANK), n)
                    if i % 4 == 3:
                        mm.then_inc(v_ps, 1)
                    if i == 0:
                        pe.wait_ge(kq_lo, ONE + 3 * g + 3)
                    if sh == 0:
                        pe.wait_ge(score_sb, ONE + QT * g + qt)
                    for a, b in PASSES:
                        mm = pe.matmul(score_ps[:, sh * BANK:(sh + 1) * BANK], qT[:, a, qt * P:(qt + 1) * P],
                                       kT[:, b, sh * BANK:(sh + 1) * BANK], start=(a, b) == PASSES[0], stop=(a, b) == PASSES[-1])
                    if sh == 1:
                        mm.then_inc(score_done, 1)
                    if not first:
                        out_group(g - 1, i)
                    if i == 5:
                        turn_v(g, 0)
                turn_v(g, 1)

                def fill(i):
                    if not last:
                        for n in range(9 * i, 9 * i + 9):
                            next_kq(g, n)

                fill(0)
                turn_p(g, 0)
                turn_p(g, 1)
                for kt in range(KT):
                    if kt + 1 < KT:
                        fill(kt + 1)
                    pv(g, kt)
                    if kt + 2 < KT:
                        turn_p(g, kt + 2)

            def end(b, g):
                for i in range(YG):
                    out_group(g, i)

            pe.wait_ge(ident_done, 2)
            heads(pe, begin, head, end)


        @block.scalar
        def _(act):
            start_counts(act, "act")
            act.wait_ge(g_in, DMA)
            nc.scalar.activation(gate[:, 1:2], gate[:, 0:1], ACT.Tanh).then_inc(gate_done, 1)
            act.wait_ge(eps_done, 1)

            def copy(out, in_, scale=1.0):
                return nc.scalar.activation(out, in_, ACT.Copy, scale=scale)

            def weight(m, g, free):
                act.wait_ge(weight_in[m], DMA * g + DMA)
                act.wait_ge(free[0], ONE + free[1])
                copy(w[m][:, HI, :], raw[:, WSLOT[m], :]).then_inc(weight_hi[m], 1)

            def kq(g, part):
                act.wait_ge(kq_ps, ONE + 3 * g + part + 1)
                act.wait_ge(score_done, ONE + QT * g)
                if part < 2:
                    ins = copy(kT[:, HI, part * BANK:(part + 1) * BANK], K_BANK[part][:, :])
                else:
                    ins = copy(qT[:, HI, :], Q_BANK[:, :], SCALE)
                ins.then_inc(kq_hi, 1)

            def begin(b, g):
                def group(k):
                    act.wait_ge(start_ps, ONE + GROUPS * b + k + 1)
                    if k == 0:
                        act.wait_ge(v_ps, ONE + 2 * g)
                        act.wait_ge(kq_ps, ONE + 3 * g)
                    tile, c = k // 2, 4 * (k % 2)
                    dst = (ctxT[:, HI, c:c + 4, tile * P:(tile + 1) * P] if tile < KT
                           else xnT[:, HI, c:c + 4, (tile - KT) * P:(tile - KT + 1) * P])
                    copy(dst, START_BANKS[k % 4].rearrange("p (c n) -> p c n", n=P)).then_inc(start_hi, 1)

                weight("k", g, (kq_ps, 3 * g))
                for k in range(8):
                    group(k)
                act.wait_ge(moments_done, ONE + QT * b + QT)
                nc.scalar.activation(std[:, :], moments[:, :, 1], ACT.Sqrt, bias=eps[:, 0:1]).then_inc(std_done, 1)
                for k in range(8, 16):
                    group(k)
                weight("q", g, (kq_ps, 3 * g))
                kq(g, 0)
                for k in range(16, 24):
                    group(k)
                weight("v", g, (v_ps, 2 * g))
                kq(g, 1)
                kq(g, 2)

            def head_out(g):
                act.wait_ge(pv_done, ONE + KT * g + KT)
                act.wait_ge(y_ps, ONE + YG * g)
                copy(oT[:, HI, :], head_ps[:, :]).then_inc(oT_hi, 1)

            def exp(g, qt):
                act.wait_ge(score_sb, ONE + QT * g + qt + 1)
                if qt == 0:
                    act.wait_ge(coef_step, ONE + 3 * g)
                nc.scalar.activation(probs[:, qt, :], probs[:, qt, :], ACT.Exp, bias=negmax[:, qt:qt + 1], scale=-1.0,
                                     accum_out=rowsum[:, qt:qt + 1]).then_inc(exp_done, 1)

            def vT_half(g, half):
                act.wait_ge(v_ps, ONE + 2 * g + half + 1)
                act.wait_ge(v_turned, ONE + 2 * g + half)
                copy(vT[:, :], V_BANK[half][:, :]).then_inc(vT_sb, 1)

            def v_half(g, half):
                act.wait_ge(v_turned, ONE + 2 * g + half + 1)
                act.wait_ge(pv_done, ONE + KT * g)
                copy(v[:, HI, 4 * half:4 * half + 4, :].rearrange("p t d -> p (t d)"), turn_ps[half][:, :]).then_inc(v_hi, 1)

            def pT_tile(g, kt):
                act.wait_ge(p_turned, ONE + KT * g + kt + 1)
                act.wait_ge(pv_done, ONE + KT * g + max(kt - 1, 0))
                copy(pT[:, kt % 2, HI, :], turn_ps[kt % 2][:, :]).then_inc(pT_hi, 1)

            def head(g, first, last):
                if not first:
                    head_out(g - 1)
                if not last:
                    weight("k", g + 1, (kq_ps, 3 * g + 2))
                exp(g, 0)
                vT_half(g, 0)
                exp(g, 1)
                if not last:
                    weight("q", g + 1, (kq_ps, 3 * g + 3))
                exp(g, 2)
                v_half(g, 0)
                vT_half(g, 1)
                exp(g, 3)
                v_half(g, 1)
                pT_tile(g, 0)
                pT_tile(g, 1)
                if not last:
                    weight("v", g + 1, (v_ps, 2 * g + 2))
                pT_tile(g, 2)
                if not last:
                    kq(g + 1, 0)
                pT_tile(g, 3)
                weight("o", g, (y_ps, YG * g))
                pT_tile(g, 4)
                pT_tile(g, 5)
                if not last:
                    kq(g + 1, 1)
                pT_tile(g, 6)
                pT_tile(g, 7)
                if not last:
                    kq(g + 1, 2)

            heads(act, begin, head, lambda b, g: head_out(g))

        @block.vector
        def _(dve):
            start_counts(dve, "dve")

            def rest(out, in_, hi, scale=1.0):
                if scale == 1.0:
                    return nc.vector.tensor_tensor(out, in_, hi.bitcast(F32), ALU.subtract)
                return nc.vector.scalar_tensor_tensor(out=out, in0=in_, scalar=scale, in1=hi.bitcast(F32),
                                                      op0=ALU.mult, op1=ALU.subtract)

            def weight(m, g):
                dve.wait_ge(weight_hi[m], ONE + g + 1)
                rest(w[m][:, LO, :], raw[:, WSLOT[m], :], w[m][:, HI, :]).then_inc(weight_lo[m], 1)

            def kq(g, part):
                dve.wait_ge(kq_hi, ONE + 3 * g + part + 1)
                if part < 2:
                    cols = slice(part * BANK, (part + 1) * BANK)
                    ins = rest(kT[:, LO, cols], K_BANK[part][:, :], kT[:, HI, cols])
                else:
                    ins = rest(qT[:, LO, :], Q_BANK[:, :], qT[:, HI, :], SCALE)
                ins.then_inc(kq_lo, 1)

            def begin(b, g):
                def group(k):
                    dve.wait_ge(start_hi, ONE + GROUPS * b + k + 1)
                    tile, c = k // 2, 4 * (k % 2)
                    dst = (ctxT[:, :, c:c + 4, tile * P:(tile + 1) * P] if tile < KT
                           else xnT[:, :, c:c + 4, (tile - KT) * P:(tile - KT + 1) * P])
                    rest(dst[:, LO], START_BANKS[k % 4].rearrange("p (c n) -> p c n", n=P), dst[:, HI]).then_inc(start_lo, 1)

                weight("k", g)
                dve.wait_ge(stage_in[0], DMA * 3 * b + DMA)
                dve.wait_ge(bias_masked, ONE + QT * g)
                nc.vector.tensor_scalar(hide[:, :, :], probs[:, 0, :].bitcast(U8).rearrange("p (t k) -> p t k", t=QT),
                                        0.0, MASKED, ALU.is_equal, ALU.mult).then_inc(hide_done, 1)
                for t in range(QT):
                    group(2 * t)
                    group(2 * t + 1)
                    dve.wait_ge(x_in, DMA * b + DMA)
                    for half in range(2):
                        nc.vector.bn_stats(stats[:, t, half, :], y[:, t, half * BANK:(half + 1) * BANK]).then_inc(stats_done, 1)
                    dve.wait_ge(stats_done, ONE + 2 * QT * b + 2 * t + 2)
                    dve.sem_inc(went_on["dve"], 1)
                    nc.vector.bn_aggr(moments[:, t, :], stats[:, t, :, :]).then_inc(moments_done, 1)
                group(8)
                group(9)
                dve.wait_ge(std_done, ONE + b + 1)
                nc.vector.reciprocal(rstd[:, :], std[:, :]).then_inc(rstd_done, 1)
                dve.wait_ge(rstd_done, ONE + b + 1)
                for t in range(QT):
                    dve.wait_ge(start_ps, ONE + GROUPS * b + 2 * (t + 5))
                    nc.vector.tensor_scalar(probs[:, (t + 1) % 4, :], y[:, t, :], moments[:, t, 0:1], rstd[:, t:t + 1],
                                            ALU.subtract, ALU.mult).then_inc(xn_done, 1)
                    if t < QT - 1:
                        group(10 + 2 * t)
                        group(11 + 2 * t)
                weight("q", g)
                kq(g, 0)
                for k in range(16, 24):
                    group(k)
                weight("v", g)
                kq(g, 1)
                kq(g, 2)

            def head_out(g):
                dve.wait_ge(oT_hi, ONE + g + 1)
                rest(oT[:, LO, :], head_ps[:, :], oT[:, HI, :]).then_inc(oT_lo, 1)

            def score(g, qt):
                if qt == 0:
                    dve.wait_ge(p_turned, ONE + KT * g)
                dve.wait_ge(score_done, ONE + QT * g + qt + 1)
                dve.wait_ge(bias_masked, ONE + QT * g + qt + 1)
                dve.sem_inc(went_on["dve"], 1)
                nc.vector.tensor_tensor_reduce(probs[:, qt, :], score_ps[:, :], bias_sb[:, qt % 2, :], -1.0, NO_SCORE,
                                               ALU.add, ALU.min, negmax[:, qt:qt + 1]).then_inc(score_sb, 1)

            def v_half(g, half):
                dve.wait_ge(v_hi, ONE + 2 * g + half + 1)
                rest(v[:, LO, 4 * half:4 * half + 4, :].rearrange("p t d -> p (t d)"), turn_ps[half][:, :],
                     v[:, HI, 4 * half:4 * half + 4, :].rearrange("p t d -> p (t d)")).then_inc(v_lo, 1)

            def pT_tile(g, kt):
                dve.wait_ge(pT_hi, ONE + KT * g + kt + 1)
                rest(pT[:, kt % 2, LO, :], turn_ps[kt % 2][:, :], pT[:, kt % 2, HI, :]).then_inc(pT_lo, 1)

            def make_coef(g):
                dve.wait_ge(exp_done, ONE + QT * g + QT)
                nc.vector.tensor_scalar(safe_sum[:, :], rowsum[:, :], LEAST_SUM, None, ALU.max).then_inc(coef_step, 1)
                dve.wait_ge(coef_step, ONE + 3 * g + 1)
                nc.vector.reciprocal(recip[:, :], safe_sum[:, :]).then_inc(coef_step, 1)
                dve.wait_ge(coef_step, ONE + 3 * g + 2)
                nc.vector.tensor_scalar(coef[:, :], recip[:, :], gate[:, 1:2], None, ALU.mult).then_inc(coef_step, 1)

            def add_out(g, i):
                if i == 0:
                    dve.wait_ge(coef_step, ONE + 3 * g + 3)
                dve.wait_ge(y_ps, ONE + YG * g + i + 1)
                qt, cols = i // 2, slice((i % 2) * BANK, (i % 2 + 1) * BANK)
                nc.vector.scalar_tensor_tensor(out=y[:, qt, cols], in0=out_ps[:, :], scalar=coef[:, qt:qt + 1],
                                               in1=y[:, qt, cols], op0=ALU.mult, op1=ALU.add).then_inc(y_sb, 1)

            def head(g, first, last):
                if not first:
                    head_out(g - 1)
                for i in range(8):
                    if i % 2 == 1:
                        score(g, i // 2)
                    if not first:
                        add_out(g - 1, i)
                    if i == 1 and not last:
                        weight("k", g + 1)
                    if i == 3 and not last:
                        weight("q", g + 1)
                    if i == 5:
                        v_half(g, 0)
                v_half(g, 1)
                make_coef(g)
                pT_tile(g, 0)
                pT_tile(g, 1)
                if not last:
                    weight("v", g + 1)
                pT_tile(g, 2)
                if not last:
                    kq(g + 1, 0)
                pT_tile(g, 3)
                weight("o", g)
                pT_tile(g, 4)
                pT_tile(g, 5)
                if not last:
                    kq(g + 1, 1)
                pT_tile(g, 6)
                pT_tile(g, 7)
                if not last:
                    kq(g + 1, 2)

            def end(b, g):
                head_out(g)
                for i in range(YG):
                    add_out(g, i)

            nc.vector.memset(eps[:, :], EPS).then_inc(eps_done, 1)
            dve.wait_ge(gate_done, 1)
            heads(dve, begin, head, end)


def feed_forward(nc, x1, out, ident, g_ffn, Wq, Wr, aux_keys, aux_values, Wvd, Wvu, Wu1, bu1, Wu2, bu2,
                 gate_w1, gate_bias, log_rel):
    B, S, D = x1.shape
    BOT, RDIM, NSLOT, VB, NU = Wq.shape[0], Wr.shape[0], aux_keys.shape[0], Wvd.shape[0], Wu1.shape[0]
    NC = D // P
    T = B * S // P
    HALVES = T * P // BANK
    TH = T // HALVES
    UT = NU // P
    ST = NSLOT // P
    TAU_LOW, TAU_HIGH, EARLY_EXIT = 0.5, 2.0, 0.05
    assert ST == 2 and UT == 2 and TH == 4 and 2 * NSLOT == BANK and BOT == VB == 64 and RDIM <= 64

    x1_t = x1.rearrange("b (t p) d -> p (b t) d", p=P)
    out_t = out.rearrange("b (t p) d -> p (b t) d", p=P)

    with ExitStack() as stack:
        def sb(name, shape, dt=F32):
            return stack.enter_context(nc.sbuf_tensor(name, shape, dt))

        def bank(name):
            return stack.enter_context(nc.psum_tensor(name, [P, BANK], F32))

        def sem(name):
            return stack.enter_context(nc.semaphore(name))

        xs = sb("xs", [P, T, D])
        hs = sb("hs", [P, T, D])
        hT = sb("hT", [P, 2, NC, BANK], F32R)
        wu_in = sb("wu_in", [P, UT, D])
        av_in = sb("av_in", [P, ST, D])
        wq_in = sb("wq_in", [BOT, D])
        wvd_in = sb("wvd_in", [VB, D])
        wvu_in = sb("wvu_in", [P, NC, VB])
        keys_in = sb("keys_in", [P, ST, BOT])
        wr_in = sb("wr_in", [RDIM, BOT])
        wuT = sb("wuT", [P, 2, NC, NU], F32R)
        wqT = sb("wqT", [P, 2, NC, BOT], F32R)
        wvuT = sb("wvuT", [VB, 2, D], F32R)
        avT = sb("avT", [P, NC, NSLOT])
        wvdT = sb("wvdT", [P, NC, VB])
        keysT = sb("keysT", [BOT, NSLOT])
        wrT = sb("wrT", [BOT, RDIM])
        rkT = sb("rkT", [RDIM, NSLOT])
        slots = sb("slots", [BOT + 1, 2, NSLOT])
        values = sb("values", [P, ST, VB])
        bu = sb("bu", [P, UT])
        wu2 = sb("wu2", [P, UT])
        scal = sb("scal", [P, 8])
        ones = sb("ones", [P, P])
        qT = sb("qT_f", [BOT + 1, BANK])
        gelu = sb("gelu", [P, UT, BANK])
        scores = sb("scores", [P, TH, 2, NSLOT])
        top = sb("top", [P, TH, 8])
        kept = sb("kept", [P, TH, NSLOT])
        attn = sb("attn", [P, TH, NSLOT])
        negmax = sb("negmax_f", [P, TH])
        prob = sb("prob", [P, TH, NSLOT])
        total = sb("total", [P, T])
        probT = sb("probT", [P, ST, BANK])
        mixT = sb("mixT", [VB, HALVES, 2, BANK], F32R)
        stats = sb("stats_f", [P, T, 2, 6])
        moments = sb("moments_f", [P, T, 2])
        small = sb("small", [P, 16, T])
        eps = sb("eps_f", [P, 1])
        (STD, R0, V1, V2, V3, RSTD, VAR1, VARH, LOGVAR, NORM, SIG, U, GATE, COEF) = range(14)
        msum = sb("msum", [P, 4])

        turn_ps = [bank("turn_ps0_f"), bank("turn_ps1_f")]
        u_ps = [bank("u_ps0"), bank("u_ps1")]
        q_ps = bank("q_ps")
        s_ps = [bank("s_ps0"), bank("s_ps1")]
        misc_ps = bank("misc_ps")

        loads = {n: sem("in_" + n) for n in ("x0", "x1", "wu", "small", "wq", "wvd", "wvu", "av")}
        dve_chain = sem("dve_chain")
        act_chain = sem("act_chain")
        ones_done = sem("ones_done")
        turned = sem("turned")
        turned_hi = sem("turned_hi")
        turned_lo = sem("turned_lo")
        small_ps = sem("small_ps")
        u_done = sem("u_done")
        q_done = sem("q_done")
        s_done = sem("s_done")
        gelu_done = sem("gelu_done")
        s_copied = sem("s_copied")
        learned_ps = sem("learned_ps")
        mean_ps = sem("mean_ps")
        prob_done = sem("prob_done")
        mix_ps = sem("mix_ps")
        mix_hi = sem("mix_hi")
        mix_lo = sem("mix_lo")
        aux_ps = sem("aux_ps")
        out_done = sem("out_done")
        stored = sem("stored")

        groups = []
        for n in range(4):
            blocks = [(wu_in[:, ut, c * P:(c + 1) * P], P) for c in (2 * n, 2 * n + 1) for ut in range(UT)]
            groups.append(("wu", blocks, lambda part, n=n: wuT[:, part, 2 * n:2 * n + 2, :].rearrange("p c u -> p (c u)"), P, True))
        groups.append(("wq", [(wq_in[:, c * P:(c + 1) * P], BOT) for c in range(NC)],
                       lambda part: wqT[:, part, :, :].rearrange("p c u -> p (c u)"), P, True))
        groups.append(("small", [(keys_in[:, s, :], P) for s in range(ST)], lambda part: keysT[:, :], BOT, False))
        groups.append(("small", [(wr_in[:, :], RDIM)], lambda part: wrT[:, :], BOT, False))
        WEIGHTS_FIRST = len(groups)
        late = []
        for n in range(4):
            blocks = [(av_in[:, s, c * P:(c + 1) * P], P) for c in (2 * n, 2 * n + 1) for s in range(ST)]
            late.append(("av", blocks, lambda part, n=n: avT[:, 2 * n:2 * n + 2, :].rearrange("p c u -> p (c u)"), P, False))
        late.append(("wvd", [(wvd_in[:, c * P:(c + 1) * P], VB) for c in range(NC)],
                     lambda part: wvdT[:, :, :].rearrange("p c u -> p (c u)"), P, False))
        for n in range(2):
            late.append(("wvu", [(wvu_in[:, c, :], P) for c in range(4 * n, 4 * n + 4)],
                         lambda part, n=n: wvuT[:, part, n * BANK:(n + 1) * BANK], VB, True))

        def h_groups(half):
            for t in range(TH):
                for c in (0, 4):
                    yield (half * TH + t, [(hs[:, half * TH + t, (c + k) * P:(c + k + 1) * P], P) for k in range(4)],
                           lambda part, t=t, c=c: hT[:, part, c:c + 4, t * P:(t + 1) * P], P, True)

        def p_groups(half):
            for s in range(ST):
                yield ("prob", [(prob[:, t, s * P:(s + 1) * P], P) for t in range(TH)],
                       lambda part, s=s: probT[:, s, :], P, False)

        order = groups + late
        H0 = len(order)
        order = order + list(h_groups(0))
        H1 = len(order)
        order = order + list(h_groups(1))
        P0 = len(order)
        order = order + list(p_groups(0))
        P1 = len(order)
        order = order + list(p_groups(1))

        def splits(k):
            return sum(g[4] for g in order[:k])

        def arrived(eng, *names):
            for n in names:
                eng.wait_ge(loads[n], {"small": 10, "x0": 4, "x1": 4}.get(n, 1) * DMA)

        block = stack.enter_context(nc.Block())

        @block.sync
        def _(sp):
            for t in range(TH):
                sp.dma_start(xs[:, t, :], x1_t[:, t, :]).then_inc(loads["x0"], DMA)
            sp.dma_start(wu_in[:, :, :], Wu1.rearrange("(p t) d -> p t d", p=P)).then_inc(loads["wu"], DMA)
            sp.dma_start(wq_in[:, :], Wq).then_inc(loads["wq"], DMA)
            sp.dma_start(keys_in[:, :, :], aux_keys.rearrange("(t p) d -> p t d", p=P)).then_inc(loads["small"], DMA)
            sp.dma_start(wr_in[:, :], Wr).then_inc(loads["small"], DMA)
            sp.dma_start(bu[:, :], bu1.rearrange("(p t) -> p t", p=P)).then_inc(loads["small"], DMA)
            sp.dma_start(wu2[:, :], Wu2.rearrange("a (p t) -> p (a t)", p=P)).then_inc(loads["small"], DMA)
            for col, v in ((0, g_ffn), (2, bu2), (4, gate_w1), (5, gate_bias)):
                sp.dma_start(scal[:, col:col + 1], v.rearrange("(a n) -> a n", a=1).to_broadcast((P, 1))).then_inc(loads["small"], DMA)
            for k in range(2):
                sp.dma_start(slots[BOT:BOT + 1, k, :], log_rel.rearrange("(a n) -> a n", a=1)).then_inc(loads["small"], DMA)
            for t in range(TH, T):
                sp.dma_start(xs[:, t, :], x1_t[:, t, :]).then_inc(loads["x1"], DMA)
            sp.dma_start(av_in[:, :, :], aux_values.rearrange("(t p) d -> p t d", p=P)).then_inc(loads["av"], DMA)
            sp.dma_start(wvd_in[:, :], Wvd).then_inc(loads["wvd"], DMA)
            sp.dma_start(wvu_in[:, :, :], Wvu.rearrange("(t p) d -> p t d", p=P)).then_inc(loads["wvu"], DMA)
            for t in range(T):
                sp.wait_ge(out_done, 2 * t + 2)
                sp.dma_start(out_t[:, t, :], xs[:, t, :]).then_inc(stored, DMA)
            sp.wait_ge(stored, DMA * T)

        mark = {}
        act_mark = {n: i + 1 for i, n in enumerate(("tanh", "halfb", "std0", "rk", "router", "slots", "values", "q0",
                                                    "std1", "q1", "logvar", "sig", "gate"))}

        @block.vector
        def _(dve):
            count = [0]

            def step(ins, name=None):
                count[0] += 1
                ins.then_inc(dve_chain, 1)
                dve.wait_ge(dve_chain, count[0])
                if name:
                    mark[name] = count[0]

            V = nc.vector

            def take_lo(k):
                if not order[k][4]:
                    return
                _, blocks, dst, np_, _ = order[k]
                dve.wait_ge(turned_hi, k + 1)
                src = turn_ps[k % 2][0:np_, 0:sum(n for _, n in blocks)]
                if len(dst(LO).shape) == 3:
                    src = src.rearrange("p (c n) -> p c n", n=P)
                V.tensor_tensor(dst(LO), src, dst(HI).bitcast(F32), ALU.subtract).then_inc(turned_lo, 1)

            def norms(half):
                arrived(dve, f"x{half}")
                for t in range(half * TH, half * TH + TH):
                    for k in range(2):
                        step(V.bn_stats(stats[:, t, k, :], xs[:, t, k * BANK:(k + 1) * BANK]))
                    step(V.bn_aggr(moments[:, t, :], stats[:, t, :, :]), f"moments{t}")
                cols = slice(half * TH, half * TH + TH)
                var = moments[:, cols, 1]
                s = lambda i: small[:, i, cols]
                step(V.tensor_scalar(s(VAR1), var, EPS, None, ALU.add), f"var{half}")
                dve.wait_ge(act_chain, act_mark[f"std{half}"])
                step(V.reciprocal(s(R0), s(STD)))
                step(V.tensor_tensor(s(V1), s(VAR1), s(R0), ALU.mult))
                step(V.tensor_tensor(s(V2), s(V1), s(R0), ALU.mult))
                step(V.tensor_scalar(s(V3), s(V2), -0.5, 1.5, ALU.mult, ALU.add))
                step(V.tensor_tensor(s(RSTD), s(R0), s(V3), ALU.mult))
                step(V.tensor_tensor(s(V1), var, s(RSTD), ALU.mult))
                step(V.tensor_tensor(s(VARH), s(V1), s(RSTD), ALU.mult), f"varh{half}")
                for t in range(half * TH, half * TH + TH):
                    step(V.tensor_scalar(hs[:, t, :], xs[:, t, :], moments[:, t, 0:1], small[:, RSTD, t:t + 1],
                                         ALU.subtract, ALU.mult), f"h{t}")

            def pick(half):
                for t in range(TH):
                    tile = half * TH + t
                    dve.wait_ge(s_copied, tile + 1)
                    if half:
                        dve.wait_ge(turned, P1)
                    router = scores[:, t, 0, :]
                    step(V.max(top[:, t, :], router))
                    step(V.match_replace(kept[:, t, :], top[:, t, :], router, MASKED))
                    step(V.tensor_tensor(kept[:, t, :], kept[:, t, :], router, ALU.is_equal))
                    step(V.scalar_tensor_tensor(out=attn[:, t, :], in0=kept[:, t, :], scalar=MASKED,
                                                in1=scores[:, t, 1, :], op0=ALU.mult, op1=ALU.add))
                    step(V.tensor_reduce(negmax[:, t:t + 1], attn[:, t, :], mybir.AxisListType.X, ALU.max, negate=True),
                         f"attn{tile}")

            def mix_rest(half):
                V.tensor_tensor(mixT[:, half, LO, :], q_ps[0:VB, :], mixT[:, half, HI, :].bitcast(F32),
                                ALU.subtract).then_inc(mix_lo, 1)

            step(V.memset(eps[:, :], EPS))
            step(V.memset(ones[:, :], 1.0))
            step(V.memset(qT[BOT:BOT + 1, :], 1.0), "ones")
            norms(0)
            for k in range(H0):
                take_lo(k)
            for k in range(H0, H1):
                take_lo(k)
            norms(1)
            pick(0)
            for k in range(H1, P0):
                take_lo(k)
            pick(1)
            dve.wait_ge(mix_hi, 1)
            mix_rest(0)
            dve.wait_ge(mean_ps, 1)
            step(V.tensor_reduce(msum[:, 0:1], misc_ps[:, 32:32 + T], mybir.AxisListType.X, ALU.add), "sum")
            step(V.tensor_scalar(msum[:, 1:2], msum[:, 0:1], 2.0 / (B * S), 2e-6, ALU.mult, ALU.add))
            step(V.reciprocal(msum[:, 2:3], msum[:, 1:2]))
            s = lambda i: small[:, i, :]
            step(V.tensor_scalar(s(NORM), s(LOGVAR), msum[:, 2:3], None, ALU.mult))
            dve.wait_ge(act_chain, act_mark["sig"])
            step(V.tensor_scalar(s(V1), s(SIG), 1.25, 1.25, ALU.mult, ALU.add))
            step(V.tensor_tensor(s(U), s(NORM), s(V1), ALU.add))
            step(V.tensor_scalar(s(U), s(U), 0.0, 5.0, ALU.max, ALU.min))
            step(V.tensor_scalar(s(U), s(U), -TAU_LOW, 1.0 / (TAU_HIGH - TAU_LOW), ALU.add, ALU.mult))
            step(V.tensor_scalar(s(U), s(U), 0.0, 1.0, ALU.max, ALU.min))
            step(V.tensor_scalar(s(V2), s(U), scal[:, 4:5], scal[:, 5:6], ALU.mult, ALU.add), "gate_in")
            dve.wait_ge(act_chain, act_mark["gate"])
            step(V.tensor_scalar(s(V3), s(GATE), 0.5, 0.5, ALU.mult, ALU.add))
            step(V.tensor_scalar(s(V1), s(V3), EARLY_EXIT, None, ALU.is_ge))
            step(V.tensor_tensor(s(V1), s(V1), s(V3), ALU.mult))
            dve.wait_ge(prob_done, T)
            step(V.reciprocal(s(V2), total[:, :]))
            step(V.tensor_tensor(s(V1), s(V1), s(V2), ALU.mult))
            step(V.tensor_scalar(s(COEF), s(V1), scal[:, 1:2], None, ALU.mult))
            dve.wait_ge(mix_hi, 2)
            mix_rest(1)
            for t in range(T):
                step(V.scalar_tensor_tensor(out=xs[:, t, :], in0=hs[:, t, :], scalar=scal[:, 1:2], in1=xs[:, t, :],
                                            op0=ALU.mult, op1=ALU.add))
                for n in range(2):
                    dve.wait_ge(aux_ps, 2 * t + n + 1)
                    cols = slice(n * BANK, (n + 1) * BANK)
                    V.scalar_tensor_tensor(out=xs[:, t, cols], in0=s_ps[n][:, :], scalar=small[:, COEF, t:t + 1],
                                           in1=xs[:, t, cols], op0=ALU.mult, op1=ALU.add).then_inc(out_done, 1)

        @block.scalar
        def _(act):
            A = nc.scalar
            count = [0]

            def step(ins, name):
                count[0] += 1
                ins.then_inc(act_chain, 1)
                assert act_mark[name] == count[0], (name, count[0])

            def take_hi(k):
                _, blocks, dst, np_, split = order[k]
                act.wait_ge(turned, k + 1)
                if k == P1:
                    act.wait_ge(mix_ps, 1)
                if k == H1:
                    act.wait_ge(q_done, 1)
                src = turn_ps[k % 2][0:np_, 0:sum(n for _, n in blocks)]
                if len(dst(HI).shape) == 3:
                    src = src.rearrange("p (c n) -> p c n", n=P)
                A.activation(dst(HI), src, ACT.Copy).then_inc(turned_hi, 1)

            def std(half):
                cols = slice(half * TH, half * TH + TH)
                act.wait_ge(dve_chain, mark[f"var{half}"])
                step(A.activation(small[:, STD, cols], moments[:, cols, 1], ACT.Sqrt, bias=eps[:, 0:1]), f"std{half}")

            def half_out(half):
                act.wait_ge(q_done, half + 1)
                if half:
                    act.wait_ge(s_done, TH)
                step(A.activation(qT[0:BOT, :], q_ps[0:BOT, :], ACT.Copy), f"q{half}")
                for t in range(TH):
                    act.wait_ge(s_done, half * TH + t + 1)
                    if half:
                        act.wait_ge(dve_chain, mark[f"attn{t}"])
                    A.activation(scores[:, t, :, :].rearrange("p a n -> p (a n)"), s_ps[t % 2][:, :], ACT.Copy).then_inc(s_copied, 1)
                for u in range(UT):
                    if half:
                        act.wait_ge(learned_ps, 1)
                    A.activation(gelu[:, u, :], u_ps[u][:, :], ACT.Gelu_apprx_tanh, bias=bu[:, u:u + 1]).then_inc(gelu_done, 1)

            def probs(half):
                for t in range(TH):
                    tile = half * TH + t
                    act.wait_ge(dve_chain, mark[f"attn{tile}"])
                    A.activation(prob[:, t, :], attn[:, t, :], ACT.Exp, bias=negmax[:, t:t + 1],
                                 accum_out=total[:, tile:tile + 1]).then_inc(prob_done, 1)

            arrived(act, "small")
            step(A.activation(scal[:, 1:2], scal[:, 0:1], ACT.Tanh), "tanh")
            step(A.activation(scal[:, 3:4], scal[:, 2:3], ACT.Copy, scale=0.5), "halfb")
            std(0)
            for k in range(WEIGHTS_FIRST):
                take_hi(k)
            act.wait_ge(small_ps, 1)
            step(A.activation(rkT[:, :], misc_ps[0:RDIM, 0:NSLOT], ACT.Copy), "rk")
            act.wait_ge(small_ps, 2)
            step(A.activation(slots[0:BOT, 0, :], misc_ps[0:BOT, 0:NSLOT], ACT.Copy, scale=float(RDIM) ** -0.5), "router")
            step(A.activation(slots[0:BOT, 1, :], keysT[:, :], ACT.Copy, scale=float(BOT) ** -0.5), "slots")
            for k in range(WEIGHTS_FIRST, H0):
                take_hi(k)
            act.wait_ge(small_ps, 3)
            step(A.activation(values[:, :, :].rearrange("p s v -> p (s v)"), misc_ps[:, 0:ST * VB], ACT.Copy), "values")
            for k in range(H0, H1):
                take_hi(k)
            half_out(0)
            std(1)
            probs(0)
            for k in range(H1, P0):
                take_hi(k)
            half_out(1)
            act.wait_ge(dve_chain, mark["varh1"])
            step(A.activation(small[:, LOGVAR, :], small[:, VARH, :], ACT.Ln, bias=ones[:, 0:1]), "logvar")
            for k in range(P0, P1):
                take_hi(k)
            act.wait_ge(mix_ps, 1)
            A.activation(mixT[:, 0, HI, :], q_ps[0:VB, :], ACT.Copy).then_inc(mix_hi, 1)
            probs(1)
            for k in range(P1, len(order)):
                take_hi(k)
            act.wait_ge(mix_ps, 2)
            A.activation(mixT[:, 1, HI, :], q_ps[0:VB, :], ACT.Copy).then_inc(mix_hi, 1)
            act.wait_ge(learned_ps, 2)
            act.wait_ge(dve_chain, mark["sum"])
            step(A.activation(small[:, SIG, :], misc_ps[:, 0:T], ACT.Tanh, scale=0.5, bias=scal[:, 3:4]), "sig")
            act.wait_ge(dve_chain, mark["gate_in"])
            step(A.activation(small[:, GATE, :], small[:, V2, :], ACT.Tanh, scale=0.5), "gate")

        @block.tensor
        def _(pe):
            def turn(k):
                name, blocks, dst, np_, split = order[k]
                if k >= 2:
                    if order[k - 2][4]:
                        pe.wait_ge(turned_lo, splits(k - 1))
                    else:
                        pe.wait_ge(turned_hi, k - 1)
                if isinstance(name, int):
                    pe.wait_ge(dve_chain, mark[f"h{name}"])
                elif name == "prob":
                    pe.wait_ge(prob_done, TH if k < P1 else T)
                else:
                    arrived(pe, name)
                at = 0
                for blk, n in blocks:
                    m = blk.shape[-1]
                    last = pe.transpose(turn_ps[k % 2][0:m, at:at + n], blk, ident[0:n, 0:n])
                    at += n
                last.then_inc(turned, 1)

            def product(out, pairs):
                for n, (a, b) in enumerate(pairs):
                    mm = pe.matmul(out, a, b, start=(n == 0), stop=(n == len(pairs) - 1))
                return mm

            def split_product(out, stationary, moving, chunks):
                return product(out, [(stationary(a, c), moving(b, c)) for c in chunks for a, b in PASSES])

            def units(half):
                pe.wait_ge(turned_lo, splits(H1 if half == 0 else P0))
                for u in range(UT):
                    if half:
                        pe.wait_ge(gelu_done, UT)
                    split_product(u_ps[u][:, :], lambda a, c: wuT[:, a, c, u * P:(u + 1) * P],
                                  lambda b, c: hT[:, b, c, :], range(NC)).then_inc(u_done, 1)
                if half:
                    pe.wait_ge(act_chain, act_mark["q0"])
                split_product(q_ps[0:BOT, :], lambda a, c: wqT[:, a, c, :],
                              lambda b, c: hT[:, b, c, :], range(NC)).then_inc(q_done, 1)

            def score(half):
                pe.wait_ge(act_chain, act_mark[f"q{half}"])
                pe.wait_ge(dve_chain, mark["ones"])
                for t in range(TH):
                    tile = half * TH + t
                    if tile >= 2:
                        pe.wait_ge(s_copied, tile - 1)
                    pe.matmul(s_ps[t % 2][:, :], qT[:, t * P:(t + 1) * P], slots[:, :, :].rearrange("p a n -> p (a n)"),
                              start=True, stop=True).then_inc(s_done, 1)

            def learned(half):
                pe.wait_ge(gelu_done, UT * (half + 1))
                for t in range(TH):
                    tile = half * TH + t
                    mm = product(misc_ps[:, tile:tile + 1], [(gelu[:, u, t * P:(t + 1) * P], wu2[:, u:u + 1]) for u in range(UT)])
                mm.then_inc(learned_ps, 1)

            def mix(half):
                pe.wait_ge(turned_hi, P1 if half == 0 else len(order))
                if half:
                    pe.wait_ge(mix_lo, 1)
                else:
                    pe.wait_ge(act_chain, act_mark["q1"])
                product(q_ps[0:VB, :], [(values[:, s, :], probT[:, s, :]) for s in range(ST)]).then_inc(mix_ps, 1)

            for k in range(WEIGHTS_FIRST):
                turn(k)
            pe.wait_ge(turned_hi, WEIGHTS_FIRST)
            product(misc_ps[0:RDIM, 0:NSLOT], [(wrT[:, :], keysT[:, :])]).then_inc(small_ps, 1)
            pe.wait_ge(act_chain, act_mark["rk"])
            product(misc_ps[0:BOT, 0:NSLOT], [(wr_in[:, :], rkT[:, :])]).then_inc(small_ps, 1)
            for k in range(WEIGHTS_FIRST, H0):
                turn(k)
            pe.wait_ge(turned_hi, H0)
            pe.wait_ge(act_chain, act_mark["slots"])
            for s in range(ST):
                mm = product(misc_ps[:, s * VB:(s + 1) * VB], [(avT[:, c, s * P:(s + 1) * P], wvdT[:, c, :]) for c in range(NC)])
            mm.then_inc(small_ps, 1)
            for k in range(H0, H1):
                turn(k)
            units(0)
            score(0)
            for k in range(H1, P0):
                turn(k)
            units(1)
            score(1)
            pe.wait_ge(act_chain, act_mark["values"])
            learned(0)
            for k in range(P0, P1):
                turn(k)
            mix(0)
            learned(1)
            pe.wait_ge(act_chain, act_mark["logvar"])
            product(misc_ps[:, 32:32 + T], [(ones[:, :], small[:, LOGVAR, :])]).then_inc(mean_ps, 1)
            for k in range(P1, len(order)):
                turn(k)
            mix(1)
            for t in range(T):
                half = t // TH
                pe.wait_ge(mix_lo, half + 1)
                for n in range(2):
                    if t:
                        pe.wait_ge(out_done, 2 * t - 1 + n)
                    else:
                        pe.wait_ge(s_copied, T)
                    split_product(s_ps[n][:, :], lambda a, c: mixT[:, half, a, (t % TH) * P:(t % TH + 1) * P],
                                  lambda b, c: wvuT[:, b, n * BANK:(n + 1) * BANK], [0]).then_inc(aux_ps, 1)


def program(nc, x, ctx_4096, fside, mask, g_xattn, g_ffn, Wq, Wk, Wv, Wo, ffn_Wq, ffn_Wr, ffn_keys, ffn_values,
            ffn_Wvd, ffn_Wvu, ffn_Wu1, ffn_bu1, ffn_Wu2, ffn_bu2, ffn_gate_w1, ffn_gate_bias, ffn_log_rel, out):
    x1 = nc.dram_tensor("x1", x.shape, F32, kind="Internal").ap()
    with nc.sbuf_tensor("ident", [P, P], F32) as ident:
        attention(nc, x, ctx_4096, fside, mask, g_xattn, Wq, Wk, Wv, Wo, x1, ident)
        feed_forward(nc, x1, out, ident, g_ffn, ffn_Wq, ffn_Wr, ffn_keys, ffn_values, ffn_Wvd, ffn_Wvu, ffn_Wu1,
                     ffn_bu1, ffn_Wu2, ffn_bu2, ffn_gate_w1, ffn_gate_bias, ffn_log_rel)


_INS = ["x", "ctx_4096", "fside_Bx32xSxS2_0", "mask_BxSxS2_bk0", "g_xattn", "g_ffn",
        "L0_xattn_Wq", "L0_xattn_Wk", "L0_xattn_Wv", "L0_xattn_Wo", "L0_ffn_Wq", "L0_ffn_Wr",
        "L0_ffn_aux_keys", "L0_ffn_aux_values", "L0_ffn_Wvd", "L0_ffn_Wvu", "L0_ffn_Wu1", "L0_ffn_bu1",
        "L0_ffn_Wu2", "L0_ffn_bu2", "L0_ffn_gate_w1", "L0_ffn_gate_bias", "L0_ffn_log_rel"]


def kernel(**inputs):
    import numpy as _np
    import concourse.bacc as _bacc
    from concourse import mybir as _mybir
    from concourse.bass_utils import run_bass_kernel_spmd as _run

    nc = _bacc.Bacc("TRN2", target_bir_lowering=False, num_devices=1, dynamic_dma_scratch_size=1024)
    arrays, args = {}, []
    for name in _INS:
        a = _np.ascontiguousarray(inputs[name])
        a = a.reshape(a.shape or (1,))
        arrays[f"in_{name}_dram"] = a
        args.append(nc.dram_tensor(f"in_{name}_dram", a.shape, _mybir.dt.from_np(a.dtype), kind="ExternalInput").ap())
    shape = inputs["x"].shape
    args.append(nc.dram_tensor("out_0_dram", shape, _mybir.dt.float32, kind="ExternalOutput").ap())
    program(nc, *args)
    r = _run(nc, [arrays], core_ids=[0])
    return r.results[0]["out_0_dram"]
```

```python
from contextlib import ExitStack

import concourse.bass as bass
from concourse import mybir

ALU = mybir.AluOpType
ACT = mybir.ActivationFunctionType
AX_X = mybir.AxisListType.X
AX_XY = mybir.AxisListType.XY
F32 = mybir.dt.float32
F32R = mybir.dt.float32r
BF16 = mybir.dt.bfloat16
U8 = mybir.dt.uint8
I32 = mybir.dt.int32

P = 128
BANK = 512
KB = 1024
DMA = 16
EPS = 1e-5
MASKED = -3e38
NO_SCORE = 1.5e38
LEAST_SUM = 1e-30
HI, LO = 0, 1
PASSES = ((HI, HI), (HI, LO), (LO, HI))
HEADS_PER_TURN = 5


def program(nc, x, ctx_in, bias, mask, g_xattn, g_ffn, Wq, Wk, Wv, Wo, ffn_Wq, ffn_Wr, ffn_keys, ffn_values,
            ffn_Wvd, ffn_Wvu, ffn_Wu1, ffn_bu1, ffn_Wu2, ffn_bu2, ffn_gate_w1, ffn_gate_bias, ffn_log_rel, out):
    B, S, D = x.shape
    SK = ctx_in.shape[1]
    H = bias.shape[1]
    DH = Wq.shape[1] // H
    NC = D // P
    QT = S // P
    KT = SK // P
    KH = SK // BANK
    YG = QT * (D // BANK)
    SCALE = float(DH) ** -0.5
    TURNS = (H - 2) // HEADS_PER_TURN
    HT = BANK // P
    GX = 2 * QT
    ALL = B * H
    BOT, RDIM, NSLOT, VB, NU = ffn_Wq.shape[0], ffn_Wr.shape[0], ffn_keys.shape[0], ffn_Wvd.shape[0], ffn_Wu1.shape[0]
    T = B * QT
    UT = NU // P
    ST = NSLOT // P
    TAU_LOW, TAU_HIGH, EARLY_EXIT = 0.5, 2.0, 0.05

    def sizes(halves):
        return HT * halves, BANK * halves, 2 * HT * halves, 2 * HT * halves + GX, halves + 1

    assert B == 2 and DH == P and S == BANK and KH == 2 and QT == 4 and NC == 8 and KT == 8 and YG == 8
    assert (H - 2) % HEADS_PER_TURN == 0
    assert ST == 2 and UT == 2 and 2 * NSLOT == BANK and BOT == VB == 64 and RDIM <= 64

    x1 = nc.dram_tensor("x1", (S, D), F32, kind="Internal").ap()
    x1_t = x1.rearrange("(t p) d -> p t d", p=P)
    x_t = x.rearrange("b (t p) d -> b p t d", p=P)
    out_t = out.rearrange("b (t p) d -> p (b t) d", p=P)
    ctx_t = ctx_in.rearrange("b (t p) d -> (b t) p d", p=P)
    mask_t = mask.rearrange("b (t p) k -> b p t k", p=P)
    bias_t = bias.rearrange("b h (t p) k -> (b h t) p k", p=P)
    w_dram = {m: w.rearrange("(c p) n -> p c n", p=P) for m, w in (("q", Wq), ("k", Wk), ("v", Wv))}

    base = (nc.sbuf_base + 31) // 32 * 32

    def at(name, where, shape, dt=F32):
        n = {F32: 4, F32R: 4, BF16: 2, U8: 1, I32: 4}[dt]
        for s in shape[1:]:
            n *= s
        assert n <= where[1], (name, n, where)
        assert where[0] + n <= nc.sbuf_usable_end
        return nc.alloc_sbuf_tensor_at(name, shape, dt, offset=where[0])

    top = [base]

    def place(kb):
        n = int(kb * KB)
        top[0] += n
        return top[0] - n, n

    def part(where, kb, of):
        assert int((kb + of) * KB) <= where[1]
        return where[0] + int(kb * KB), int(of * KB)

    C, X, Y, HIDE, RAW = place(64), place(32), place(16), place(8), place(8)
    WK, WQ, WV, WO = place(8), place(8), place(8), place(8)
    KQ_K, KQ_Q, VT, VV, BIAS = place(8), place(4), place(2), place(8), place(8)
    PROBS, PT, OT = place(16), place(8), place(4)

    ctxT = at("ctxT", C, [P, 2, NC, SK], F32R)
    xnT = at("xnT", X, [P, 2, NC, S], F32R)
    y = at("y", Y, [P, QT, D])
    hide = at("hide", HIDE, [P, QT, SK], BF16)
    raw = at("raw", RAW, [P, 2, D])
    w = {m: at("w" + m, where, [P, 2, D], F32R) for m, where in (("k", WK), ("q", WQ), ("v", WV), ("o", WO))}
    kT = at("kT", KQ_K, [P, 2, SK], F32R)
    qT = at("qT", KQ_Q, [P, 2, S], F32R)
    vT = at("vT", VT, [P, BANK])
    v = at("v", VV, [P, 2, KT, DH], F32R)
    bias_sb = at("bias_sb", BIAS, [P, 2 * SK])
    probs = at("probs", PROBS, [P, QT, SK])
    pT = at("pT", PT, [P, 2, 2, S], F32R)
    oT = at("oT", OT, [P, 2, S], F32R)
    stage = at("stage", X, [P, KT, D])
    mask_in = at("mask_in", PT, [P, QT, SK], U8)
    mask_all = at("mask_all", PT, [P, B, QT, SK], U8)
    ident = at("ident", place(0.5), [P, P])
    ones = at("ones", place(0.5), [P, P])
    row = at("row", place(0.5), [P, 5, QT])
    negmax, rowsum, safe_sum, recip, coef = (row[:, i, :] for i in range(5))
    stats = at("stats", place(0.5), [P, QT, 2, 6])
    scal = at("scal", place(0.0625), [P, 12])
    (G_X, TG_X, G_F, TG_F, BU2, HALF_BU2, W1, GBIAS, EPS_C, MEAN_0, MEAN_1, MEAN_2) = range(12)
    moments = at("moments", place(0.0625), [P, T, 2])
    token = at("token", place(0.5), [P, 14, T])
    (STD, R0, V1, V2, V3, RSTD, VAR1, LOGVAR, NORM, SIG, U, GATE, COEF, TOTAL) = range(14)
    seen = at("seen", place(0.0625), [P, 4 * B])
    plan = at("plan", place(0.03125), [P, 2 + 2 * B], I32)
    ALL_SEEN, FIRST_KEY, FIRST_TILE = 0, 1, 1 + B
    bu = at("bu", place(0.03125), [P, UT])
    wu2 = at("wu2", place(0.03125), [P, UT])

    xs0 = at("xs0", part(X, 0, 16), [P, QT, D])
    wu_in = at("wu_in", part(X, 16, 8), [P, UT, D])
    wq_in = at("wq_in", part(X, 24, 4), [BOT, D])
    wvd_in = at("wvd_in", part(X, 28, 4), [VB, D])
    hs0 = at("hs0", (WK[0], WK[1] + WQ[1]), [P, QT, D])
    keys_in = at("keys_in", part(RAW, 0, 0.5), [P, ST, BOT])
    wr_in = at("wr_in", part(RAW, 0.5, 0.25), [RDIM, BOT])
    keysT = at("keysT", part(RAW, 0.75, 1), [BOT, NSLOT])
    wvu_in = at("wvu_in", part(RAW, 1.75, 2), [P, NC, VB])
    slots = at("slots", part(RAW, 4, 2), [BOT + 1, 2, NSLOT])
    queryT = at("queryT", part(RAW, 6, 2), [BOT + 1, BANK])
    hT = at("hT", part(C, 0, 32), [P, 2, NC, BANK], F32R)
    wuT = at("wuT", part(C, 32, 16), [P, 2, NC, NU], F32R)
    av_in = at("av_in", part(C, 48, 8), [P, ST, D])
    avT = at("avT", part(C, 56, 8), [P, NC, NSLOT])
    wqT = at("wqT", KQ_Q, [P, 2, NC, BOT], F32R)
    wvuT = at("wvuT", WV, [VB, 2, D], F32R)
    scores = at("scores", KQ_K, [P, QT, 2, NSLOT])
    gelu = at("gelu", part(HIDE, 0, 4), [P, UT, BANK])
    rkT = at("rkT", part(HIDE, 4, 1), [RDIM, NSLOT])
    wrT = at("wrT", part(HIDE, 5, 0.25), [BOT, RDIM])
    wvdT = at("wvdT", part(HIDE, 5.25, 2), [P, NC, VB])
    values = at("values", part(HIDE, 7.25, 0.5), [P, ST, VB])
    top8 = at("top8", part(HIDE, 7.75, 0.125), [P, QT, 8])
    negmax_f = at("negmax_f", part(HIDE, 7.875, 0.0625), [P, QT])
    mixT = at("mixT", BIAS, [VB, B, 2, BANK], F32R)
    hs1 = at("hs1", PROBS, [P, QT, D])
    kept = at("kept", part(PT, 0, 4), [P, QT, NSLOT])
    attn = at("attn", part(PT, 4, 4), [P, QT, NSLOT])
    prob = at("prob", part(VV, 0, 4), [P, QT, NSLOT])
    probT = at("probT", part(VV, 4, 4), [P, ST, BANK])
    xs, hs = (xs0, y), (hs0, hs1)

    def var_of(half):
        return moments[:, half * QT:half * QT + QT, 1]

    with ExitStack() as stack:
        def bank(name, n=1):
            return stack.enter_context(nc.psum_tensor(name, [P, n * BANK], F32))

        score_ps = bank("score_ps", 2)
        proj_ps = [bank("proj_ps0"), bank("proj_ps1")]
        turn_ps = [bank("turn_ps0"), bank("turn_ps1")]
        head_ps = bank("head_ps")
        out_ps = bank("out_ps")
        score_half = [score_ps[:, 0:BANK], score_ps[:, BANK:]]
        K_BANK = proj_ps
        Q_BANK = {2: proj_ps[0], 1: proj_ps[1]}
        OUT_BANKS = {1: [out_ps], 2: [out_ps, proj_ps[1]]}
        V_BANK = {2: [proj_ps[1], head_ps], 1: [proj_ps[0]]}
        F_TURN = score_half
        F_QUERY = proj_ps[0]
        F_UNITS = [proj_ps[1], head_ps]
        F_SCORES = turn_ps
        F_MISC = out_ps

        START_BANKS = [score_half[0], score_half[1], proj_ps[1][:], turn_ps[0][:], turn_ps[1][:]]

        KQ_AT = {2: {0: 0, 3: 1, 7: 2}, 1: {0: 0, 3: 1}}

        def bias_slot(qt, halves):
            slots_ = 4 // halves
            W, n = halves * BANK, qt % slots_
            return n, bias_sb[:, n * W:(n + 1) * W], QT // slots_

        def start_bank(k, GC):
            return k % 3 if k < GC else (0, 1, 3, 4)[k % 4]

        def start_bank_before(k, GC):
            return max((j for j in range(k) if start_bank(j, GC) == start_bank(k, GC)), default=None)

        def sem(name):
            return stack.enter_context(nc.semaphore(name))

        weight_in = {m: sem("weight_in_" + m) for m in "qkvo"}
        weight_hi = {m: sem("weight_hi_" + m) for m in "qkvo"}
        weight_lo = {m: sem("weight_lo_" + m) for m in "qkvo"}
        bias_in = [sem(f"bias_in{i}") for i in range(4)]
        bias_masked = sem("bias_masked")
        ctx_load = [sem(f"ctx_load{t}") for t in range(KT)]
        x_load = [sem(f"x_load{t}") for t in range(QT)]
        mask_load = sem("mask_load")
        mask_all_load = sem("mask_all_load")
        seen_done = sem("seen_done")
        seen_ps = sem("seen_ps")
        plan_step = sem("plan_step")
        PLANNED = 6
        y_load = sem("y_load")
        y_out = sem("y_out")
        g_in = sem("g_in")
        went_on = {"sp": sem("went_on_sp"), "dve": sem("went_on_dve")}
        ident_done = sem("ident_done")
        gate_done = sem("gate_done")
        hide_done = sem("hide_done")
        norm_step = sem("norm_step")
        STATS_STEPS, RSTD_STEPS = 3 * QT, 6
        std_done = sem("std_done")
        xn_done = sem("xn_done")
        start_ps = sem("start_ps")
        start_hi = sem("start_hi")
        start_lo = sem("start_lo")
        kq_ps = sem("kq_ps")
        kq_hi = sem("kq_hi")
        kq_lo = sem("kq_lo")
        v_ps = sem("v_ps")
        vT_sb = sem("vT_sb")
        v_turned = sem("v_turned")
        v_hi = sem("v_hi")
        v_lo = sem("v_lo")
        score_done = sem("score_done")
        score_sb = sem("score_sb")
        exp_done = sem("exp_done")
        coef_step = sem("coef_step")
        p_turned = sem("p_turned")
        pT_hi = sem("pT_hi")
        pT_lo = sem("pT_lo")
        pv_done = sem("pv_done")
        oT_hi = sem("oT_hi")
        oT_lo = sem("oT_lo")
        y_ps = sem("y_ps")
        y_sb = sem("y_sb")
        f_load = {n: sem("f_load_" + n) for n in ("x", "wu", "wq", "wvd", "small", "rows", "av", "wvu")}
        F_LOADS = {"x": QT, "small": 8, "rows": 2}
        dve_step = sem("dve_step")
        act_step = sem("act_step")
        turned = sem("turned")
        turned_hi = sem("turned_hi")
        turned_lo = sem("turned_lo")
        product_ps = sem("product_ps")
        unit_ps = sem("unit_ps")
        query_ps = sem("query_ps")
        slot_ps = sem("slot_ps")
        slot_sb = sem("slot_sb")
        gelu_done = sem("gelu_done")
        learned_ps = sem("learned_ps")
        prob_done = sem("prob_done")
        mix_ps = sem("mix_ps")
        mix_hi = sem("mix_hi")
        mix_lo = sem("mix_lo")
        sum_step = sem("sum_step")
        aux_ps = sem("aux_ps")
        out_done = sem("out_done")
        stored = sem("stored")

        WSLOT = {"k": 0, "v": 0, "q": 1, "o": 1}

        def run_heads(eng, start, head):
            for b in range(B):
                start(b, b * H)
                head(b * H, True, False)
                with eng.Fori(0, TURNS) as turn:
                    for u in range(HEADS_PER_TURN):
                        head(turn * HEADS_PER_TURN + (b * H + 1 + u), False, False)
                head(b * H + (H - 1), False, True)

        order = []
        for n in range(4):
            blocks = [(wu_in[:, ut, c * P:(c + 1) * P], P) for c in (2 * n, 2 * n + 1) for ut in range(UT)]
            order.append(("wu", blocks, lambda p, n=n: wuT[:, p, 2 * n:2 * n + 2, :].rearrange("p c u -> p (c u)"), P, True))
        order.append(("wq", [(wq_in[:, c * P:(c + 1) * P], BOT) for c in range(NC)],
                      lambda p: wqT[:, p, :, :].rearrange("p c u -> p (c u)"), P, True))
        order.append(("small", [(keys_in[:, s, :], P) for s in range(ST)], lambda p: keysT[:, :], BOT, False))
        order.append(("small", [(wr_in[:, :], RDIM)], lambda p: wrT[:, :], BOT, False))

        def h_groups(half):
            return [(half * QT + t, [(hs[half][:, t, (c + k) * P:(c + k + 1) * P], P) for k in range(4)],
                     lambda p, t=t, c=c: hT[:, p, c:c + 4, t * P:(t + 1) * P], P, True) for t in range(QT) for c in (0, 4)]

        H0 = len(order)
        order += h_groups(0)
        AV = len(order)
        for n in range(4):
            blocks = [(av_in[:, s, c * P:(c + 1) * P], P) for c in (2 * n, 2 * n + 1) for s in range(ST)]
            order.append(("av", blocks, lambda p, n=n: avT[:, 2 * n:2 * n + 2, :].rearrange("p c u -> p (c u)"), P, False))
        order.append(("wvd", [(wvd_in[:, c * P:(c + 1) * P], VB) for c in range(NC)],
                      lambda p: wvdT[:, :, :].rearrange("p c u -> p (c u)"), P, False))
        for n in range(2):
            order.append(("wvu", [(wvu_in[:, c, :], P) for c in range(4 * n, 4 * n + 4)],
                          lambda p, n=n: wvuT[:, p, n * BANK:(n + 1) * BANK], VB, True))
        H1 = len(order)
        order += h_groups(1)
        P0 = len(order)
        for half in range(B):
            for s in range(ST):
                order.append(("prob", [(prob[:, t, s * P:(s + 1) * P], P) for t in range(QT)],
                              lambda p, s=s: probT[:, s, :], P, False))
        P1, END = P0 + ST, P0 + 2 * ST
        FILLS = [(0, 1), (2, 3), (4, 5, 6), (7, 8), (9, 10), (11, 12), (13, 14), (15, 16)]
        assert FILLS[-1][-1] + 1 == AV + 2

        def fill_groups(i, halves):
            return FILLS[i] if halves == 2 else FILLS[2 * i] + FILLS[2 * i + 1]

        def splits(k):
            return sum(g[4] for g in order[:k])

        def arrived(eng, *names):
            for n in names:
                eng.wait_ge(f_load[n], F_LOADS.get(n, 1) * DMA)

        def f_source(k):
            _, blocks, dst, parts, _ = order[k]
            src = F_TURN[k % 2][0:parts, 0:sum(n for _, n in blocks)]
            return src.rearrange("p (c n) -> p c n", n=P) if len(dst(HI).shape) == 3 else src

        act_mark = {n: i + 1 for i, n in enumerate(("std0", "rk", "router", "slots", "query0", "std1", "values", "logvar",
                                                    "sig0", "query1", "gate0", "sig1", "gate1"))}
        dve_mark = {}

        block = stack.enter_context(nc.Block())

        @block.sync
        def _(sp):
            def when(s, n):
                sp.wait_ge(s, n)
                sp.sem_inc(went_on["sp"], 1)

            def scalar_in(column, ap, s):
                sp.dma_start(scal[:, column:column + 1], ap.rearrange("(a n) -> a n", a=1).to_broadcast((P, 1))).then_inc(s, DMA)

            def load_weight(m, h):
                dst = raw[:, WSLOT[m], :]
                if m == "o":
                    src = Wo[bass.ds(h * DH, DH), :]
                else:
                    src = w_dram[m][:, :, bass.ds(h * DH, DH)]
                    dst = dst.rearrange("p (c n) -> p c n", n=DH)
                sp.dma_start(dst, src).then_inc(weight_in[m], DMA)

            def load_x(b):
                for t in range(QT):
                    sp.dma_start(probs[:, t, :], x_t[b, :, t, :]).then_inc(x_load[t], DMA)

            def load_y(b):
                sp.dma_start(y[:, :, :], x_t[b]).then_inc(y_load, DMA)

            def attend(halves):
                KT, W, GC, G, KQ = sizes(halves)

                def load_bias(b, g, qt):
                    n, slot, _ = bias_slot(qt, halves)
                    sp.dma_start(slot,
                                 bias_t[bass.ds(g * QT + qt, 1), :, keys_of(b)].rearrange("a p k -> p (a k)")).then_inc(bias_in[n], DMA)

                def load_ctx(b):
                    for t in range(KT):
                        tile = bass.ds(first_tile[b] + (b * (SK // P) + t), 1) if halves == 1 else slice(b * KT + t, b * KT + t + 1)
                        sp.dma_start(stage[:, t, :], ctx_t[tile, :, :].rearrange("a p d -> p (a d)")).then_inc(ctx_load[t], DMA)

                def load_mask(b):
                    sp.dma_start(mask_in[:, :, 0:W], mask_t[b][:, :, keys_of(b)]).then_inc(mask_load, DMA)

                def keys_of(b):
                    return bass.ds(first_key[b], W) if halves == 1 else slice(0, SK)

                def start():
                    load_ctx(0)
                    when(weight_lo["k"], 1)
                    load_weight("v", 0)
                    load_weight("q", 0)
                    load_mask(0)
                    for qt in range(4 // halves):
                        load_bias(0, 0, qt)
                    load_y(0)

                def head(b, h, last):
                    final = last and b == B - 1
                    g = h + b * H
                    following = 0 if last else h + 1
                    if not final:
                        when(weight_lo["v"], g + 1)
                        load_weight("k", following)
                        when(weight_lo["q"], g + 1)
                        when(weight_lo["o"], g)
                        load_weight("q", following)
                    if last:
                        when(kq_ps, KQ * (g + 1))
                    if last and not final:
                        load_ctx(1)
                    if final:
                        when(y_out, DMA)
                        for t in range(QT):
                            sp.dma_start(xs0[:, t, :], x1_t[:, t, :]).then_inc(f_load["x"], DMA)
                        sp.dma_start(wu_in[:, :, :], ffn_Wu1.rearrange("(p t) d -> p t d", p=P)).then_inc(f_load["wu"], DMA)
                        sp.dma_start(wq_in[:, :], ffn_Wq).then_inc(f_load["wq"], DMA)
                        when(weight_lo["v"], g + 1)
                        sp.dma_start(keys_in[:, :, :], ffn_keys.rearrange("(t p) d -> p t d", p=P)).then_inc(f_load["small"], DMA)
                        sp.dma_start(wr_in[:, :], ffn_Wr).then_inc(f_load["small"], DMA)
                        sp.dma_start(bu[:, :], ffn_bu1.rearrange("(p t) -> p t", p=P)).then_inc(f_load["small"], DMA)
                        sp.dma_start(wu2[:, :], ffn_Wu2.rearrange("a (p t) -> p (a t)", p=P)).then_inc(f_load["small"], DMA)
                        for column, ap in ((G_F, g_ffn), (BU2, ffn_bu2), (W1, ffn_gate_w1), (GBIAS, ffn_gate_bias)):
                            scalar_in(column, ap, f_load["small"])
                    if halves == 2:
                        for qt in range(2, QT):
                            when(score_sb, QT * g + qt - 1)
                            load_bias(b, g, qt)

                    def next_bias(qt):
                        when(score_sb, QT * g + (QT - 1 if halves == 2 else 1) + qt)
                        load_bias(b + 1 if last else b, g + 1, qt)

                    if not final:
                        if halves == 1:
                            next_bias(0)
                        when(weight_lo["k"], g + 2)
                        load_weight("v", following)
                        if halves == 1:
                            next_bias(1)
                        when(weight_lo["q"], g + 2)
                    else:
                        when(weight_lo["q"], g + 1)
                        when(weight_lo["o"], g)
                        sp.dma_start(wvd_in[:, :], ffn_Wvd).then_inc(f_load["wvd"], DMA)
                        sp.dma_start(wvu_in[:, :, :], ffn_Wvu.rearrange("(t p) d -> p t d", p=P)).then_inc(f_load["wvu"], DMA)
                    load_weight("o", h)
                    if not final:
                        for qt in (0, 1) if halves == 2 else (2, 3):
                            next_bias(qt)
                    if last and not final:
                        when(p_turned, KT * (g + 1))
                        load_x(1)
                        when(pv_done, KT * (g + 1))
                        load_mask(1)
                        when(y_sb, YG * (g + 1))
                        sp.dma_start(x1_t, y[:, :, :]).then_inc(y_out, DMA)
                        when(y_out, DMA)
                        load_y(1)
                    if final:
                        when(v_ps, halves * (g + 1))
                        sp.dma_start(av_in[:, :, :], ffn_values.rearrange("(t p) d -> p t d", p=P)).then_inc(f_load["av"], DMA)
                        when(weight_lo["o"], g + 1)
                        for k in range(2):
                            sp.dma_start(slots[BOT:BOT + 1, k, :], ffn_log_rel.rearrange("(a n) -> a n", a=1)).then_inc(f_load["rows"], DMA)

                start()
                for b in range(B):
                    head(b, 0, False)
                    with sp.Fori(0, TURNS) as turn:
                        for u in range(HEADS_PER_TURN):
                            head(b, turn * HEADS_PER_TURN + (1 + u), False)
                    head(b, H - 1, True)

            scalar_in(G_X, g_xattn, g_in)
            sp.dma_start(mask_all[:, :, :, :], mask.rearrange("b (t p) k -> p b t k", p=P)).then_inc(mask_all_load, DMA)
            load_weight("k", 0)
            load_x(0)
            sp.wait_ge(plan_step, PLANNED)
            all_seen = sp.value_load(plan[0:1, ALL_SEEN:ALL_SEEN + 1], min_val=0, max_val=1)
            first_key = [sp.value_load(plan[0:1, FIRST_KEY + b:FIRST_KEY + b + 1], min_val=0, max_val=SK - BANK) for b in range(B)]
            first_tile = [sp.value_load(plan[0:1, FIRST_TILE + b:FIRST_TILE + b + 1], min_val=0, max_val=HT) for b in range(B)]
            with sp.If(all_seen == 1):
                attend(2)
            with sp.Else():
                attend(1)
            for t in range(T):
                sp.wait_ge(out_done, 2 * t + 2)
                sp.dma_start(out_t[:, t, :], xs[t // QT][:, t % QT, :]).then_inc(stored, DMA)
            sp.wait_ge(stored, DMA * T)

        @block.gpsimd
        def _(pool):
            nc.gpsimd.memset(ident[:], 0.0).then_inc(ident_done, 1)
            pool.wait_ge(ident_done, 1)
            nc.gpsimd.affine_select(out=ident[:], in_=ident[:], compare_op=ALU.not_equal, fill=1.0,
                                    base=0, pattern=[[-1, P]], channel_multiplier=1).then_inc(ident_done, 1)

            def attend(halves):
                KT, W, GC, G, KQ = sizes(halves)

                def head(g, first, last):
                    for qt in range(QT):
                        if first:
                            pool.wait_ge(hide_done, QT * (g // H) + qt + 1)
                        n, slot, per_head = bias_slot(qt, halves)
                        pool.wait_ge(bias_in[n], DMA * per_head * g + DMA * (qt * per_head // QT + 1))
                        nc.gpsimd.tensor_tensor(slot, slot, hide[:, qt, 0:W], ALU.add).then_inc(bias_masked, 1)

                run_heads(pool, lambda b, g: None, head)

            pool.wait_ge(plan_step, PLANNED)
            all_seen = pool.value_load(plan[0:1, ALL_SEEN:ALL_SEEN + 1], min_val=0, max_val=1)
            with pool.If(all_seen == 1):
                attend(2)
            with pool.Else():
                attend(1)
            pool.wait_ge(gate_done, 3)
            for t in range(QT):
                pool.wait_ge(turned, H0 + 2 * t + 2)
                nc.gpsimd.tensor_scalar(hs0[:, t, :], hs0[:, t, :], scal[:, TG_F:TG_F + 1], None, ALU.mult).then_inc(sum_step, 1)
                pool.wait_ge(sum_step, 2 * t + 1)
                nc.gpsimd.tensor_tensor(xs0[:, t, :], xs0[:, t, :], hs0[:, t, :], ALU.add).then_inc(sum_step, 1)


        @block.vector
        def _(dve):
            V = nc.vector
            count = [0]
            norms = [0]

            def step(ins, name=None, wait=True):
                count[0] += 1
                ins.then_inc(dve_step, 1)
                if wait:
                    dve.wait_ge(dve_step, count[0])
                if name:
                    dve_mark[name] = count[0]

            def norm(ins, wait=True):
                norms[0] += 1
                ins.then_inc(norm_step, 1)
                if wait:
                    dve.wait_ge(norm_step, norms[0])

            def less(dst, src, hi, scale=1.0):
                if scale == 1.0:
                    return V.tensor_tensor(dst, src, hi.bitcast(F32), ALU.subtract)
                return V.scalar_tensor_tensor(out=dst, in0=src, scalar=scale, in1=hi.bitcast(F32),
                                              op0=ALU.mult, op1=ALU.subtract)

            def weight(m, g):
                dve.wait_ge(weight_hi[m], g + 1)
                less(w[m][:, LO, :], raw[:, WSLOT[m], :], w[m][:, HI, :]).then_inc(weight_lo[m], 1)

            def tile_stats(did, src, t, half):
                for k in range(2):
                    did(V.bn_stats(stats[:, t, k, :], src[:, t, k * BANK:(k + 1) * BANK]), wait=(k == 1))
                did(V.bn_aggr(moments[:, half * QT + t, :], stats[:, t, :, :]), wait=(t == QT - 1))

            def make_rstd(did, half, std_sem, std_count):
                s = lambda i: token[:, i, half * QT:half * QT + QT]
                did(V.tensor_scalar(s(VAR1), var_of(half), EPS, None, ALU.add))
                dve.wait_ge(std_sem, std_count)
                did(V.reciprocal(s(R0), s(STD)))
                did(V.tensor_tensor(s(V1), s(VAR1), s(R0), ALU.mult))
                did(V.tensor_tensor(s(V2), s(V1), s(R0), ALU.mult))
                did(V.tensor_scalar(s(V3), s(V2), -0.5, 1.5, ALU.mult, ALU.add))
                did(V.tensor_tensor(s(RSTD), s(R0), s(V3), ALU.mult))

            def normalise(dst, src, half, t):
                tile = half * QT + t
                return V.tensor_scalar(dst, src, moments[:, tile, 0:1], token[:, RSTD, tile:tile + 1],
                                       ALU.subtract, ALU.mult)

            def x_stats(b, t):
                dve.wait_ge(x_load[t], DMA * (b + 1))
                tile_stats(norm, probs, t, 0)

            def head_out(g):
                dve.wait_ge(oT_hi, g + 1)
                less(oT[:, LO, :], head_ps[:, :], oT[:, HI, :]).then_inc(oT_lo, 1)

            def make_coef(g):
                dve.wait_ge(exp_done, QT * g + QT)
                V.tensor_scalar(safe_sum, rowsum, LEAST_SUM, None, ALU.max).then_inc(coef_step, 1)
                dve.wait_ge(coef_step, 3 * g + 1)
                V.reciprocal(recip, safe_sum).then_inc(coef_step, 1)
                dve.wait_ge(coef_step, 3 * g + 2)
                V.tensor_scalar(coef, recip, scal[:, TG_X:TG_X + 1], None, ALU.mult).then_inc(coef_step, 1)

            def add_out(g, i, banks=1):
                if i == 0:
                    dve.wait_ge(coef_step, 3 * g + 3)
                dve.wait_ge(y_ps, YG * g + i + 1)
                qt, cols = i // 2, slice((i % 2) * BANK, (i % 2 + 1) * BANK)
                V.scalar_tensor_tensor(out=y[:, qt, cols], in0=OUT_BANKS[banks][i % banks][:, :], scalar=coef[:, qt:qt + 1],
                                       in1=y[:, qt, cols], op0=ALU.mult, op1=ALU.add).then_inc(y_sb, 1)

            def take(k):
                if order[k][4]:
                    dve.wait_ge(turned_hi, k + 1)
                    less(order[k][2](LO), f_source(k), order[k][2](HI)).then_inc(turned_lo, 1)

            def h_tile(half, t):
                step(normalise(hs[half][:, t, :], xs[half][:, t, :], half, t), f"h{half * QT + t}", wait=False)

            def var_h(half):
                s = lambda i: token[:, i, half * QT:half * QT + QT]
                step(V.tensor_tensor(s(V1), var_of(half), s(RSTD), ALU.mult))
                step(V.tensor_tensor(s(U), s(V1), s(RSTD), ALU.mult), "var_h", wait=False)

            def pick(half, t):
                tile = half * QT + t
                dve.wait_ge(slot_sb, tile + 1)
                if half:
                    dve.wait_ge(prob_done, QT)
                router = scores[:, t, 0, :]
                step(V.max(top8[:, t, :], router))
                step(V.match_replace(kept[:, t, :], top8[:, t, :], router, MASKED))
                step(V.tensor_tensor(kept[:, t, :], kept[:, t, :], router, ALU.is_equal))
                step(V.scalar_tensor_tensor(out=attn[:, t, :], in0=kept[:, t, :], scalar=MASKED,
                                            in1=scores[:, t, 1, :], op0=ALU.mult, op1=ALU.add))
                step(V.tensor_reduce(negmax_f[:, t:t + 1], attn[:, t, :], AX_X, ALU.max, negate=True), f"attn{tile}", wait=False)

            def mean_logvar():
                dve.wait_ge(learned_ps, 1)
                dve.wait_ge(act_step, act_mark["sig0"])
                m = lambda i: scal[:, i:i + 1]
                step(V.tensor_reduce(m(MEAN_0), F_MISC[:, P + 32:P + 32 + T], AX_X, ALU.add), "sum")
                step(V.tensor_scalar(m(MEAN_1), m(MEAN_0), 2.0 / (B * S), 2e-6, ALU.mult, ALU.add))
                step(V.reciprocal(m(MEAN_2), m(MEAN_1)))

            def gate_in(half):
                s = lambda i: token[:, i, half * QT:half * QT + QT]
                step(V.tensor_scalar(s(NORM), s(LOGVAR), scal[:, MEAN_2:MEAN_2 + 1], None, ALU.mult))
                dve.wait_ge(act_step, act_mark[f"sig{half}"])
                step(V.tensor_scalar(s(V1), s(SIG), 1.25, 1.25, ALU.mult, ALU.add))
                step(V.tensor_tensor(s(U), s(NORM), s(V1), ALU.add))
                step(V.tensor_scalar(s(U), s(U), 0.0, 5.0, ALU.max, ALU.min))
                step(V.tensor_scalar(s(U), s(U), -TAU_LOW, 1.0 / (TAU_HIGH - TAU_LOW), ALU.add, ALU.mult))
                step(V.tensor_scalar(s(U), s(U), 0.0, 1.0, ALU.max, ALU.min))
                step(V.tensor_scalar(s(V2), s(U), scal[:, W1:W1 + 1], scal[:, GBIAS:GBIAS + 1], ALU.mult, ALU.add),
                     f"gate_in{half}", wait=False)

            def gate_out(half):
                s = lambda i: token[:, i, half * QT:half * QT + QT]
                dve.wait_ge(act_step, act_mark[f"gate{half}"])
                step(V.tensor_scalar(s(V3), s(GATE), 0.5, 0.5, ALU.mult, ALU.add))
                step(V.tensor_scalar(s(V1), s(V3), EARLY_EXIT, None, ALU.is_ge))
                step(V.tensor_tensor(s(V1), s(V1), s(V3), ALU.mult))
                dve.wait_ge(prob_done, QT * (half + 1))
                step(V.reciprocal(s(R0), s(TOTAL)))
                step(V.tensor_tensor(s(V1), s(V1), s(R0), ALU.mult))
                step(V.tensor_scalar(s(COEF), s(V1), scal[:, TG_F:TG_F + 1], None, ALU.mult))

            def mix(half):
                dve.wait_ge(mix_hi, half + 1)
                less(mixT[:, half, LO, :], F_QUERY[0:VB, :], mixT[:, half, HI, :]).then_inc(mix_lo, 1)

            def memory_out(half):
                for t in range(QT):
                    tile = half * QT + t
                    for n in range(2):
                        if half == 0:
                            dve.wait_ge(sum_step, 2 * t + 2)
                        dve.wait_ge(aux_ps, 2 * tile + n + 1)
                        cols = slice(n * BANK, (n + 1) * BANK)
                        V.scalar_tensor_tensor(out=xs[half][:, t, cols], in0=F_SCORES[n][:, :], scalar=token[:, COEF, tile:tile + 1],
                                               in1=xs[half][:, t, cols], op0=ALU.mult, op1=ALU.add).then_inc(out_done, 1)

            def rest():
                dve.wait_ge(weight_lo["o"], ALL)
                step(V.memset(queryT[BOT:BOT + 1, :], 1.0), "ones", wait=False)
                head_out(ALL - 1)
                for i in range(YG):
                    add_out(ALL - 1, i)
                    if i % 2:
                        dve.wait_ge(y_sb, YG * (ALL - 1) + i + 1)
                        tile_stats(step, y, i // 2, 1)
                dve_mark["var1"] = count[0]
                make_rstd(step, 1, act_step, act_mark["std1"])
                var_h(1)
                for t in range(QT):
                    h_tile(1, t)
                pick(0, 0)
                pick(0, 1)
                for k in range(FILLS[-1][-1] + 1, H1):
                    take(k)
                pick(0, 2)
                pick(0, 3)
                for k in range(H1, P0):
                    take(k)
                mean_logvar()
                gate_in(0)
                dve.wait_ge(gate_done, 3)
                for t in range(QT):
                    dve.wait_ge(turned, H1 + 2 * t + 2)
                    step(V.scalar_tensor_tensor(out=y[:, t, :], in0=hs1[:, t, :], scalar=scal[:, TG_F:TG_F + 1], in1=y[:, t, :],
                                                op0=ALU.mult, op1=ALU.add), wait=False)
                gate_out(0)
                pick(1, 0)
                pick(1, 1)
                mix(0)
                pick(1, 2)
                pick(1, 3)
                gate_in(1)
                memory_out(0)
                mix(1)
                gate_out(1)
                memory_out(1)

            def attend(halves):
                KT, W, GC, G, KQ = sizes(halves)
                count[0], norms[0] = INIT, 0
                out_banks = 3 - halves
                TURN_V = 7 - halves

                def kq(g, part_):
                    dve.wait_ge(kq_hi, KQ * g + part_ + 1)
                    if part_ < halves:
                        cols = slice(part_ * BANK, (part_ + 1) * BANK)
                        ins = less(kT[:, LO, cols], K_BANK[part_][:, :], kT[:, HI, cols])
                    else:
                        ins = less(qT[:, LO, :], Q_BANK[halves][:, :], qT[:, HI, :], SCALE)
                    ins.then_inc(kq_lo, 1)

                def start_group(b, k):
                    dve.wait_ge(start_hi, G * b + k + 1)
                    tile, c = k // 2, 4 * (k % 2)
                    dst = (ctxT[:, :, c:c + 4, tile * P:(tile + 1) * P] if tile < KT
                           else xnT[:, :, c:c + 4, (tile - KT) * P:(tile - KT + 1) * P])
                    less(dst[:, LO], START_BANKS[start_bank(k, GC)].rearrange("p (c n) -> p c n", n=P), dst[:, HI]).then_inc(start_lo, 1)

                def start(b, g):
                    if b == 0:
                        weight("k", 0)
                        for k in range(GC):
                            start_group(b, k)
                        weight("v", 0)
                        kq(g, 0)
                        weight("q", 0)
                        for t in range(QT):
                            x_stats(b, t)
                    if b or halves == 2:
                        kq(g, halves - 1)
                    make_rstd(norm, 0, std_done, b + 1)
                    for t in range(QT):
                        normalise(probs[:, t, :], probs[:, t, :], 0, t).then_inc(xn_done, 1)
                    dve.wait_ge(mask_load, DMA * (b + 1))
                    if b:
                        dve.wait_ge(bias_masked, QT * g)
                    for k in range(GC, G):
                        start_group(b, k)
                        if k % 2 == 0:
                            qt = (k - GC) // 2
                            V.tensor_scalar(hide[:, qt, 0:W], mask_in[:, qt, 0:W], 0.0, MASKED,
                                            ALU.is_equal, ALU.mult).then_inc(hide_done, 1)
                    kq(g, halves)

                def score(g, qt):
                    if qt == 0:
                        dve.wait_ge(p_turned, KT * g)
                    dve.wait_ge(score_done, QT * g + qt + 1)
                    dve.wait_ge(bias_masked, QT * g + qt + 1)
                    dve.sem_inc(went_on["dve"], 1)
                    src = score_ps[:, :] if halves == 2 else score_half[qt % 2]
                    V.tensor_tensor_reduce(probs[:, qt, 0:W], src, bias_slot(qt, halves)[1], -1.0, NO_SCORE,
                                           ALU.add, ALU.min, negmax[:, qt:qt + 1]).then_inc(score_sb, 1)

                def v_half(g, half):
                    dve.wait_ge(v_hi, halves * g + half + 1)
                    less(v[:, LO, 4 * half:4 * half + 4, :].rearrange("p t d -> p (t d)"), turn_ps[half][:, :],
                         v[:, HI, 4 * half:4 * half + 4, :].rearrange("p t d -> p (t d)")).then_inc(v_lo, 1)

                def pT_tile(g, kt):
                    dve.wait_ge(pT_hi, KT * g + kt + 1)
                    less(pT[:, kt % 2, LO, :], turn_ps[kt % 2][:, :], pT[:, kt % 2, HI, :]).then_inc(pT_lo, 1)

                def head(g, first, last):
                    final = last and g == ALL - 1
                    if not first:
                        head_out(g - 1)
                    for i in range(8):
                        if i % 2 == halves - 1:
                            score(g, i // 2)
                        if not first:
                            add_out(g - 1, i, out_banks)
                        if i == 1 and not final:
                            weight("k", g + 1)
                        if i == 3 and not final:
                            weight("q", g + 1)
                        if final and 2 <= i < 6:
                            if i == 2:
                                arrived(dve, "x")
                            tile_stats(step, xs0, i - 2, 0)
                            if i == 5:
                                dve_mark["var0"] = count[0]
                        if i == TURN_V:
                            v_half(g, 0)
                        if final and i == 6:
                            make_rstd(step, 0, act_step, act_mark["std0"])
                            var_h(0)
                            h_tile(0, 0)
                        if final and i == 7:
                            h_tile(0, 1)
                    if halves == 2:
                        v_half(g, 1)
                    make_coef(g)
                    if final:
                        h_tile(0, 2)
                        h_tile(0, 3)

                    def fill(i):
                        if final:
                            for k in fill_groups(i, halves):
                                take(k)
                        elif last:
                            start_group(1, 2 * i)
                            start_group(1, 2 * i + 1)

                    fill(0)
                    pT_tile(g, 0)
                    pT_tile(g, 1)
                    if not final:
                        weight("v", g + 1)
                    for kt in range(KT):
                        if kt + 1 < KT:
                            fill(kt + 1)
                        if kt + 2 < KT:
                            pT_tile(g, kt + 2)
                        if not last and kt in KQ_AT[halves]:
                            kq(g + 1, KQ_AT[halves][kt])
                        if kt == halves - 1:
                            weight("o", g)
                    if first:
                        dve.wait_ge(y_load, DMA * (g // H + 1))
                    if last and not final:
                        if halves == 2:
                            kq(g + 1, 0)
                        head_out(g)
                        for i in range(YG):
                            add_out(g, i)
                            if i >= 4:
                                x_stats(1, i - 4)

                run_heads(dve, start, head)

            def make_plan():
                def plan_it(n, ins):
                    ins.then_inc(plan_step, 1)
                    dve.wait_ge(plan_step, n)

                dve.wait_ge(mask_all_load, DMA)
                words = mask_all[:, :, :, :].bitcast(I32)
                for b in range(B):
                    for half in range(2):
                        V.tensor_reduce(seen[:, 2 * b + half:2 * b + half + 1],
                                        words[:, b, :, half * BANK // 4:(half + 1) * BANK // 4], AX_XY, ALU.max).then_inc(seen_done, 1)
                dve.wait_ge(seen_ps, 1)
                plan_it(1, V.tensor_copy(seen[:, 4:8], out_ps[:, 0:2 * B]))
                plan_it(2, V.tensor_tensor(seen[:, 0:2], seen[:, 4:8:2], seen[:, 5:8:2], ALU.min))
                plan_it(3, V.tensor_tensor(seen[:, 2:3], seen[:, 0:1], seen[:, 1:2], ALU.max))
                plan_it(4, V.tensor_scalar(plan[:, ALL_SEEN:ALL_SEEN + 1], seen[:, 2:3], 0.0, None, ALU.is_gt))
                plan_it(5, V.tensor_scalar(plan[:, FIRST_KEY:FIRST_KEY + B], seen[:, 4:8:2], 0.0, float(BANK), ALU.is_le, ALU.mult))
                plan_it(6, V.tensor_scalar(plan[:, FIRST_TILE:FIRST_TILE + B], seen[:, 4:8:2], 0.0, float(HT), ALU.is_le, ALU.mult))

            step(V.memset(scal[:, EPS_C:EPS_C + 1], EPS), wait=False)
            step(V.memset(ones[:, :], 1.0), "init")
            INIT = count[0]
            make_plan()
            dve.wait_ge(gate_done, 1)
            all_seen = dve.value_load(plan[0:1, ALL_SEEN:ALL_SEEN + 1], min_val=0, max_val=1)
            with dve.If(all_seen == 1):
                attend(2)
            with dve.Else():
                attend(1)
            rest()

        @block.tensor
        def _(pe):
            def turn_blocks(dst, blocks):
                for n, blk in enumerate(blocks):
                    last = pe.transpose(dst[:, n * P:(n + 1) * P], blk, ident[:])
                return last

            def product(dst, pairs):
                for n, (a, b) in enumerate(pairs):
                    mm = pe.matmul(dst, a, b, start=(n == 0), stop=(n == len(pairs) - 1))
                return mm

            def split_product(dst, stationary, moving, chunks=(0,)):
                return product(dst, [(stationary(a, c), moving(b, c)) for c in chunks for a, b in PASSES])

            def project(dst, m, src, cols, n):
                c, (a, b) = n // 3, PASSES[n % 3]
                return pe.matmul(dst[:, 0:BANK], w[m][:, a, c * DH:(c + 1) * DH], src[:, b, c, cols],
                                 start=(n == 0), stop=(n == 3 * NC - 1))

            def out_group(g, i, banks=1):
                if i == 0:
                    pe.wait_ge(oT_lo, g + 1)
                    pe.wait_ge(weight_lo["o"], g + 1)
                pe.wait_ge(y_sb, YG * g + i - (banks - 1 if i else 0))
                qt, n = i // 2, i % 2
                split_product(OUT_BANKS[banks][i % banks][:, :], lambda a, c: oT[:, a, qt * P:(qt + 1) * P],
                              lambda b, c: w["o"][:, b, n * BANK:(n + 1) * BANK]).then_inc(y_ps, 1)

            def turn(k):
                need, blocks, _, parts, _ = order[k]
                if k < 2:
                    pe.wait_ge(score_sb, QT * ALL)
                elif order[k - 2][4]:
                    pe.wait_ge(turned_lo, splits(k - 1))
                else:
                    pe.wait_ge(turned_hi, k - 1)
                if isinstance(need, int):
                    pe.wait_ge(dve_step, dve_mark[f"h{need}"])
                elif need == "prob":
                    pe.wait_ge(prob_done, QT if k < P1 else T)
                else:
                    arrived(pe, need)
                col = 0
                for blk, n in blocks:
                    mm = pe.transpose(F_TURN[k % 2][0:parts, col:col + n], blk, ident[0:n, 0:n])
                    col += n
                mm.then_inc(turned, 1)

            def f_fill(i):
                for k in FILLS[i]:
                    turn(k)
                if i == 3:
                    pe.wait_ge(turned_hi, H0)
                    product(F_QUERY[0:RDIM, 0:NSLOT], [(wrT[:, :], keysT[:, :])]).then_inc(product_ps, 1)
                if i == 4:
                    pe.wait_ge(act_step, act_mark["rk"])
                    product(F_QUERY[0:BOT, 0:NSLOT], [(wr_in[:, :], rkT[:, :])]).then_inc(product_ps, 1)

            def query_chunk(half, c):
                if c == 0:
                    pe.wait_ge(turned_lo, splits(H0 + GX if half == 0 else P0))
                    pe.wait_ge(act_step, act_mark["router" if half == 0 else "query0"])
                for n, (a, b) in enumerate(PASSES):
                    mm = pe.matmul(F_QUERY[0:BOT, :], wqT[:, a, c, :], hT[:, b, c, :],
                                   start=(c == 0 and n == 0), stop=(c == NC - 1 and n == 2))
                if c == NC - 1:
                    mm.then_inc(query_ps, 1)

            def units(half, u):
                if half:
                    pe.wait_ge(gelu_done, UT)
                else:
                    pe.wait_ge(oT_lo, ALL)
                split_product(F_UNITS[u][:, :], lambda a, c: wuT[:, a, c, u * P:(u + 1) * P],
                              lambda b, c: hT[:, b, c, :], range(NC)).then_inc(unit_ps, 1)

            def slot_scores(half):
                if half == 0:
                    arrived(pe, "rows")
                    pe.wait_ge(dve_step, dve_mark["ones"])
                    pe.wait_ge(act_step, act_mark["slots"])
                pe.wait_ge(act_step, act_mark[f"query{half}"])
                for t in range(QT):
                    tile = half * QT + t
                    if tile >= 2:
                        pe.wait_ge(slot_sb, tile - 1)
                    pe.matmul(F_SCORES[t % 2][:, :], queryT[:, t * P:(t + 1) * P], slots[:, :, :].rearrange("p a n -> p (a n)"),
                              start=True, stop=True).then_inc(slot_ps, 1)

            def learned(half):
                pe.wait_ge(gelu_done, UT * (half + 1))
                for t in range(QT):
                    tile = half * QT + t
                    mm = product(F_MISC[:, P + tile:P + tile + 1],
                                 [(gelu[:, u, t * P:(t + 1) * P], wu2[:, u:u + 1]) for u in range(UT)])
                return mm

            def mix(half):
                pe.wait_ge(turned_hi, P1 if half == 0 else END)
                if half:
                    pe.wait_ge(mix_lo, 1)
                else:
                    pe.wait_ge(act_step, act_mark["query1"])
                product(F_QUERY[0:VB, :], [(values[:, s, :], probT[:, s, :]) for s in range(ST)]).then_inc(mix_ps, 1)

            def memory_out(half):
                pe.wait_ge(mix_lo, half + 1)
                for t in range(QT):
                    tile = half * QT + t
                    for n in range(2):
                        if tile:
                            pe.wait_ge(out_done, 2 * tile - 1 + n)
                        else:
                            pe.wait_ge(slot_sb, T)
                        split_product(F_SCORES[n][:, :], lambda a, c: mixT[:, half, a, t * P:(t + 1) * P],
                                      lambda b, c: wvuT[:, b, n * BANK:(n + 1) * BANK]).then_inc(aux_ps, 1)

            def rest():
                query_chunk(0, 0)
                query_chunk(0, 1)
                for i in range(YG):
                    out_group(ALL - 1, i)
                    if i + 2 < NC:
                        query_chunk(0, i + 2)
                for u in range(UT):
                    units(0, u)
                slot_scores(0)
                for k in range(FILLS[-1][-1] + 1, H1):
                    turn(k)
                pe.wait_ge(turned_hi, H1 - 2)
                pe.wait_ge(y_sb, YG * ALL)
                for s in range(ST):
                    mm = product(F_MISC[:, s * VB:(s + 1) * VB], [(avT[:, c, s * P:(s + 1) * P], wvdT[:, c, :]) for c in range(NC)])
                mm.then_inc(product_ps, 1)
                for k in range(H1, P0):
                    turn(k)
                pe.wait_ge(act_step, act_mark["logvar"])
                learned(0)
                product(F_MISC[:, P + 32:P + 32 + T], [(ones[:, :], token[:, LOGVAR, :])]).then_inc(learned_ps, 1)
                for c in range(NC):
                    query_chunk(1, c)
                units(1, 0)
                slot_scores(1)
                for k in range(P0, P1):
                    turn(k)
                mix(0)
                units(1, 1)
                pe.wait_ge(dve_step, dve_mark["sum"])
                learned(1).then_inc(learned_ps, 1)
                memory_out(0)
                for k in range(P1, END):
                    turn(k)
                mix(1)
                memory_out(1)

            def attend(halves):
                KT, W, GC, G, KQ = sizes(halves)
                out_banks = 3 - halves
                TURN_V = 7 - halves

                def kq(g, n, bank_free):
                    part_, n = n // (3 * NC), n % (3 * NC)
                    if n == 0:
                        pe.wait_ge(weight_lo["q" if part_ == halves else "k"], g + 1)
                        pe.wait_ge(*bank_free[part_])
                    if part_ < halves:
                        mm = project(K_BANK[part_], "k", ctxT, slice(part_ * BANK, (part_ + 1) * BANK), n)
                    else:
                        mm = project(Q_BANK[halves], "q", xnT, slice(0, S), n)
                    if n == 3 * NC - 1:
                        mm.then_inc(kq_ps, 1)

                def kq_chunk(b, part_, c):
                    g = b * H
                    if c == 0:
                        pe.wait_ge(start_lo, G * b + (G if part_ == halves else 2 * HT * (part_ + 1)))
                    if halves == 2:
                        free = ((kq_lo, 3 * g), (start_lo, G * b + GC), (kq_lo, 3 * g + 1))
                    else:
                        free = ((vT_sb, g), (start_lo, G * b + GC))
                    for n in range(3 * c, 3 * c + 3):
                        kq(g, part_ * 3 * NC + n, free)

                def start_group(b, k):
                    g, tile, half = b * H, k // 2, k % 2
                    before = start_bank_before(k, GC)
                    if before is not None:
                        pe.wait_ge(start_lo, G * b + before + 1)
                    elif b:
                        last_use = (vT_sb, 2 * g - 1) if halves == 2 else (y_sb, YG * (g - 1))
                        pe.wait_ge(*((score_sb, QT * g), (score_sb, QT * g), last_use, (pT_lo, KT * g), (pT_lo, KT * g))[start_bank(k, GC)])
                    if tile < KT:
                        pe.wait_ge(ctx_load[tile], DMA * (b + 1))
                        src = stage[:, tile, :]
                    else:
                        pe.wait_ge(xn_done, QT * b + tile - KT + 1)
                        src = probs[:, tile - KT, :]
                    turn_blocks(START_BANKS[start_bank(k, GC)],
                                [src[:, (4 * half + c) * P:(4 * half + c + 1) * P] for c in range(4)]).then_inc(start_ps, 1)

                def v_mms(g, half, ns):
                    if ns[0] == 0 and half == 0:
                        pe.wait_ge(weight_lo["v"], g + 1)
                        pe.wait_ge(kq_lo, KQ * g + halves)
                    if ns[0] == 0 and half == 1:
                        pe.wait_ge(oT_lo, g)
                    for n in ns:
                        mm = project(V_BANK[halves][half], "v", ctxT, slice(half * BANK, (half + 1) * BANK), n)
                    if ns[-1] == 3 * NC - 1:
                        mm.then_inc(v_ps, 1)

                def turn_v(g, half):
                    pe.wait_ge(vT_sb, halves * g + half + 1)
                    pe.wait_ge(pT_lo, KT * g)
                    if half == 0 and isinstance(g, int) and g % H == 0:
                        pe.wait_ge(start_lo, G * (g // H) + G)
                    turn_blocks(turn_ps[half], [vT[:, k * P:(k + 1) * P] for k in range(4)]).then_inc(v_turned, 1)

                def turn_p(g, kt):
                    if kt == 0:
                        pe.wait_ge(exp_done, QT * g + QT)
                    if kt < halves:
                        pe.wait_ge(v_lo, halves * g + kt + 1)
                    elif kt >= 2:
                        pe.wait_ge(pT_lo, KT * g + kt - 1)
                    turn_blocks(turn_ps[kt % 2], [probs[:, qt, kt * P:(kt + 1) * P] for qt in range(QT)]).then_inc(p_turned, 1)

                def pv(g, kt):
                    pe.wait_ge(pT_lo, KT * g + kt + 1)
                    if kt == 0:
                        pe.wait_ge(v_lo, halves * g + halves)
                        pe.wait_ge(vT_sb, halves * g + halves)
                    for a, b in PASSES:
                        mm = pe.matmul(head_ps[:, :], v[:, a, kt, :], pT[:, kt % 2, b, :],
                                       start=(kt == 0 and (a, b) == PASSES[0]), stop=(kt == KT - 1 and (a, b) == PASSES[-1]))
                    mm.then_inc(pv_done, 1)

                def start(b, g):
                    if b == 0:
                        for k in range(2 * HT):
                            start_group(b, k)
                        for c in range(NC):
                            if halves == 2:
                                start_group(b, 2 * HT + c)
                            kq_chunk(b, 0, c)
                        if halves == 2:
                            for c in range(NC):
                                kq_chunk(b, 1, c)
                    v_mms(g, 0, range(3 * NC))
                    for k in range(GC, G):
                        start_group(b, k)
                    for c in range(NC):
                        kq_chunk(b, halves, c)

                def head(g, first, last):
                    final = last and g == ALL - 1
                    for i in range(8):
                        qt, sh = i // 2, i % 2
                        if halves == 2 and not (first and i < 4):
                            v_mms(g, i // 4, range(6 * (i % 4), 6 * (i % 4) + 6))
                        if halves == 1 and not first and i < 6:
                            v_mms(g, 0, range(4 * i, 4 * i + 4))
                        if i == 0:
                            pe.wait_ge(kq_lo, KQ * g + KQ)
                            if first:
                                pe.wait_ge(start_lo, G * (g // H) + G)
                        if halves == 1:
                            if sh == 0:
                                if not first or qt >= 2:
                                    pe.wait_ge(score_sb, QT * g + qt - 1)
                                split_product(score_half[qt % 2], lambda a, c: qT[:, a, qt * P:(qt + 1) * P],
                                              lambda b, c: kT[:, b, 0:BANK]).then_inc(score_done, 1)
                        else:
                            if sh == 0:
                                pe.wait_ge(score_sb, QT * g + qt)
                            mm = split_product(score_half[sh], lambda a, c: qT[:, a, qt * P:(qt + 1) * P],
                                               lambda b, c: kT[:, b, sh * BANK:(sh + 1) * BANK])
                            if sh:
                                mm.then_inc(score_done, 1)
                        if not first:
                            out_group(g - 1, i, out_banks)
                        if i == TURN_V:
                            turn_v(g, 0)
                    if halves == 2:
                        turn_v(g, 1)

                    def fill(i):
                        if final:
                            for n in ((i,) if halves == 2 else (2 * i, 2 * i + 1)):
                                f_fill(n)
                        elif last:
                            for k in (2 * i, 2 * i + 1):
                                start_group(1, k)
                            if i >= 4:
                                for c in (2 * (i - 4), 2 * (i - 4) + 1):
                                    kq_chunk(1, 0, c)
                        else:
                            if halves == 2:
                                free = ((kq_lo, 3 * g + 3), (vT_sb, 2 * g + 1), (kq_lo, 3 * g + 4))
                            else:
                                free = ((vT_sb, g + 1), (y_sb, YG * g))
                            share = 3 * NC * KQ // KT
                            for n in range(share * i, share * i + share):
                                kq(g + 1, n, free)

                    fill(0)
                    turn_p(g, 0)
                    turn_p(g, 1)
                    for kt in range(KT):
                        if kt + 1 < KT:
                            fill(kt + 1)
                        pv(g, kt)
                        if kt + 2 < KT:
                            turn_p(g, kt + 2)
                    if last and not final:
                        kq_chunk(1, halves - 1, 0)
                        for i in range(YG):
                            if i + 1 < NC:
                                kq_chunk(1, halves - 1, i + 1)
                            out_group(g, i)

                run_heads(pe, start, head)

            pe.wait_ge(dve_step, dve_mark["init"])
            pe.wait_ge(seen_done, 2 * B)
            pe.matmul(out_ps[:, 0:2 * B], ones[:, :], seen[:, 0:2 * B], start=True, stop=True).then_inc(seen_ps, 1)
            pe.wait_ge(ident_done, 2)
            pe.wait_ge(plan_step, PLANNED)
            all_seen = pe.value_load(plan[0:1, ALL_SEEN:ALL_SEEN + 1], min_val=0, max_val=1)
            with pe.If(all_seen == 1):
                attend(2)
            with pe.Else():
                attend(1)
            rest()

        @block.scalar
        def _(act):
            A = nc.scalar
            count = [0]

            def step(ins, name):
                count[0] += 1
                ins.then_inc(act_step, 1)
                assert act_mark[name] == count[0], (name, count[0])

            def copy(dst, src, scale=1.0):
                return A.activation(dst, src, ACT.Copy, scale=scale)

            def weight(m, g, free):
                act.wait_ge(weight_in[m], DMA * g + DMA)
                act.wait_ge(*free)
                copy(w[m][:, HI, :], raw[:, WSLOT[m], :]).then_inc(weight_hi[m], 1)

            def take(k):
                act.wait_ge(turned, k + 1)
                if k == P1:
                    act.wait_ge(mix_ps, 1)
                if k == H1:
                    act.wait_ge(unit_ps, UT)
                    act.wait_ge(query_ps, 1)
                copy(order[k][2](HI), f_source(k)).then_inc(turned_hi, 1)

            def std(half):
                act.wait_ge(dve_step, dve_mark[f"var{half}"])
                cols = slice(half * QT, half * QT + QT)
                step(A.activation(token[:, STD, cols], var_of(half), ACT.Sqrt, bias=scal[:, EPS_C:EPS_C + 1]), f"std{half}")

            def f_fill(i):
                for k in FILLS[i]:
                    take(k)
                if i == 3:
                    act.wait_ge(product_ps, 1)
                    step(copy(rkT[:, :], F_QUERY[0:RDIM, 0:NSLOT]), "rk")
                if i == 4:
                    act.wait_ge(product_ps, 2)
                    act.wait_ge(weight_lo["o"], ALL)
                    step(copy(slots[0:BOT, 0, :], F_QUERY[0:BOT, 0:NSLOT], float(RDIM) ** -0.5), "router")
                    step(copy(slots[0:BOT, 1, :], keysT[:, :], float(BOT) ** -0.5), "slots")

            def query(half):
                act.wait_ge(query_ps, half + 1)
                if half:
                    act.wait_ge(slot_ps, QT)
                step(copy(queryT[0:BOT, :], F_QUERY[0:BOT, :]), f"query{half}")

            def slot_tiles(half):
                for t in range(QT):
                    act.wait_ge(slot_ps, half * QT + t + 1)
                    if half:
                        act.wait_ge(dve_step, dve_mark[f"attn{t}"])
                    copy(scores[:, t, :, :].rearrange("p a n -> p (a n)"), F_SCORES[t % 2][:, :]).then_inc(slot_sb, 1)

            def units(half, u):
                act.wait_ge(unit_ps, half * UT + u + 1)
                if half:
                    act.wait_ge(learned_ps, 1)
                A.activation(gelu[:, u, :], F_UNITS[u][:, :], ACT.Gelu_apprx_tanh, bias=bu[:, u:u + 1]).then_inc(gelu_done, 1)

            def weigh(half):
                for t in range(QT):
                    tile = half * QT + t
                    act.wait_ge(dve_step, dve_mark[f"attn{tile}"])
                    if half and t == 0:
                        act.wait_ge(turned, P1)
                    A.activation(prob[:, t, :], attn[:, t, :], ACT.Exp, bias=negmax_f[:, t:t + 1],
                                 accum_out=token[:, TOTAL, tile:tile + 1]).then_inc(prob_done, 1)

            def sig(half):
                act.wait_ge(learned_ps, half + 1)
                cols = slice(half * QT, half * QT + QT)
                step(A.activation(token[:, SIG, cols], F_MISC[:, P + half * QT:P + half * QT + QT], ACT.Tanh, scale=0.5,
                                  bias=scal[:, HALF_BU2:HALF_BU2 + 1]), f"sig{half}")

            def gate(half):
                act.wait_ge(dve_step, dve_mark[f"gate_in{half}"])
                cols = slice(half * QT, half * QT + QT)
                step(A.activation(token[:, GATE, cols], token[:, V2, cols], ACT.Tanh, scale=0.5), f"gate{half}")

            def mix(half):
                act.wait_ge(mix_ps, half + 1)
                copy(mixT[:, half, HI, :], F_QUERY[0:VB, :]).then_inc(mix_hi, 1)

            def rest():
                arrived(act, "small")
                A.activation(scal[:, TG_F:TG_F + 1], scal[:, G_F:G_F + 1], ACT.Tanh).then_inc(gate_done, 1)
                copy(scal[:, HALF_BU2:HALF_BU2 + 1], scal[:, BU2:BU2 + 1], 0.5).then_inc(gate_done, 1)
                query(0)
                std(1)
                for u in range(UT):
                    units(0, u)
                slot_tiles(0)
                for k in range(FILLS[-1][-1] + 1, H1):
                    take(k)
                act.wait_ge(product_ps, 3)
                step(copy(values[:, :, :].rearrange("p s v -> p (s v)"), F_MISC[:, 0:ST * VB]), "values")
                act.wait_ge(dve_step, dve_mark["var_h"])
                step(A.activation(token[:, LOGVAR, :], token[:, U, :], ACT.Ln, bias=ones[:, 0:1]), "logvar")
                for k in range(H1, P0):
                    take(k)
                weigh(0)
                sig(0)
                query(1)
                gate(0)
                units(1, 0)
                slot_tiles(1)
                for k in range(P0, P1):
                    take(k)
                mix(0)
                units(1, 1)
                weigh(1)
                sig(1)
                for k in range(P1, END):
                    take(k)
                mix(1)
                gate(1)

            act.wait_ge(g_in, DMA)
            A.activation(scal[:, TG_X:TG_X + 1], scal[:, G_X:G_X + 1], ACT.Tanh).then_inc(gate_done, 1)
            def attend(halves):
                KT, W, GC, G, KQ = sizes(halves)
                count[0] = 0

                def kq(g, part_):
                    act.wait_ge(kq_ps, KQ * g + part_ + 1)
                    act.wait_ge(score_done, QT * g)
                    if part_ < halves:
                        ins = copy(kT[:, HI, part_ * BANK:(part_ + 1) * BANK], K_BANK[part_][:, :])
                    else:
                        ins = copy(qT[:, HI, :], Q_BANK[halves][:, :], SCALE)
                    ins.then_inc(kq_hi, 1)

                def start_group(b, k):
                    act.wait_ge(start_ps, G * b + k + 1)
                    if k == 0:
                        act.wait_ge(v_ps, halves * H * b)
                    if k == GC:
                        act.wait_ge(kq_ps, KQ * H * b)
                    tile, c = k // 2, 4 * (k % 2)
                    dst = (ctxT[:, HI, c:c + 4, tile * P:(tile + 1) * P] if tile < KT
                           else xnT[:, HI, c:c + 4, (tile - KT) * P:(tile - KT + 1) * P])
                    copy(dst, START_BANKS[start_bank(k, GC)].rearrange("p (c n) -> p c n", n=P)).then_inc(start_hi, 1)

                def start(b, g):
                    if b == 0:
                        weight("k", 0, (kq_ps, 0))
                        for k in range(GC):
                            start_group(b, k)
                        weight("v", 0, (v_ps, 0))
                        kq(g, 0)
                        weight("q", 0, (kq_ps, 0))
                    if b or halves == 2:
                        kq(g, halves - 1)
                    act.wait_ge(norm_step, STATS_STEPS + b * (STATS_STEPS + RSTD_STEPS))
                    A.activation(token[:, STD, 0:QT], var_of(0), ACT.Sqrt, bias=scal[:, EPS_C:EPS_C + 1]).then_inc(std_done, 1)
                    vT_half(g, 0)
                    for k in range(GC, G):
                        start_group(b, k)
                    kq(g, halves)

                def head_out(g):
                    act.wait_ge(pv_done, KT * g + KT)
                    act.wait_ge(y_ps, YG * g)
                    copy(oT[:, HI, :], head_ps[:, :]).then_inc(oT_hi, 1)

                def exp(g, qt):
                    act.wait_ge(score_sb, QT * g + qt + 1)
                    if qt == 0:
                        act.wait_ge(coef_step, 3 * g)
                    A.activation(probs[:, qt, 0:W], probs[:, qt, 0:W], ACT.Exp, bias=negmax[:, qt:qt + 1], scale=-1.0,
                                 accum_out=rowsum[:, qt:qt + 1]).then_inc(exp_done, 1)

                def vT_half(g, half):
                    act.wait_ge(v_ps, halves * g + half + 1)
                    act.wait_ge(v_turned, halves * g + half)
                    copy(vT[:, :], V_BANK[halves][half][:, :]).then_inc(vT_sb, 1)

                def v_half(g, half):
                    act.wait_ge(v_turned, halves * g + half + 1)
                    act.wait_ge(pv_done, KT * g)
                    copy(v[:, HI, 4 * half:4 * half + 4, :].rearrange("p t d -> p (t d)"), turn_ps[half][:, :]).then_inc(v_hi, 1)

                def pT_tile(g, kt):
                    act.wait_ge(p_turned, KT * g + kt + 1)
                    act.wait_ge(pv_done, KT * g + max(kt - 1, 0))
                    copy(pT[:, kt % 2, HI, :], turn_ps[kt % 2][:, :]).then_inc(pT_hi, 1)

                def head(g, first, last):
                    final = last and g == ALL - 1
                    if not first:
                        head_out(g - 1)
                    if not final:
                        weight("k", g + 1, (kq_ps, KQ * g + halves))
                    exp(g, 0)
                    if halves == 2 and not first:
                        vT_half(g, 0)
                    exp(g, 1)
                    if not final:
                        weight("q", g + 1, (kq_ps, KQ * g + KQ))
                    exp(g, 2)
                    if halves == 2:
                        v_half(g, 0)
                    elif not first:
                        vT_half(g, 0)
                    if final:
                        std(0)
                    if halves == 2:
                        vT_half(g, 1)
                    exp(g, 3)
                    v_half(g, halves - 1)

                    def fill(i):
                        if final:
                            for n in ((i,) if halves == 2 else (2 * i, 2 * i + 1)):
                                f_fill(n)
                        elif last:
                            start_group(1, 2 * i)
                            start_group(1, 2 * i + 1)

                    fill(0)
                    pT_tile(g, 0)
                    pT_tile(g, 1)
                    if not final:
                        weight("v", g + 1, (v_ps, halves * (g + 1)))
                    for kt in range(KT):
                        if kt + 1 < KT:
                            fill(kt + 1)
                        if kt + 2 < KT:
                            pT_tile(g, kt + 2)
                        if not last and kt in KQ_AT[halves]:
                            kq(g + 1, KQ_AT[halves][kt])
                        if kt == halves - 1:
                            weight("o", g, (y_ps, YG * g))
                    if last:
                        if not final and halves == 2:
                            kq(g + 1, 0)
                        head_out(g)

                run_heads(act, start, head)

            act.wait_ge(plan_step, PLANNED)
            all_seen = act.value_load(plan[0:1, ALL_SEEN:ALL_SEEN + 1], min_val=0, max_val=1)
            with act.If(all_seen == 1):
                attend(2)
            with act.Else():
                attend(1)
            rest()


_INS = ["x", "ctx_4096", "fside_Bx32xSxS2_0", "mask_BxSxS2_bk0", "g_xattn", "g_ffn",
        "L0_xattn_Wq", "L0_xattn_Wk", "L0_xattn_Wv", "L0_xattn_Wo", "L0_ffn_Wq", "L0_ffn_Wr",
        "L0_ffn_aux_keys", "L0_ffn_aux_values", "L0_ffn_Wvd", "L0_ffn_Wvu", "L0_ffn_Wu1", "L0_ffn_bu1",
        "L0_ffn_Wu2", "L0_ffn_bu2", "L0_ffn_gate_w1", "L0_ffn_gate_bias", "L0_ffn_log_rel"]


def kernel(**inputs):
    import numpy as _np
    import concourse.bacc as _bacc
    from concourse import mybir as _mybir
    from concourse.bass_utils import run_bass_kernel_spmd as _run

    nc = _bacc.Bacc("TRN2", target_bir_lowering=False, num_devices=1, dynamic_dma_scratch_size=1024)
    arrays, args = {}, []
    for name in _INS:
        a = _np.ascontiguousarray(inputs[name])
        a = a.reshape(a.shape or (1,))
        arrays[f"in_{name}_dram"] = a
        args.append(nc.dram_tensor(f"in_{name}_dram", a.shape, _mybir.dt.from_np(a.dtype), kind="ExternalInput").ap())
    shape = inputs["x"].shape
    args.append(nc.dram_tensor("out_0_dram", shape, _mybir.dt.float32, kind="ExternalOutput").ap())
    program(nc, *args)
    r = _run(nc, [arrays], core_ids=[0])
    return r.results[0]["out_0_dram"]
```

```python
from contextlib import ExitStack

import concourse.bass as bass
from concourse import mybir

ALU = mybir.AluOpType
ACT = mybir.ActivationFunctionType
AX_X = mybir.AxisListType.X
AX_XY = mybir.AxisListType.XY
F32 = mybir.dt.float32
F32R = mybir.dt.float32r
BF16 = mybir.dt.bfloat16
U8 = mybir.dt.uint8
I32 = mybir.dt.int32

P = 128
BANK = 512
KB = 1024
DMA = 16
EPS = 1e-5
MASKED = -3e38
NO_SCORE = 1.5e38
LEAST_SUM = 1e-30
HI, LO = 0, 1
PASSES = ((HI, HI), (HI, LO), (LO, HI))
HEADS_PER_TURN = 5


def program(nc, x, ctx_in, bias, mask, g_xattn, g_ffn, Wq, Wk, Wv, Wo, ffn_Wq, ffn_Wr, ffn_keys, ffn_values,
            ffn_Wvd, ffn_Wvu, ffn_Wu1, ffn_bu1, ffn_Wu2, ffn_bu2, ffn_gate_w1, ffn_gate_bias, ffn_log_rel, out):
    B, S, D = x.shape
    SK = ctx_in.shape[1]
    H = bias.shape[1]
    DH = Wq.shape[1] // H
    NC = D // P
    QT = S // P
    KT = SK // P
    KH = SK // BANK
    YG = QT * (D // BANK)
    SCALE = float(DH) ** -0.5
    TURNS = (H - 2) // HEADS_PER_TURN
    QUARTER = SK // 4
    T = B * QT
    HT = BANK // P
    GX = 2 * QT
    ALL = B * H
    BOT, RDIM, NSLOT, VB, NU = ffn_Wq.shape[0], ffn_Wr.shape[0], ffn_keys.shape[0], ffn_Wvd.shape[0], ffn_Wu1.shape[0]
    UT = NU // P
    ST = NSLOT // P
    TAU_LOW, TAU_HIGH, EARLY_EXIT = 0.5, 2.0, 0.05

    def sizes(halves):
        return HT * halves, BANK * halves, 2 * HT * halves, 2 * HT * halves + GX, halves + 1

    assert B == 2 and DH == P and S == BANK and KH == 2 and QT == 4 and NC == 8 and KT == 8 and YG == 8
    assert (H - 2) % HEADS_PER_TURN == 0
    assert ST == 2 and UT == 2 and 2 * NSLOT == BANK and BOT == VB == 64 and RDIM <= 64

    x1 = nc.dram_tensor("x1", (S, D), F32, kind="Internal").ap()
    x1_t = x1.rearrange("(t p) d -> p t d", p=P)
    x_t = x.rearrange("b (t p) d -> b p t d", p=P)
    out_t = out.rearrange("b (t p) d -> p (b t) d", p=P)
    ctx_t = ctx_in.rearrange("b (t p) d -> (b t) p d", p=P)
    mask_t = mask.rearrange("b (t p) k -> b p t k", p=P)
    bias_t = bias.rearrange("b h (t p) k -> (b h t) p k", p=P)
    w_dram = {m: w.rearrange("(c p) n -> p c n", p=P) for m, w in (("q", Wq), ("k", Wk), ("v", Wv))}

    base = (nc.sbuf_base + 31) // 32 * 32

    def at(name, where, shape, dt=F32):
        n = {F32: 4, F32R: 4, BF16: 2, U8: 1, I32: 4}[dt]
        for s in shape[1:]:
            n *= s
        assert n <= where[1], (name, n, where)
        assert where[0] + n <= nc.sbuf_usable_end
        return nc.alloc_sbuf_tensor_at(name, shape, dt, offset=where[0])

    top = [base]

    def place(kb):
        n = int(kb * KB)
        top[0] += n
        return top[0] - n, n

    def part(where, kb, of):
        assert int((kb + of) * KB) <= where[1]
        return where[0] + int(kb * KB), int(of * KB)

    C, X, Y, HIDE, RAW = place(64), place(32), place(16), place(8), place(8)
    WK, WQ, WV, WO = place(8), place(8), place(8), place(8)
    KQ_K, KQ_Q, VT, VV, BIAS = place(8), place(4), place(2), place(8), place(8)
    PROBS, PT, OT = place(16), place(8), place(4)

    ctxT = at("ctxT", C, [P, 2, NC, SK], F32R)
    xnT = at("xnT", X, [P, 2, NC, S], F32R)
    y = at("y", Y, [P, QT, D])
    hide = at("hide", HIDE, [P, QT, SK], BF16)
    raw = at("raw", RAW, [P, 2, D])
    w = {m: at("w" + m, where, [P, 2, D], F32R) for m, where in (("k", WK), ("q", WQ), ("v", WV), ("o", WO))}
    kT = at("kT", KQ_K, [P, 2, SK], F32R)
    qT = at("qT", KQ_Q, [P, 2, S], F32R)
    vT = at("vT", VT, [P, BANK])
    v = at("v", VV, [P, 2, KT, DH], F32R)
    bias_sb = at("bias_sb", BIAS, [P, 2 * SK])
    probs = at("probs", PROBS, [P, QT, SK])
    pT = at("pT", PT, [P, 2, 2, S], F32R)
    oT = at("oT", OT, [P, 2, S], F32R)
    stage = at("stage", X, [P, KT, D])
    mask_in = at("mask_in", PT, [P, QT, SK], U8)
    mask_all = at("mask_all", PT, [P, B, QT, SK], U8)
    ctxT_p = at("ctxT_p", part(C, 0, 32), [P, 2, NC, B * QUARTER], F32R)
    xnT_p = at("xnT_p", (C[0] + 32 * KB, 64 * KB), [P, 2, NC, B * S], F32R)
    y0 = probs
    hide_p = at("hide_p", part(HIDE, 4, 4), [P, T, QUARTER], BF16)
    kT_p = at("kT_p", part(KQ_K, 0, 4), [P, 2, B * QUARTER], F32R)
    qT_p = at("qT_p", (KQ_K[0] + 4 * KB, 8 * KB), [P, 2, B * S], F32R)
    v_p = at("v_p", part(VV, 0, 4), [P, 2, 4, DH], F32R)
    bias_p = at("bias_p", part(VV, 4, 4), [P, 4, QUARTER])
    probs_p = at("probs_p", BIAS, [P, T, QUARTER])
    oT_p = [at("oT_p0", part(HIDE, 0, 4), [P, 2, S], F32R), at("oT_p1", OT, [P, 2, S], F32R)]
    stage_p = [at("stage_p0", BIAS, [P, 2, D]), at("stage_p1", WO, [P, 2, D])]
    mask_p = at("mask_p", part(VV, 0, 2), [P, T, QUARTER], U8)
    xn_stage = at("xn_stage", PT, [P, 2, D])
    hs1_paired = at("hs1_paired", part(X, 0, 16), [P, QT, D])
    ident = at("ident", place(0.5), [P, P])
    ones = at("ones", place(0.5), [P, P])
    row = at("row", place(0.5), [P, 5, T])
    negmax, rowsum, safe_sum, recip, coef = (row[:, i, 0:QT] for i in range(5))
    negmax_p, rowsum_p, safe_sum_p, recip_p, coef_p = (row[:, i, :] for i in range(5))
    stats = at("stats", place(0.5), [P, QT, 2, 6])
    scal = at("scal", place(0.0625), [P, 12])
    (G_X, TG_X, G_F, TG_F, BU2, HALF_BU2, W1, GBIAS, EPS_C, MEAN_0, MEAN_1, MEAN_2) = range(12)
    moments = at("moments", place(0.0625), [P, T, 2])
    token = at("token", place(0.5), [P, 14, T])
    (STD, R0, V1, V2, V3, RSTD, VAR1, LOGVAR, NORM, SIG, U, GATE, COEF, TOTAL) = range(14)
    seen = at("seen", place(0.1875), [P, 6 * 4 * B])
    plan = at("plan", place(0.0625), [P, 1 + 4 * B], I32)
    MODE = 0
    FIRST_KEY, FIRST_TILE, QUARTER_KEY, QUARTER_TILE = (1 + n * B for n in range(4))
    PAIRED, ONE_HALF, BOTH_HALVES = 0, 1, 2
    bu = at("bu", place(0.03125), [P, UT])
    wu2 = at("wu2", place(0.03125), [P, UT])

    xs0 = at("xs0", part(X, 0, 16), [P, QT, D])
    wu_in = at("wu_in", part(X, 16, 8), [P, UT, D])
    wq_in = at("wq_in", part(X, 24, 4), [BOT, D])
    wvd_in = at("wvd_in", part(X, 28, 4), [VB, D])
    hs0 = at("hs0", (WK[0], WK[1] + WQ[1]), [P, QT, D])
    keys_in = at("keys_in", part(RAW, 0, 0.5), [P, ST, BOT])
    wr_in = at("wr_in", part(RAW, 0.5, 0.25), [RDIM, BOT])
    keysT = at("keysT", part(RAW, 0.75, 1), [BOT, NSLOT])
    wvu_in = at("wvu_in", part(RAW, 1.75, 2), [P, NC, VB])
    slots = at("slots", part(RAW, 4, 2), [BOT + 1, 2, NSLOT])
    queryT = at("queryT", part(RAW, 6, 2), [BOT + 1, BANK])
    hT = at("hT", part(C, 0, 32), [P, 2, NC, BANK], F32R)
    wuT = at("wuT", part(C, 32, 16), [P, 2, NC, NU], F32R)
    av_in = at("av_in", part(C, 48, 8), [P, ST, D])
    avT = at("avT", part(C, 56, 8), [P, NC, NSLOT])
    wqT = at("wqT", KQ_Q, [P, 2, NC, BOT], F32R)
    wvuT = at("wvuT", WV, [VB, 2, D], F32R)
    scores = at("scores", KQ_K, [P, QT, 2, NSLOT])
    gelu = at("gelu", part(HIDE, 0, 4), [P, UT, BANK])
    rkT = at("rkT", part(HIDE, 4, 1), [RDIM, NSLOT])
    wrT = at("wrT", part(HIDE, 5, 0.25), [BOT, RDIM])
    wvdT = at("wvdT", part(HIDE, 5.25, 2), [P, NC, VB])
    values = at("values", part(HIDE, 7.25, 0.5), [P, ST, VB])
    top8 = at("top8", part(HIDE, 7.75, 0.125), [P, QT, 8])
    negmax_f = at("negmax_f", part(HIDE, 7.875, 0.0625), [P, QT])
    mixT = at("mixT", BIAS, [VB, B, 2, BANK], F32R)
    hs1 = at("hs1", PROBS, [P, QT, D])
    kept = at("kept", part(PT, 0, 4), [P, QT, NSLOT])
    attn = at("attn", part(PT, 4, 4), [P, QT, NSLOT])
    prob = at("prob", part(VV, 0, 4), [P, QT, NSLOT])
    probT = at("probT", part(VV, 4, 4), [P, ST, BANK])

    def var_of(half):
        return moments[:, half * QT:half * QT + QT, 1]

    with ExitStack() as stack:
        def bank(name, n=1):
            return stack.enter_context(nc.psum_tensor(name, [P, n * BANK], F32))

        score_ps = bank("score_ps", 2)
        proj_ps = [bank("proj_ps0"), bank("proj_ps1")]
        turn_ps = [bank("turn_ps0"), bank("turn_ps1")]
        head_ps = bank("head_ps")
        out_ps = bank("out_ps")
        score_half = [score_ps[:, 0:BANK], score_ps[:, BANK:]]
        K_BANK = proj_ps
        Q_BANK = {2: proj_ps[0], 1: proj_ps[1]}
        OUT_BANKS = {1: [out_ps], 2: [out_ps, proj_ps[1]]}
        V_BANK = {2: [proj_ps[1], head_ps], 1: [proj_ps[0]]}
        F_TURN = score_half
        F_QUERY = proj_ps[0]
        F_UNITS = [proj_ps[1], head_ps]
        F_SCORES = turn_ps
        F_MISC = out_ps

        START_BANKS = [score_half[0], score_half[1], proj_ps[1][:], turn_ps[0][:], turn_ps[1][:]]

        PV_BANKS, OUT_PAIRED = [head_ps, out_ps], [head_ps, proj_ps[1]]
        START_PAIRED = [score_half[0], score_half[1], turn_ps[0][:], turn_ps[1][:]]
        KQ_AT_PAIRED = {0: 0, 1: 1, 3: 2}

        def start_dst(k):
            t, c = (k % 8) // 2 + (QT if k >= 16 else 0), 4 * (k % 2)
            return (ctxT_p if 8 <= k < 16 else xnT_p)[:, :, c:c + 4, t * P:(t + 1) * P]

        KQ_AT = {2: {0: 0, 3: 1, 7: 2}, 1: {0: 0, 3: 1}}

        def bias_slot(qt, halves):
            slots_ = 4 // halves
            W, n = halves * BANK, qt % slots_
            return n, bias_sb[:, n * W:(n + 1) * W], QT // slots_

        def start_bank(k, GC):
            return k % 3 if k < GC else (0, 1, 3, 4)[k % 4]

        def start_bank_before(k, GC):
            return max((j for j in range(k) if start_bank(j, GC) == start_bank(k, GC)), default=None)

        def sem(name):
            return stack.enter_context(nc.semaphore(name))

        weight_in = {m: sem("weight_in_" + m) for m in "qkvo"}
        weight_hi = {m: sem("weight_hi_" + m) for m in "qkvo"}
        weight_lo = {m: sem("weight_lo_" + m) for m in "qkvo"}
        bias_in = [sem(f"bias_in{i}") for i in range(4)]
        bias_masked = sem("bias_masked")
        ctx_load = [sem(f"ctx_load{t}") for t in range(KT)]
        x_load = [sem(f"x_load{t}") for t in range(QT)]
        mask_load = sem("mask_load")
        mask_all_load = sem("mask_all_load")
        seen_done = sem("seen_done")
        seen_ps = sem("seen_ps")
        plan_step = sem("plan_step")
        PLANNED = 15
        y_load = sem("y_load")
        y_out = sem("y_out")
        g_in = sem("g_in")
        went_on = {"sp": sem("went_on_sp"), "dve": sem("went_on_dve")}
        ident_done = sem("ident_done")
        gate_done = sem("gate_done")
        hide_done = sem("hide_done")
        norm_step = sem("norm_step")
        STATS_STEPS, RSTD_STEPS = 3 * QT, 6
        std_done = sem("std_done")
        xn_done = sem("xn_done")
        start_ps = sem("start_ps")
        start_hi = sem("start_hi")
        start_lo = sem("start_lo")
        kq_ps = sem("kq_ps")
        kq_hi = sem("kq_hi")
        kq_lo = sem("kq_lo")
        v_ps = sem("v_ps")
        vT_sb = sem("vT_sb")
        v_turned = sem("v_turned")
        v_hi = sem("v_hi")
        v_lo = sem("v_lo")
        score_done = sem("score_done")
        score_sb = sem("score_sb")
        exp_done = sem("exp_done")
        coef_step = sem("coef_step")
        p_turned = sem("p_turned")
        pT_hi = sem("pT_hi")
        pT_lo = sem("pT_lo")
        pv_done = sem("pv_done")
        oT_hi = sem("oT_hi")
        oT_lo = sem("oT_lo")
        y_ps = sem("y_ps")
        y_sb = sem("y_sb")
        f_load = {n: sem("f_load_" + n) for n in ("x", "wu", "wq", "wvd", "small", "rows", "av", "wvu")}
        F_LOADS = {"x": QT, "small": 8, "rows": 2}
        dve_step = sem("dve_step")
        act_step = sem("act_step")
        turned = sem("turned")
        turned_hi = sem("turned_hi")
        turned_lo = sem("turned_lo")
        product_ps = sem("product_ps")
        unit_ps = sem("unit_ps")
        query_ps = sem("query_ps")
        slot_ps = sem("slot_ps")
        slot_sb = sem("slot_sb")
        gelu_done = sem("gelu_done")
        learned_ps = sem("learned_ps")
        prob_done = sem("prob_done")
        mix_ps = sem("mix_ps")
        mix_hi = sem("mix_hi")
        mix_lo = sem("mix_lo")
        sum_step = sem("sum_step")
        aux_ps = sem("aux_ps")
        out_done = sem("out_done")
        stored = sem("stored")

        WSLOT = {"k": 0, "v": 0, "q": 1, "o": 1}

        def run_paired(eng, head):
            head(0, True, False)
            with eng.Fori(0, TURNS) as turn:
                for u in range(HEADS_PER_TURN):
                    head(turn * HEADS_PER_TURN + (1 + u), False, False)
            head(H - 1, False, True)

        def run_heads(eng, start, head):
            for b in range(B):
                start(b, b * H)
                head(b * H, True, False)
                with eng.Fori(0, TURNS) as turn:
                    for u in range(HEADS_PER_TURN):
                        head(turn * HEADS_PER_TURN + (b * H + 1 + u), False, False)
                head(b * H + (H - 1), False, True)

        order = []
        for n in range(4):
            blocks = [(wu_in[:, ut, c * P:(c + 1) * P], P) for c in (2 * n, 2 * n + 1) for ut in range(UT)]
            order.append(("wu", blocks, lambda p, n=n: wuT[:, p, 2 * n:2 * n + 2, :].rearrange("p c u -> p (c u)"), P, True))
        order.append(("wq", [(wq_in[:, c * P:(c + 1) * P], BOT) for c in range(NC)],
                      lambda p: wqT[:, p, :, :].rearrange("p c u -> p (c u)"), P, True))
        order.append(("small", [(keys_in[:, s, :], P) for s in range(ST)], lambda p: keysT[:, :], BOT, False))
        order.append(("small", [(wr_in[:, :], RDIM)], lambda p: wrT[:, :], BOT, False))

        def h_groups(half, source):
            return [(half * QT + t, [(source[:, t, (c + k) * P:(c + k + 1) * P], P) for k in range(4)],
                     lambda p, t=t, c=c: hT[:, p, c:c + 4, t * P:(t + 1) * P], P, True) for t in range(QT) for c in (0, 4)]

        HEAD_OF_H = len(order)
        order += h_groups(0, hs0)
        AV = len(order)
        for n in range(4):
            blocks = [(av_in[:, s, c * P:(c + 1) * P], P) for c in (2 * n, 2 * n + 1) for s in range(ST)]
            order.append(("av", blocks, lambda p, n=n: avT[:, 2 * n:2 * n + 2, :].rearrange("p c u -> p (c u)"), P, False))
        order.append(("wvd", [(wvd_in[:, c * P:(c + 1) * P], VB) for c in range(NC)],
                      lambda p: wvdT[:, :, :].rearrange("p c u -> p (c u)"), P, False))
        for n in range(2):
            order.append(("wvu", [(wvu_in[:, c, :], P) for c in range(4 * n, 4 * n + 4)],
                          lambda p, n=n: wvuT[:, p, n * BANK:(n + 1) * BANK], VB, True))
        H1 = len(order)
        order += h_groups(1, hs1)
        P0 = len(order)
        for half in range(B):
            for s in range(ST):
                order.append(("prob", [(prob[:, t, s * P:(s + 1) * P], P) for t in range(QT)],
                              lambda p, s=s: probT[:, s, :], P, False))
        P1, END = P0 + ST, P0 + 2 * ST
        order_paired = order[:HEAD_OF_H] + order[AV:H1] + order[HEAD_OF_H:AV] + h_groups(1, hs1_paired) + order[P0:]
        FILLS_PAIRED = [(0, 1, 2, 3), (4, 5, 6, 7), (8, 9, 10), (11, 12, 13)]
        FILLS = [(0, 1), (2, 3), (4, 5, 6), (7, 8), (9, 10), (11, 12), (13, 14), (15, 16)]
        assert FILLS[-1][-1] + 1 == AV + 2

        def fill_groups(i, halves):
            return FILLS[i] if halves == 2 else FILLS[2 * i] + FILLS[2 * i + 1]

        def splits(k):
            return sum(g[4] for g in F["order"][:k])

        def arrived(eng, *names):
            for n in names:
                eng.wait_ge(f_load[n], F_LOADS.get(n, 1) * DMA)

        def f_source(k):
            _, blocks, dst, parts, _ = F["order"][k]
            src = F_TURN[k % 2][0:parts, 0:sum(n for _, n in blocks)]
            return src.rearrange("p (c n) -> p c n", n=P) if len(dst(HI).shape) == 3 else src

        act_mark = {n: i + 1 for i, n in enumerate(("std0", "rk", "router", "slots", "std1", "query0", "values", "logvar",
                                                    "query1", "sig0", "gate0", "sig1", "gate1"))}
        marks = {paired: {} for paired in (False, True)}
        INIT_STEPS = 2
        F = {}

        def follow(paired):
            F.update(order=order_paired if paired else order, mark=marks[paired],
                     H0=HEAD_OF_H + (H1 - AV if paired else 0), SMALL=HEAD_OF_H + 5 if paired else H1 - 2, xs=(y0, y) if paired else (xs0, y),
                     hs=(hs0, hs1_paired if paired else hs1))

        block = stack.enter_context(nc.Block())

        @block.sync
        def _(sp):
            def when(s, n):
                sp.wait_ge(s, n)
                sp.sem_inc(went_on["sp"], 1)

            def scalar_in(column, ap, s):
                sp.dma_start(scal[:, column:column + 1], ap.rearrange("(a n) -> a n", a=1).to_broadcast((P, 1))).then_inc(s, DMA)

            def load_weight(m, h):
                dst = raw[:, WSLOT[m], :]
                if m == "o":
                    src = Wo[bass.ds(h * DH, DH), :]
                else:
                    src = w_dram[m][:, :, bass.ds(h * DH, DH)]
                    dst = dst.rearrange("p (c n) -> p c n", n=DH)
                sp.dma_start(dst, src).then_inc(weight_in[m], DMA)

            def load_x(b):
                for t in range(QT):
                    sp.dma_start(probs[:, t, :], x_t[b, :, t, :]).then_inc(x_load[t], DMA)

            def load_y(b):
                sp.dma_start(y[:, :, :], x_t[b]).then_inc(y_load, DMA)

            def attend(halves):
                KT, W, GC, G, KQ = sizes(halves)

                def load_bias(b, g, qt):
                    n, slot, _ = bias_slot(qt, halves)
                    sp.dma_start(slot,
                                 bias_t[bass.ds(g * QT + qt, 1), :, keys_of(b)].rearrange("a p k -> p (a k)")).then_inc(bias_in[n], DMA)

                def load_ctx(b):
                    for t in range(KT):
                        tile = bass.ds(first_tile[b] + (b * (SK // P) + t), 1) if halves == 1 else slice(b * KT + t, b * KT + t + 1)
                        sp.dma_start(stage[:, t, :], ctx_t[tile, :, :].rearrange("a p d -> p (a d)")).then_inc(ctx_load[t], DMA)

                def load_mask(b):
                    sp.dma_start(mask_in[:, :, 0:W], mask_t[b][:, :, keys_of(b)]).then_inc(mask_load, DMA)

                def keys_of(b):
                    return bass.ds(first_key[b], W) if halves == 1 else slice(0, SK)

                def start():
                    load_ctx(0)
                    when(weight_lo["k"], 1)
                    load_weight("v", 0)
                    load_weight("q", 0)
                    load_mask(0)
                    for qt in range(4 // halves):
                        load_bias(0, 0, qt)
                    load_y(0)

                def head(b, h, last):
                    final = last and b == B - 1
                    g = h + b * H
                    following = 0 if last else h + 1
                    if not final:
                        when(weight_lo["v"], g + 1)
                        load_weight("k", following)
                        when(weight_lo["q"], g + 1)
                        when(weight_lo["o"], g)
                        load_weight("q", following)
                    if last:
                        when(kq_ps, KQ * (g + 1))
                    if last and not final:
                        load_ctx(1)
                    if final:
                        when(y_out, DMA)
                        for t in range(QT):
                            sp.dma_start(xs0[:, t, :], x1_t[:, t, :]).then_inc(f_load["x"], DMA)
                        sp.dma_start(wu_in[:, :, :], ffn_Wu1.rearrange("(p t) d -> p t d", p=P)).then_inc(f_load["wu"], DMA)
                        sp.dma_start(wq_in[:, :], ffn_Wq).then_inc(f_load["wq"], DMA)
                        when(weight_lo["v"], g + 1)
                        sp.dma_start(keys_in[:, :, :], ffn_keys.rearrange("(t p) d -> p t d", p=P)).then_inc(f_load["small"], DMA)
                        sp.dma_start(wr_in[:, :], ffn_Wr).then_inc(f_load["small"], DMA)
                        sp.dma_start(bu[:, :], ffn_bu1.rearrange("(p t) -> p t", p=P)).then_inc(f_load["small"], DMA)
                        sp.dma_start(wu2[:, :], ffn_Wu2.rearrange("a (p t) -> p (a t)", p=P)).then_inc(f_load["small"], DMA)
                        for column, ap in ((G_F, g_ffn), (BU2, ffn_bu2), (W1, ffn_gate_w1), (GBIAS, ffn_gate_bias)):
                            scalar_in(column, ap, f_load["small"])
                    if halves == 2:
                        for qt in range(2, QT):
                            when(score_sb, QT * g + qt - 1)
                            load_bias(b, g, qt)

                    def next_bias(qt):
                        when(score_sb, QT * g + (QT - 1 if halves == 2 else 1) + qt)
                        load_bias(b + 1 if last else b, g + 1, qt)

                    if not final:
                        if halves == 1:
                            next_bias(0)
                        when(weight_lo["k"], g + 2)
                        load_weight("v", following)
                        if halves == 1:
                            next_bias(1)
                        when(weight_lo["q"], g + 2)
                    else:
                        when(weight_lo["q"], g + 1)
                        when(weight_lo["o"], g)
                        sp.dma_start(wvd_in[:, :], ffn_Wvd).then_inc(f_load["wvd"], DMA)
                        sp.dma_start(wvu_in[:, :, :], ffn_Wvu.rearrange("(t p) d -> p t d", p=P)).then_inc(f_load["wvu"], DMA)
                    load_weight("o", h)
                    if not final:
                        for qt in (0, 1) if halves == 2 else (2, 3):
                            next_bias(qt)
                    if last and not final:
                        when(p_turned, KT * (g + 1))
                        load_x(1)
                        when(pv_done, KT * (g + 1))
                        load_mask(1)
                        when(y_sb, YG * (g + 1))
                        sp.dma_start(x1_t, y[:, :, :]).then_inc(y_out, DMA)
                        when(y_out, DMA)
                        load_y(1)
                    if final:
                        when(v_ps, halves * (g + 1))
                        sp.dma_start(av_in[:, :, :], ffn_values.rearrange("(t p) d -> p t d", p=P)).then_inc(f_load["av"], DMA)
                        when(weight_lo["o"], g + 1)
                        for k in range(2):
                            sp.dma_start(slots[BOT:BOT + 1, k, :], ffn_log_rel.rearrange("(a n) -> a n", a=1)).then_inc(f_load["rows"], DMA)

                start()
                for b in range(B):
                    head(b, 0, False)
                    with sp.Fori(0, TURNS) as turn:
                        for u in range(HEADS_PER_TURN):
                            head(b, turn * HEADS_PER_TURN + (1 + u), False)
                    head(b, H - 1, True)

            def rest(paired):
                for t in range(T):
                    sp.wait_ge(out_done, 2 * t + 2)
                    sp.dma_start(out_t[:, t, :], F["xs"][t // QT][:, t % QT, :]).then_inc(stored, DMA)
                sp.wait_ge(stored, DMA * T)

            def attend_paired():
                def load_bias(g, t):
                    b, qt = t // QT, t % QT
                    sp.dma_start(bias_p[:, t % 4, :], bias_t[bass.ds(g * QT + (b * H * QT + qt), 1), :, bass.ds(quarter_key[b], QUARTER)]
                                 .rearrange("a p k -> p (a k)")).then_inc(bias_in[t % 4], DMA)

                def next_bias(g, t):
                    when(score_sb, T * g + t - 3)
                    load_bias(g if t < T else g + 1, t % T)

                def head(g, last):
                    if not last:
                        when(weight_lo["v"], g + 1)
                        load_weight("k", g + 1)
                        when(weight_lo["q"], g + 1)
                        when(weight_lo["o"], g)
                        load_weight("q", g + 1)
                    next_bias(g, 4)
                    next_bias(g, 5)
                    if not last:
                        when(weight_lo["k"], g + 2)
                        load_weight("v", g + 1)
                    next_bias(g, 6)
                    next_bias(g, 7)
                    if not last:
                        when(weight_lo["q"], g + 2)
                    else:
                        when(weight_lo["q"], H)
                        when(weight_lo["o"], H - 1)
                    load_weight("o", g)
                    if not last:
                        for t in range(T, T + 4):
                            next_bias(g, t)
                    else:
                        when(kq_ps, 3 * H)
                        when(v_ps, H)
                        sp.dma_start(wu_in[:, :, :], ffn_Wu1.rearrange("(p t) d -> p t d", p=P)).then_inc(f_load["wu"], DMA)
                        sp.dma_start(wq_in[:, :], ffn_Wq).then_inc(f_load["wq"], DMA)
                        when(weight_lo["v"], H)
                        sp.dma_start(keys_in[:, :, :], ffn_keys.rearrange("(t p) d -> p t d", p=P)).then_inc(f_load["small"], DMA)
                        sp.dma_start(wr_in[:, :], ffn_Wr).then_inc(f_load["small"], DMA)
                        sp.dma_start(bu[:, :], ffn_bu1.rearrange("(p t) -> p t", p=P)).then_inc(f_load["small"], DMA)
                        sp.dma_start(wu2[:, :], ffn_Wu2.rearrange("a (p t) -> p (a t)", p=P)).then_inc(f_load["small"], DMA)
                        for column, ap in ((G_F, g_ffn), (BU2, ffn_bu2), (W1, ffn_gate_w1), (GBIAS, ffn_gate_bias)):
                            scalar_in(column, ap, f_load["small"])
                        sp.dma_start(av_in[:, :, :], ffn_values.rearrange("(t p) d -> p t d", p=P)).then_inc(f_load["av"], DMA)
                        sp.dma_start(wvd_in[:, :], ffn_Wvd).then_inc(f_load["wvd"], DMA)
                        sp.dma_start(wvu_in[:, :, :], ffn_Wvu.rearrange("(t p) d -> p t d", p=P)).then_inc(f_load["wvu"], DMA)
                        when(weight_lo["o"], H)
                        for k in range(2):
                            sp.dma_start(slots[BOT:BOT + 1, k, :], ffn_log_rel.rearrange("(a n) -> a n", a=1)).then_inc(f_load["rows"], DMA)

                for b in range(B):
                    for k in range(2):
                        sp.dma_start(stage_p[b][:, k, :], ctx_t[bass.ds(quarter_tile[b] + (b * (SK // P) + k), 1), :, :]
                                     .rearrange("a p d -> p (a d)")).then_inc(ctx_load[2 * b + k], DMA)
                load_y(1)
                load_weight("q", 0)
                when(weight_lo["k"], 1)
                load_weight("v", 0)
                for b in range(B):
                    sp.dma_start(mask_p[:, b * QT:(b + 1) * QT, :], mask_t[b][:, :, bass.ds(quarter_key[b], QUARTER)]).then_inc(mask_load, DMA)
                for t in range(4):
                    load_bias(0, t)
                head(0, False)
                with sp.Fori(0, TURNS) as turn:
                    for u in range(HEADS_PER_TURN):
                        head(turn * HEADS_PER_TURN + (1 + u), False)
                head(H - 1, True)

            scalar_in(G_X, g_xattn, g_in)
            sp.dma_start(mask_all[:, :, :, :], mask.rearrange("b (t p) k -> p b t k", p=P)).then_inc(mask_all_load, DMA)
            load_weight("k", 0)
            load_x(0)
            sp.wait_ge(plan_step, PLANNED)
            mode = sp.value_load(plan[0:1, MODE:MODE + 1], min_val=0, max_val=2)
            first_key = [sp.value_load(plan[0:1, FIRST_KEY + b:FIRST_KEY + b + 1], min_val=0, max_val=SK - BANK) for b in range(B)]
            first_tile = [sp.value_load(plan[0:1, FIRST_TILE + b:FIRST_TILE + b + 1], min_val=0, max_val=HT) for b in range(B)]
            quarter_key = [sp.value_load(plan[0:1, QUARTER_KEY + b:QUARTER_KEY + b + 1], min_val=0, max_val=SK - QUARTER) for b in range(B)]
            quarter_tile = [sp.value_load(plan[0:1, QUARTER_TILE + b:QUARTER_TILE + b + 1], min_val=0, max_val=SK // P - 2) for b in range(B)]
            with sp.If(mode == PAIRED):
                follow(True)
                attend_paired()
                rest(True)
            with sp.Else():
                follow(False)
                with sp.If(mode == BOTH_HALVES):
                    attend(2)
                with sp.Else():
                    attend(1)
                rest(False)

        @block.gpsimd
        def _(pool):
            nc.gpsimd.memset(ident[:], 0.0).then_inc(ident_done, 1)
            pool.wait_ge(ident_done, 1)
            nc.gpsimd.affine_select(out=ident[:], in_=ident[:], compare_op=ALU.not_equal, fill=1.0,
                                    base=0, pattern=[[-1, P]], channel_multiplier=1).then_inc(ident_done, 1)

            def attend(halves):
                KT, W, GC, G, KQ = sizes(halves)

                def head(g, first, last):
                    for qt in range(QT):
                        if first:
                            pool.wait_ge(hide_done, QT * (g // H) + qt + 1)
                        n, slot, per_head = bias_slot(qt, halves)
                        pool.wait_ge(bias_in[n], DMA * per_head * g + DMA * (qt * per_head // QT + 1))
                        nc.gpsimd.tensor_tensor(slot, slot, hide[:, qt, 0:W], ALU.add).then_inc(bias_masked, 1)

                run_heads(pool, lambda b, g: None, head)

            def attend_paired():
                def head(g, first, last):
                    for n in range(T):
                        if first:
                            pool.wait_ge(hide_done, 1)
                        pool.wait_ge(bias_in[n % 4], DMA * 2 * g + DMA * (n // 4 + 1))
                        nc.gpsimd.tensor_tensor(bias_p[:, n % 4, :], bias_p[:, n % 4, :], hide_p[:, n, :],
                                                ALU.add).then_inc(bias_masked, 1)

                run_paired(pool, head)

            def rest(paired):
                pool.wait_ge(gate_done, 3)
                for tile in range(T):
                    half, t = tile // QT, tile % QT
                    x1_tile, h_tile = F["xs"][half][:, t, :], F["hs"][half][:, t, :]
                    pool.wait_ge(turned, (H1 if half else F["H0"]) + 2 * t + 2)
                    nc.gpsimd.tensor_scalar(h_tile, h_tile, scal[:, TG_F:TG_F + 1], None, ALU.mult).then_inc(sum_step, 1)
                    pool.wait_ge(sum_step, 2 * tile + 1)
                    nc.gpsimd.tensor_tensor(x1_tile, x1_tile, h_tile, ALU.add).then_inc(sum_step, 1)

            pool.wait_ge(plan_step, PLANNED)
            mode = pool.value_load(plan[0:1, MODE:MODE + 1], min_val=0, max_val=2)
            with pool.If(mode == PAIRED):
                follow(True)
                attend_paired()
                rest(True)
            with pool.Else():
                follow(False)
                with pool.If(mode == BOTH_HALVES):
                    attend(2)
                with pool.Else():
                    attend(1)
                rest(False)


        @block.vector
        def _(dve):
            V = nc.vector
            count = [0]
            norms = [0]

            def step(ins, name=None, wait=True):
                count[0] += 1
                ins.then_inc(dve_step, 1)
                if wait:
                    dve.wait_ge(dve_step, count[0])
                if name:
                    F["mark"][name] = count[0]

            def norm(ins, wait=True):
                norms[0] += 1
                ins.then_inc(norm_step, 1)
                if wait:
                    dve.wait_ge(norm_step, norms[0])

            def less(dst, src, hi, scale=1.0):
                if scale == 1.0:
                    return V.tensor_tensor(dst, src, hi.bitcast(F32), ALU.subtract)
                return V.scalar_tensor_tensor(out=dst, in0=src, scalar=scale, in1=hi.bitcast(F32),
                                              op0=ALU.mult, op1=ALU.subtract)

            def weight(m, g):
                dve.wait_ge(weight_hi[m], g + 1)
                less(w[m][:, LO, :], raw[:, WSLOT[m], :], w[m][:, HI, :]).then_inc(weight_lo[m], 1)

            def tile_stats(did, src, t, half):
                for k in range(2):
                    did(V.bn_stats(stats[:, t, k, :], src[:, t, k * BANK:(k + 1) * BANK]), wait=(k == 1))
                did(V.bn_aggr(moments[:, half * QT + t, :], stats[:, t, :, :]), wait=(t == QT - 1))

            def make_rstd(did, half, std_sem, std_count):
                s = lambda i: token[:, i, half * QT:half * QT + QT]
                did(V.tensor_scalar(s(VAR1), var_of(half), EPS, None, ALU.add))
                dve.wait_ge(std_sem, std_count)
                did(V.reciprocal(s(R0), s(STD)))
                did(V.tensor_tensor(s(V1), s(VAR1), s(R0), ALU.mult))
                did(V.tensor_tensor(s(V2), s(V1), s(R0), ALU.mult))
                did(V.tensor_scalar(s(V3), s(V2), -0.5, 1.5, ALU.mult, ALU.add))
                did(V.tensor_tensor(s(RSTD), s(R0), s(V3), ALU.mult))

            def normalise(dst, src, half, t):
                tile = half * QT + t
                return V.tensor_scalar(dst, src, moments[:, tile, 0:1], token[:, RSTD, tile:tile + 1],
                                       ALU.subtract, ALU.mult)

            def x_stats(b, t):
                dve.wait_ge(x_load[t], DMA * (b + 1))
                tile_stats(norm, probs, t, 0)

            def head_out(g):
                dve.wait_ge(oT_hi, g + 1)
                less(oT[:, LO, :], head_ps[:, :], oT[:, HI, :]).then_inc(oT_lo, 1)

            def make_coef(g):
                dve.wait_ge(exp_done, QT * g + QT)
                V.tensor_scalar(safe_sum, rowsum, LEAST_SUM, None, ALU.max).then_inc(coef_step, 1)
                dve.wait_ge(coef_step, 3 * g + 1)
                V.reciprocal(recip, safe_sum).then_inc(coef_step, 1)
                dve.wait_ge(coef_step, 3 * g + 2)
                V.tensor_scalar(coef, recip, scal[:, TG_X:TG_X + 1], None, ALU.mult).then_inc(coef_step, 1)

            def add_out(g, i, banks=1):
                if i == 0:
                    dve.wait_ge(coef_step, 3 * g + 3)
                dve.wait_ge(y_ps, YG * g + i + 1)
                qt, cols = i // 2, slice((i % 2) * BANK, (i % 2 + 1) * BANK)
                V.scalar_tensor_tensor(out=y[:, qt, cols], in0=OUT_BANKS[banks][i % banks][:, :], scalar=coef[:, qt:qt + 1],
                                       in1=y[:, qt, cols], op0=ALU.mult, op1=ALU.add).then_inc(y_sb, 1)

            def take(k):
                if F["order"][k][4]:
                    dve.wait_ge(turned_hi, k + 1)
                    less(F["order"][k][2](LO), f_source(k), F["order"][k][2](HI)).then_inc(turned_lo, 1)

            def h_tile(half, t):
                step(normalise(F["hs"][half][:, t, :], F["xs"][half][:, t, :], half, t), f"h{half * QT + t}", wait=False)

            def var_h(half):
                s = lambda i: token[:, i, half * QT:half * QT + QT]
                step(V.tensor_tensor(s(V1), var_of(half), s(RSTD), ALU.mult))
                step(V.tensor_tensor(s(U), s(V1), s(RSTD), ALU.mult), "var_h", wait=False)

            def pick(half, t):
                tile = half * QT + t
                dve.wait_ge(slot_sb, tile + 1)
                if half:
                    dve.wait_ge(prob_done, QT)
                router = scores[:, t, 0, :]
                step(V.max(top8[:, t, :], router))
                step(V.match_replace(kept[:, t, :], top8[:, t, :], router, MASKED))
                step(V.tensor_tensor(kept[:, t, :], kept[:, t, :], router, ALU.is_equal))
                step(V.scalar_tensor_tensor(out=attn[:, t, :], in0=kept[:, t, :], scalar=MASKED,
                                            in1=scores[:, t, 1, :], op0=ALU.mult, op1=ALU.add))
                step(V.tensor_reduce(negmax_f[:, t:t + 1], attn[:, t, :], AX_X, ALU.max, negate=True), f"attn{tile}", wait=False)

            def mean_logvar():
                dve.wait_ge(learned_ps, 1)
                dve.wait_ge(act_step, act_mark["sig0"])
                m = lambda i: scal[:, i:i + 1]
                step(V.tensor_reduce(m(MEAN_0), F_MISC[:, P + 32:P + 32 + T], AX_X, ALU.add), "sum")
                step(V.tensor_scalar(m(MEAN_1), m(MEAN_0), 2.0 / (B * S), 2e-6, ALU.mult, ALU.add))
                step(V.reciprocal(m(MEAN_2), m(MEAN_1)))

            def gate_in(half):
                s = lambda i: token[:, i, half * QT:half * QT + QT]
                step(V.tensor_scalar(s(NORM), s(LOGVAR), scal[:, MEAN_2:MEAN_2 + 1], None, ALU.mult))
                dve.wait_ge(act_step, act_mark[f"sig{half}"])
                step(V.tensor_scalar(s(V1), s(SIG), 1.25, 1.25, ALU.mult, ALU.add))
                step(V.tensor_tensor(s(U), s(NORM), s(V1), ALU.add))
                step(V.tensor_scalar(s(U), s(U), 0.0, 5.0, ALU.max, ALU.min))
                step(V.tensor_scalar(s(U), s(U), -TAU_LOW, 1.0 / (TAU_HIGH - TAU_LOW), ALU.add, ALU.mult))
                step(V.tensor_scalar(s(U), s(U), 0.0, 1.0, ALU.max, ALU.min))
                step(V.tensor_scalar(s(V2), s(U), scal[:, W1:W1 + 1], scal[:, GBIAS:GBIAS + 1], ALU.mult, ALU.add),
                     f"gate_in{half}", wait=False)

            def gate_out(half):
                s = lambda i: token[:, i, half * QT:half * QT + QT]
                dve.wait_ge(act_step, act_mark[f"gate{half}"])
                step(V.tensor_scalar(s(V3), s(GATE), 0.5, 0.5, ALU.mult, ALU.add))
                step(V.tensor_scalar(s(V1), s(V3), EARLY_EXIT, None, ALU.is_ge))
                step(V.tensor_tensor(s(V1), s(V1), s(V3), ALU.mult))
                dve.wait_ge(prob_done, QT * (half + 1))
                step(V.reciprocal(s(R0), s(TOTAL)))
                step(V.tensor_tensor(s(V1), s(V1), s(R0), ALU.mult))
                step(V.tensor_scalar(s(COEF), s(V1), scal[:, TG_F:TG_F + 1], None, ALU.mult))

            def mix(half):
                dve.wait_ge(mix_hi, half + 1)
                less(mixT[:, half, LO, :], F_QUERY[0:VB, :], mixT[:, half, HI, :]).then_inc(mix_lo, 1)

            def memory_out(half):
                for t in range(QT):
                    tile = half * QT + t
                    for n in range(2):
                        dve.wait_ge(sum_step, 2 * tile + 2)
                        dve.wait_ge(aux_ps, 2 * tile + n + 1)
                        cols = slice(n * BANK, (n + 1) * BANK)
                        V.scalar_tensor_tensor(out=F["xs"][half][:, t, cols], in0=F_SCORES[n][:, :], scalar=token[:, COEF, tile:tile + 1],
                                               in1=F["xs"][half][:, t, cols], op0=ALU.mult, op1=ALU.add).then_inc(out_done, 1)

            def rest(paired):
                if paired:
                    dve.wait_ge(weight_lo["o"], H)
                    step(V.memset(queryT[BOT:BOT + 1, :], 1.0), "ones", wait=False)
                    out_p(H - 1, 1)
                    for i in range(2 * YG):
                        add_p(H - 1, i)
                        if i % 2:
                            dve.wait_ge(y_sb, 2 * YG * (H - 1) + i + 1)
                            tile_stats(step, F["xs"][i // YG], (i // 2) % QT, i // YG)
                        if i == YG - 1:
                            F["mark"]["var0"] = count[0]
                            make_rstd(step, 0, act_step, act_mark["std0"])
                            var_h(0)
                            for t in range(QT):
                                h_tile(0, t)
                        if i >= YG:
                            take(F["H0"] + i - YG)
                else:
                    dve.wait_ge(weight_lo["o"], ALL)
                    step(V.memset(queryT[BOT:BOT + 1, :], 1.0), "ones", wait=False)
                    head_out(ALL - 1)
                    for i in range(YG):
                        add_out(ALL - 1, i)
                        if i % 2:
                            dve.wait_ge(y_sb, YG * (ALL - 1) + i + 1)
                            tile_stats(step, y, i // 2, 1)
                F["mark"]["var1"] = count[0]
                make_rstd(step, 1, act_step, act_mark["std1"])
                var_h(1)
                for t in range(QT):
                    h_tile(1, t)
                pick(0, 0)
                pick(0, 1)
                if not paired:
                    for k in range(FILLS[-1][-1] + 1, H1):
                        take(k)
                pick(0, 2)
                pick(0, 3)
                for k in range(H1, P0):
                    take(k)
                mean_logvar()
                gate_in(0)
                dve.wait_ge(gate_done, 3)
                gate_out(0)
                for t in range(QT):
                    pick(1, t)
                mix(0)
                gate_in(1)
                mix(1)
                memory_out(0)
                gate_out(1)
                memory_out(1)

            def attend(halves):
                KT, W, GC, G, KQ = sizes(halves)
                count[0], norms[0] = INIT_STEPS, 0
                out_banks = 3 - halves
                TURN_V = 7 - halves

                def kq(g, part_):
                    dve.wait_ge(kq_hi, KQ * g + part_ + 1)
                    if part_ < halves:
                        cols = slice(part_ * BANK, (part_ + 1) * BANK)
                        ins = less(kT[:, LO, cols], K_BANK[part_][:, :], kT[:, HI, cols])
                    else:
                        ins = less(qT[:, LO, :], Q_BANK[halves][:, :], qT[:, HI, :], SCALE)
                    ins.then_inc(kq_lo, 1)

                def start_group(b, k):
                    dve.wait_ge(start_hi, G * b + k + 1)
                    tile, c = k // 2, 4 * (k % 2)
                    dst = (ctxT[:, :, c:c + 4, tile * P:(tile + 1) * P] if tile < KT
                           else xnT[:, :, c:c + 4, (tile - KT) * P:(tile - KT + 1) * P])
                    less(dst[:, LO], START_BANKS[start_bank(k, GC)].rearrange("p (c n) -> p c n", n=P), dst[:, HI]).then_inc(start_lo, 1)

                def start(b, g):
                    if b == 0:
                        weight("k", 0)
                        for k in range(GC):
                            start_group(b, k)
                        weight("v", 0)
                        kq(g, 0)
                        weight("q", 0)
                        for t in range(QT):
                            x_stats(b, t)
                    if b or halves == 2:
                        kq(g, halves - 1)
                    make_rstd(norm, 0, std_done, b + 1)
                    for t in range(QT):
                        normalise(probs[:, t, :], probs[:, t, :], 0, t).then_inc(xn_done, 1)
                    dve.wait_ge(mask_load, DMA * (b + 1))
                    if b:
                        dve.wait_ge(bias_masked, QT * g)
                    for k in range(GC, G):
                        start_group(b, k)
                        if k % 2 == 0:
                            qt = (k - GC) // 2
                            V.tensor_scalar(hide[:, qt, 0:W], mask_in[:, qt, 0:W], 0.0, MASKED,
                                            ALU.is_equal, ALU.mult).then_inc(hide_done, 1)
                    kq(g, halves)

                def score(g, qt):
                    if qt == 0:
                        dve.wait_ge(p_turned, KT * g)
                    dve.wait_ge(score_done, QT * g + qt + 1)
                    dve.wait_ge(bias_masked, QT * g + qt + 1)
                    dve.sem_inc(went_on["dve"], 1)
                    src = score_ps[:, :] if halves == 2 else score_half[qt % 2]
                    V.tensor_tensor_reduce(probs[:, qt, 0:W], src, bias_slot(qt, halves)[1], -1.0, NO_SCORE,
                                           ALU.add, ALU.min, negmax[:, qt:qt + 1]).then_inc(score_sb, 1)

                def v_half(g, half):
                    dve.wait_ge(v_hi, halves * g + half + 1)
                    less(v[:, LO, 4 * half:4 * half + 4, :].rearrange("p t d -> p (t d)"), turn_ps[half][:, :],
                         v[:, HI, 4 * half:4 * half + 4, :].rearrange("p t d -> p (t d)")).then_inc(v_lo, 1)

                def pT_tile(g, kt):
                    dve.wait_ge(pT_hi, KT * g + kt + 1)
                    less(pT[:, kt % 2, LO, :], turn_ps[kt % 2][:, :], pT[:, kt % 2, HI, :]).then_inc(pT_lo, 1)

                def head(g, first, last):
                    final = last and g == ALL - 1
                    if not first:
                        head_out(g - 1)
                    for i in range(8):
                        if i % 2 == halves - 1:
                            score(g, i // 2)
                        if not first:
                            add_out(g - 1, i, out_banks)
                        if i == 1 and not final:
                            weight("k", g + 1)
                        if i == 3 and not final:
                            weight("q", g + 1)
                        if final and 2 <= i < 6:
                            if i == 2:
                                arrived(dve, "x")
                            tile_stats(step, xs0, i - 2, 0)
                            if i == 5:
                                F["mark"]["var0"] = count[0]
                        if i == TURN_V:
                            v_half(g, 0)
                        if final and i == 6:
                            make_rstd(step, 0, act_step, act_mark["std0"])
                            var_h(0)
                            h_tile(0, 0)
                        if final and i == 7:
                            h_tile(0, 1)
                    if halves == 2:
                        v_half(g, 1)
                    make_coef(g)
                    if final:
                        h_tile(0, 2)
                        h_tile(0, 3)

                    def fill(i):
                        if final:
                            for k in fill_groups(i, halves):
                                take(k)
                        elif last:
                            start_group(1, 2 * i)
                            start_group(1, 2 * i + 1)

                    fill(0)
                    pT_tile(g, 0)
                    pT_tile(g, 1)
                    if not final:
                        weight("v", g + 1)
                    for kt in range(KT):
                        if kt + 1 < KT:
                            fill(kt + 1)
                        if kt + 2 < KT:
                            pT_tile(g, kt + 2)
                        if not last and kt in KQ_AT[halves]:
                            kq(g + 1, KQ_AT[halves][kt])
                        if kt == halves - 1:
                            weight("o", g)
                    if first:
                        dve.wait_ge(y_load, DMA * (g // H + 1))
                    if last and not final:
                        if halves == 2:
                            kq(g + 1, 0)
                        head_out(g)
                        for i in range(YG):
                            add_out(g, i)
                            if i >= 4:
                                x_stats(1, i - 4)

                run_heads(dve, start, head)

            def out_p(g, b):
                dve.wait_ge(oT_hi, 2 * g + b + 1)
                less(oT_p[b][:, LO, :], PV_BANKS[b][:, :], oT_p[b][:, HI, :]).then_inc(oT_lo, 1)

            def add_p(g, i):
                if i == 0:
                    dve.wait_ge(coef_step, 3 * g + 3)
                dve.wait_ge(y_ps, 2 * YG * g + i + 1)
                b, qt, cols = i // YG, (i // 2) % QT, slice((i % 2) * BANK, (i % 2 + 1) * BANK)
                y_b = (y0, y)[b]
                V.scalar_tensor_tensor(out=y_b[:, qt, cols], in0=OUT_PAIRED[i % 2][:, :], scalar=coef_p[:, b * QT + qt:b * QT + qt + 1],
                                       in1=y_b[:, qt, cols], op0=ALU.mult, op1=ALU.add).then_inc(y_sb, 1)

            def attend_paired():
                count[0], norms[0] = INIT_STEPS, 0

                def kq(g, part_):
                    dve.wait_ge(kq_hi, 3 * g + part_ + 1)
                    if part_ == 0:
                        ins = less(kT_p[:, LO, :], proj_ps[0][:, :], kT_p[:, HI, :])
                    else:
                        cols = slice((part_ - 1) * S, part_ * S)
                        ins = less(qT_p[:, LO, cols], proj_ps[part_ % 2][:, :], qT_p[:, HI, cols], SCALE)
                    ins.then_inc(kq_lo, 1)

                def start_group(k):
                    dve.wait_ge(start_hi, k + 1)
                    dst = start_dst(k)
                    less(dst[:, LO], START_PAIRED[k % 4].rearrange("p (c n) -> p c n", n=P), dst[:, HI]).then_inc(start_lo, 1)

                def normal(t):
                    if t >= 2:
                        dve.wait_ge(start_ps, 2 * (t - 1) + (8 if t >= QT + 2 else 0))
                    normalise(xn_stage[:, t % 2, :], (y0, y)[t // QT][:, t % QT, :], t // QT, t % QT).then_inc(xn_done, 1)

                def score(g, t):
                    if t == 0:
                        dve.wait_ge(p_turned, 4 * g)
                    dve.wait_ge(score_done, T * g + t + 1)
                    dve.wait_ge(bias_masked, T * g + t + 1)
                    dve.sem_inc(went_on["dve"], 1)
                    V.tensor_tensor_reduce(probs_p[:, t, :], score_half[t % 2][:, 0:QUARTER], bias_p[:, t % 4, :], -1.0, NO_SCORE,
                                           ALU.add, ALU.min, negmax_p[:, t:t + 1]).then_inc(score_sb, 1)

                def v_all(g):
                    dve.wait_ge(v_hi, g + 1)
                    less(v_p[:, LO, :, :].rearrange("p t d -> p (t d)"), turn_ps[0][:, :],
                         v_p[:, HI, :, :].rearrange("p t d -> p (t d)")).then_inc(v_lo, 1)

                def pT_tile(g, n):
                    dve.wait_ge(pT_hi, 4 * g + n + 1)
                    less(pT[:, n % 2, LO, :], turn_ps[n % 2][:, :], pT[:, n % 2, HI, :]).then_inc(pT_lo, 1)

                def make_coef(g):
                    dve.wait_ge(exp_done, T * g + T)
                    V.tensor_scalar(safe_sum_p, rowsum_p, LEAST_SUM, None, ALU.max).then_inc(coef_step, 1)
                    dve.wait_ge(coef_step, 3 * g + 1)
                    V.reciprocal(recip_p, safe_sum_p).then_inc(coef_step, 1)
                    dve.wait_ge(coef_step, 3 * g + 2)
                    V.tensor_scalar(coef_p, recip_p, scal[:, TG_X:TG_X + 1], None, ALU.mult).then_inc(coef_step, 1)

                def head(g, first, last):
                    if not first:
                        out_p(g - 1, 1)
                    for i in range(2 * YG):
                        if i % 2 == 0:
                            score(g, i // 2)
                        if not first:
                            add_p(g - 1, i)
                        if not last and i == 3:
                            weight("k", g + 1)
                        if not last and i == 7:
                            weight("q", g + 1)
                    v_all(g)
                    make_coef(g)

                    def fill(n):
                        if last:
                            for k in FILLS_PAIRED[n]:
                                take(k)

                    fill(0)
                    pT_tile(g, 0)
                    pT_tile(g, 1)
                    if not last:
                        weight("v", g + 1)
                    for n in range(4):
                        if n < 3:
                            fill(n + 1)
                        if n < 2:
                            pT_tile(g, n + 2)
                        if not last and n in KQ_AT_PAIRED:
                            kq(g + 1, KQ_AT_PAIRED[n])
                        if n == 0:
                            weight("o", g)
                        if n == 1:
                            out_p(g, 0)

                for t in range(QT):
                    dve.wait_ge(x_load[t], DMA)
                    tile_stats(norm, y0, t, 0)
                weight("k", 0)
                make_rstd(norm, 0, std_done, 1)
                normal(0)
                normal(1)
                for t in range(QT):
                    start_group(2 * t)
                    start_group(2 * t + 1)
                    if t + 2 < QT:
                        normal(t + 2)
                for k in range(8, 16):
                    start_group(k)
                weight("q", 0)
                weight("v", 0)
                kq(0, 0)
                dve.wait_ge(y_load, DMA)
                for t in range(QT):
                    tile_stats(norm, y, t, 1)
                make_rstd(norm, 1, std_done, 2)
                kq(0, 1)
                normal(QT)
                normal(QT + 1)
                dve.wait_ge(mask_load, DMA * B)
                V.tensor_scalar(hide_p[:, :, :], mask_p[:, :, :], 0.0, MASKED, ALU.is_equal, ALU.mult).then_inc(hide_done, 1)
                for t in range(QT):
                    start_group(16 + 2 * t)
                    start_group(17 + 2 * t)
                    if t + 2 < QT:
                        normal(QT + t + 2)
                kq(0, 2)
                run_paired(dve, head)

            def make_plan():
                def plan_it(n, ins):
                    ins.then_inc(plan_step, 1)
                    dve.wait_ge(plan_step, n)

                dve.wait_ge(mask_all_load, DMA)
                words = mask_all[:, :, :, :].bitcast(I32)
                W4 = QUARTER // 4
                for b in range(B):
                    for q in range(4):
                        V.tensor_reduce(seen[:, 4 * b + q:4 * b + q + 1], words[:, b, :, q * W4:(q + 1) * W4],
                                        AX_XY, ALU.max).then_inc(seen_done, 1)
                z, two, low, n_seen, first, m = (seen[:, 8 * n:8 * n + 8] for n in range(6))
                one = lambda row_, n: row_[:, n:n + 1]
                dve.wait_ge(seen_ps, 1)
                plan_it(1, V.tensor_scalar(z, out_ps[:, 0:4 * B], 0.0, None, ALU.is_gt))
                plan_it(2, V.tensor_tensor(two[:, 0:4], z[:, 0:8:2], z[:, 1:8:2], ALU.max))
                plan_it(3, V.tensor_tensor(low[:, 0:2], two[:, 0:4:2], two[:, 1:4:2], ALU.min))
                plan_it(4, V.tensor_tensor(one(m, 0), one(low, 0), one(low, 1), ALU.max))
                plan_it(5, V.tensor_tensor(n_seen[:, 0:4], z[:, 0:8:2], z[:, 1:8:2], ALU.add))
                plan_it(6, V.tensor_tensor(n_seen[:, 4:6], n_seen[:, 0:4:2], n_seen[:, 1:4:2], ALU.add))
                plan_it(7, V.tensor_tensor(one(m, 1), one(n_seen, 4), one(n_seen, 5), ALU.max))
                plan_it(8, V.tensor_scalar(one(m, 2), one(m, 1), 1.0, None, ALU.is_gt))
                plan_it(9, V.tensor_tensor(plan[:, MODE:MODE + 1], one(m, 2), one(m, 0), ALU.add))
                plan_it(10, V.tensor_scalar(plan[:, FIRST_KEY:FIRST_KEY + B], two[:, 0:4:2], 0.0, float(BANK), ALU.is_le, ALU.mult))
                plan_it(11, V.tensor_scalar(plan[:, FIRST_TILE:FIRST_TILE + B], two[:, 0:4:2], 0.0, float(HT), ALU.is_le, ALU.mult))
                plan_it(12, V.scalar_tensor_tensor(out=first[:, 0:2], in0=two[:, 1:4:2], scalar=2.0, in1=z[:, 1:8:4],
                                                   op0=ALU.mult, op1=ALU.add))
                plan_it(13, V.tensor_tensor(first[:, 2:4], first[:, 0:2], z[:, 3:8:4], ALU.add))
                plan_it(14, V.tensor_scalar(plan[:, QUARTER_KEY:QUARTER_KEY + B], first[:, 2:4], 3.0, float(QUARTER), ALU.min, ALU.mult))
                plan_it(15, V.tensor_scalar(plan[:, QUARTER_TILE:QUARTER_TILE + B], first[:, 2:4], 3.0, float(QUARTER // P),
                                            ALU.min, ALU.mult))

            step(V.memset(scal[:, EPS_C:EPS_C + 1], EPS), wait=False)
            step(V.memset(ones[:, :], 1.0), "init")
            assert count[0] == INIT_STEPS
            make_plan()
            dve.wait_ge(gate_done, 1)
            mode = dve.value_load(plan[0:1, MODE:MODE + 1], min_val=0, max_val=2)
            with dve.If(mode == PAIRED):
                follow(True)
                attend_paired()
                rest(True)
            with dve.Else():
                follow(False)
                with dve.If(mode == BOTH_HALVES):
                    attend(2)
                with dve.Else():
                    attend(1)
                rest(False)

        @block.tensor
        def _(pe):
            def turn_blocks(dst, blocks):
                for n, blk in enumerate(blocks):
                    last = pe.transpose(dst[:, n * P:(n + 1) * P], blk, ident[:])
                return last

            def product(dst, pairs):
                for n, (a, b) in enumerate(pairs):
                    mm = pe.matmul(dst, a, b, start=(n == 0), stop=(n == len(pairs) - 1))
                return mm

            def split_product(dst, stationary, moving, chunks=(0,)):
                return product(dst, [(stationary(a, c), moving(b, c)) for c in chunks for a, b in PASSES])

            def project(dst, m, src, cols, n):
                c, (a, b) = n // 3, PASSES[n % 3]
                return pe.matmul(dst[:, 0:BANK], w[m][:, a, c * DH:(c + 1) * DH], src[:, b, c, cols],
                                 start=(n == 0), stop=(n == 3 * NC - 1))

            def out_group(g, i, banks=1):
                if i == 0:
                    pe.wait_ge(oT_lo, g + 1)
                    pe.wait_ge(weight_lo["o"], g + 1)
                pe.wait_ge(y_sb, YG * g + i - (banks - 1 if i else 0))
                qt, n = i // 2, i % 2
                split_product(OUT_BANKS[banks][i % banks][:, :], lambda a, c: oT[:, a, qt * P:(qt + 1) * P],
                              lambda b, c: w["o"][:, b, n * BANK:(n + 1) * BANK]).then_inc(y_ps, 1)

            def turn(k):
                need, blocks, _, parts, _ = F["order"][k]
                if k < 2:
                    pe.wait_ge(score_sb, QT * ALL)
                elif F["order"][k - 2][4]:
                    pe.wait_ge(turned_lo, splits(k - 1))
                else:
                    pe.wait_ge(turned_hi, k - 1)
                if isinstance(need, int):
                    pe.wait_ge(dve_step, F["mark"][f"h{need}"])
                elif need == "prob":
                    pe.wait_ge(prob_done, QT if k < P1 else T)
                else:
                    arrived(pe, need)
                col = 0
                for blk, n in blocks:
                    mm = pe.transpose(F_TURN[k % 2][0:parts, col:col + n], blk, ident[0:n, 0:n])
                    col += n
                mm.then_inc(turned, 1)

            def router(n):
                if n == 0:
                    pe.wait_ge(turned_hi, HEAD_OF_H)
                    product(F_QUERY[0:RDIM, 0:NSLOT], [(wrT[:, :], keysT[:, :])]).then_inc(product_ps, 1)
                else:
                    pe.wait_ge(act_step, act_mark["rk"])
                    product(F_QUERY[0:BOT, 0:NSLOT], [(wr_in[:, :], rkT[:, :])]).then_inc(product_ps, 1)

            def f_fill(i):
                for k in FILLS[i]:
                    turn(k)
                if i in (3, 4):
                    router(i - 3)

            def query_chunk(half, c):
                if c == 0:
                    pe.wait_ge(turned_lo, splits(F["H0"] + GX if half == 0 else P0))
                    pe.wait_ge(act_step, act_mark["router" if half == 0 else "query0"])
                for n, (a, b) in enumerate(PASSES):
                    mm = pe.matmul(F_QUERY[0:BOT, :], wqT[:, a, c, :], hT[:, b, c, :],
                                   start=(c == 0 and n == 0), stop=(c == NC - 1 and n == 2))
                if c == NC - 1:
                    mm.then_inc(query_ps, 1)

            def units(half, u):
                if half:
                    pe.wait_ge(gelu_done, UT)
                else:
                    pe.wait_ge(oT_lo, ALL)
                split_product(F_UNITS[u][:, :], lambda a, c: wuT[:, a, c, u * P:(u + 1) * P],
                              lambda b, c: hT[:, b, c, :], range(NC)).then_inc(unit_ps, 1)

            def slot_scores(half):
                if half == 0:
                    arrived(pe, "rows")
                    pe.wait_ge(dve_step, F["mark"]["ones"])
                    pe.wait_ge(act_step, act_mark["slots"])
                pe.wait_ge(act_step, act_mark[f"query{half}"])
                for t in range(QT):
                    tile = half * QT + t
                    if tile >= 2:
                        pe.wait_ge(slot_sb, tile - 1)
                    pe.matmul(F_SCORES[t % 2][:, :], queryT[:, t * P:(t + 1) * P], slots[:, :, :].rearrange("p a n -> p (a n)"),
                              start=True, stop=True).then_inc(slot_ps, 1)

            def learned(half):
                pe.wait_ge(gelu_done, UT * (half + 1))
                for t in range(QT):
                    tile = half * QT + t
                    mm = product(F_MISC[:, P + tile:P + tile + 1],
                                 [(gelu[:, u, t * P:(t + 1) * P], wu2[:, u:u + 1]) for u in range(UT)])
                return mm

            def mix(half):
                pe.wait_ge(turned_hi, P1 if half == 0 else END)
                if half:
                    pe.wait_ge(mix_lo, 1)
                else:
                    pe.wait_ge(act_step, act_mark["query1"])
                product(F_QUERY[0:VB, :], [(values[:, s, :], probT[:, s, :]) for s in range(ST)]).then_inc(mix_ps, 1)

            def memory_out(half):
                pe.wait_ge(mix_lo, half + 1)
                for t in range(QT):
                    tile = half * QT + t
                    for n in range(2):
                        if tile:
                            pe.wait_ge(out_done, 2 * tile - 1 + n)
                        else:
                            pe.wait_ge(slot_sb, T)
                        split_product(F_SCORES[n][:, :], lambda a, c: mixT[:, half, a, t * P:(t + 1) * P],
                                      lambda b, c: wvuT[:, b, n * BANK:(n + 1) * BANK]).then_inc(aux_ps, 1)

            def small_values():
                pe.wait_ge(turned_hi, F["SMALL"])
                pe.wait_ge(y_sb, YG * ALL)
                for s in range(ST):
                    mm = product(F_MISC[:, s * VB:(s + 1) * VB], [(avT[:, c, s * P:(s + 1) * P], wvdT[:, c, :]) for c in range(NC)])
                mm.then_inc(product_ps, 1)

            def rest(paired):
                if paired:
                    for i in range(2 * YG):
                        out_p(H - 1, i)
                        if i == 3:
                            router(0)
                        if i == YG:
                            router(1)
                        if i >= YG:
                            turn(F["H0"] + i - YG)
                    for c in range(NC):
                        query_chunk(0, c)
                    pe.wait_ge(y_sb, YG * ALL)
                    small_values()
                    slot_scores(0)
                    for u in range(UT):
                        units(0, u)
                else:
                    query_chunk(0, 0)
                    query_chunk(0, 1)
                    for i in range(YG):
                        out_group(ALL - 1, i)
                        if i + 2 < NC:
                            query_chunk(0, i + 2)
                    for u in range(UT):
                        units(0, u)
                    slot_scores(0)
                    for k in range(FILLS[-1][-1] + 1, H1):
                        turn(k)
                    small_values()
                for k in range(H1, P0):
                    turn(k)
                for c in range(NC):
                    query_chunk(1, c)
                pe.wait_ge(act_step, act_mark["logvar"])
                learned(0)
                product(F_MISC[:, P + 32:P + 32 + T], [(ones[:, :], token[:, LOGVAR, :])]).then_inc(learned_ps, 1)
                slot_scores(1)
                units(1, 0)
                for k in range(P0, P1):
                    turn(k)
                mix(0)
                units(1, 1)
                for k in range(P1, END):
                    turn(k)
                pe.wait_ge(dve_step, F["mark"]["sum"])
                learned(1).then_inc(learned_ps, 1)
                mix(1)
                memory_out(0)
                memory_out(1)

            def attend(halves):
                KT, W, GC, G, KQ = sizes(halves)
                out_banks = 3 - halves
                TURN_V = 7 - halves

                def kq(g, n, bank_free):
                    part_, n = n // (3 * NC), n % (3 * NC)
                    if n == 0:
                        pe.wait_ge(weight_lo["q" if part_ == halves else "k"], g + 1)
                        pe.wait_ge(*bank_free[part_])
                    if part_ < halves:
                        mm = project(K_BANK[part_], "k", ctxT, slice(part_ * BANK, (part_ + 1) * BANK), n)
                    else:
                        mm = project(Q_BANK[halves], "q", xnT, slice(0, S), n)
                    if n == 3 * NC - 1:
                        mm.then_inc(kq_ps, 1)

                def kq_chunk(b, part_, c):
                    g = b * H
                    if c == 0:
                        pe.wait_ge(start_lo, G * b + (G if part_ == halves else 2 * HT * (part_ + 1)))
                    if halves == 2:
                        free = ((kq_lo, 3 * g), (start_lo, G * b + GC), (kq_lo, 3 * g + 1))
                    else:
                        free = ((vT_sb, g), (start_lo, G * b + GC))
                    for n in range(3 * c, 3 * c + 3):
                        kq(g, part_ * 3 * NC + n, free)

                def start_group(b, k):
                    g, tile, half = b * H, k // 2, k % 2
                    before = start_bank_before(k, GC)
                    if before is not None:
                        pe.wait_ge(start_lo, G * b + before + 1)
                    elif b:
                        last_use = (vT_sb, 2 * g - 1) if halves == 2 else (y_sb, YG * (g - 1))
                        pe.wait_ge(*((score_sb, QT * g), (score_sb, QT * g), last_use, (pT_lo, KT * g), (pT_lo, KT * g))[start_bank(k, GC)])
                    if tile < KT:
                        pe.wait_ge(ctx_load[tile], DMA * (b + 1))
                        src = stage[:, tile, :]
                    else:
                        pe.wait_ge(xn_done, QT * b + tile - KT + 1)
                        src = probs[:, tile - KT, :]
                    turn_blocks(START_BANKS[start_bank(k, GC)],
                                [src[:, (4 * half + c) * P:(4 * half + c + 1) * P] for c in range(4)]).then_inc(start_ps, 1)

                def v_mms(g, half, ns):
                    if ns[0] == 0 and half == 0:
                        pe.wait_ge(weight_lo["v"], g + 1)
                        pe.wait_ge(kq_lo, KQ * g + halves)
                    if ns[0] == 0 and half == 1:
                        pe.wait_ge(oT_lo, g)
                    for n in ns:
                        mm = project(V_BANK[halves][half], "v", ctxT, slice(half * BANK, (half + 1) * BANK), n)
                    if ns[-1] == 3 * NC - 1:
                        mm.then_inc(v_ps, 1)

                def turn_v(g, half):
                    pe.wait_ge(vT_sb, halves * g + half + 1)
                    pe.wait_ge(pT_lo, KT * g)
                    if half == 0 and isinstance(g, int) and g % H == 0:
                        pe.wait_ge(start_lo, G * (g // H) + G)
                    turn_blocks(turn_ps[half], [vT[:, k * P:(k + 1) * P] for k in range(4)]).then_inc(v_turned, 1)

                def turn_p(g, kt):
                    if kt == 0:
                        pe.wait_ge(exp_done, QT * g + QT)
                    if kt < halves:
                        pe.wait_ge(v_lo, halves * g + kt + 1)
                    elif kt >= 2:
                        pe.wait_ge(pT_lo, KT * g + kt - 1)
                    turn_blocks(turn_ps[kt % 2], [probs[:, qt, kt * P:(kt + 1) * P] for qt in range(QT)]).then_inc(p_turned, 1)

                def pv(g, kt):
                    pe.wait_ge(pT_lo, KT * g + kt + 1)
                    if kt == 0:
                        pe.wait_ge(v_lo, halves * g + halves)
                        pe.wait_ge(vT_sb, halves * g + halves)
                    for a, b in PASSES:
                        mm = pe.matmul(head_ps[:, :], v[:, a, kt, :], pT[:, kt % 2, b, :],
                                       start=(kt == 0 and (a, b) == PASSES[0]), stop=(kt == KT - 1 and (a, b) == PASSES[-1]))
                    mm.then_inc(pv_done, 1)

                def start(b, g):
                    if b == 0:
                        for k in range(2 * HT):
                            start_group(b, k)
                        for c in range(NC):
                            if halves == 2:
                                start_group(b, 2 * HT + c)
                            kq_chunk(b, 0, c)
                        if halves == 2:
                            for c in range(NC):
                                kq_chunk(b, 1, c)
                    v_mms(g, 0, range(3 * NC))
                    for k in range(GC, G):
                        start_group(b, k)
                    for c in range(NC):
                        kq_chunk(b, halves, c)

                def head(g, first, last):
                    final = last and g == ALL - 1
                    for i in range(8):
                        qt, sh = i // 2, i % 2
                        if halves == 2 and not (first and i < 4):
                            v_mms(g, i // 4, range(6 * (i % 4), 6 * (i % 4) + 6))
                        if halves == 1 and not first and i < 6:
                            v_mms(g, 0, range(4 * i, 4 * i + 4))
                        if i == 0:
                            pe.wait_ge(kq_lo, KQ * g + KQ)
                            if first:
                                pe.wait_ge(start_lo, G * (g // H) + G)
                        if halves == 1:
                            if sh == 0:
                                if not first or qt >= 2:
                                    pe.wait_ge(score_sb, QT * g + qt - 1)
                                split_product(score_half[qt % 2], lambda a, c: qT[:, a, qt * P:(qt + 1) * P],
                                              lambda b, c: kT[:, b, 0:BANK]).then_inc(score_done, 1)
                        else:
                            if sh == 0:
                                pe.wait_ge(score_sb, QT * g + qt)
                            mm = split_product(score_half[sh], lambda a, c: qT[:, a, qt * P:(qt + 1) * P],
                                               lambda b, c: kT[:, b, sh * BANK:(sh + 1) * BANK])
                            if sh:
                                mm.then_inc(score_done, 1)
                        if not first:
                            out_group(g - 1, i, out_banks)
                        if i == TURN_V:
                            turn_v(g, 0)
                    if halves == 2:
                        turn_v(g, 1)

                    def fill(i):
                        if final:
                            for n in ((i,) if halves == 2 else (2 * i, 2 * i + 1)):
                                f_fill(n)
                        elif last:
                            for k in (2 * i, 2 * i + 1):
                                start_group(1, k)
                            if i >= 4:
                                for c in (2 * (i - 4), 2 * (i - 4) + 1):
                                    kq_chunk(1, 0, c)
                        else:
                            if halves == 2:
                                free = ((kq_lo, 3 * g + 3), (vT_sb, 2 * g + 1), (kq_lo, 3 * g + 4))
                            else:
                                free = ((vT_sb, g + 1), (y_sb, YG * g))
                            share = 3 * NC * KQ // KT
                            for n in range(share * i, share * i + share):
                                kq(g + 1, n, free)

                    fill(0)
                    turn_p(g, 0)
                    turn_p(g, 1)
                    for kt in range(KT):
                        if kt + 1 < KT:
                            fill(kt + 1)
                        pv(g, kt)
                        if kt + 2 < KT:
                            turn_p(g, kt + 2)
                    if last and not final:
                        kq_chunk(1, halves - 1, 0)
                        for i in range(YG):
                            if i + 1 < NC:
                                kq_chunk(1, halves - 1, i + 1)
                            out_group(g, i)

                run_heads(pe, start, head)

            def out_p(g, i):
                b, qt, n = i // YG, (i // 2) % QT, i % 2
                if i % YG == 0:
                    pe.wait_ge(oT_lo, 2 * g + b + 1)
                if i == 0:
                    pe.wait_ge(weight_lo["o"], g + 1)
                pe.wait_ge(y_sb, 2 * YG * g + i - (1 if i else 0))
                split_product(OUT_PAIRED[i % 2][:, :], lambda a, c: oT_p[b][:, a, qt * P:(qt + 1) * P],
                              lambda h, c: w["o"][:, h, n * BANK:(n + 1) * BANK]).then_inc(y_ps, 1)

            def attend_paired():
                def kq(g, n, bank_free):
                    part_, n = n // (3 * NC), n % (3 * NC)
                    if n == 0:
                        pe.wait_ge(weight_lo["q" if part_ else "k"], g + 1)
                        if bank_free[part_]:
                            pe.wait_ge(*bank_free[part_])
                    if part_ == 0:
                        mm = project(proj_ps[0], "k", ctxT_p, slice(0, BANK), n)
                    else:
                        mm = project(proj_ps[part_ % 2], "q", xnT_p, slice((part_ - 1) * S, part_ * S), n)
                    if n == 3 * NC - 1:
                        mm.then_inc(kq_ps, 1)

                def v_mms(g, ns, first=False):
                    if ns[0] == 0:
                        pe.wait_ge(weight_lo["v"], g + 1)
                        pe.wait_ge(kq_lo, 1 if first else 3 * g + 3)
                    for n in ns:
                        mm = project(proj_ps[0], "v", ctxT_p, slice(0, BANK), n)
                    if ns[-1] == 3 * NC - 1:
                        mm.then_inc(v_ps, 1)

                def start_group(k):
                    if k >= 4:
                        pe.wait_ge(start_lo, k - 3)
                    if 8 <= k < 16:
                        pe.wait_ge(ctx_load[(k - 8) // 2], DMA)
                        src = stage_p[(k - 8) // 4][:, (k // 2) % 2, :]
                    else:
                        t = k // 2 if k < 8 else k // 2 - 4
                        pe.wait_ge(xn_done, t + 1)
                        src = xn_stage[:, t % 2, :]
                    c = 4 * (k % 2)
                    turn_blocks(START_PAIRED[k % 4], [src[:, (c + n) * P:(c + n + 1) * P] for n in range(4)]).then_inc(start_ps, 1)

                def turn_p(g, n):
                    if n == 0:
                        pe.wait_ge(exp_done, T * g + T)
                        pe.wait_ge(v_lo, g + 1)
                    if n >= 2:
                        pe.wait_ge(pT_lo, 4 * g + n - 1)
                    b, kt = n // 2, n % 2
                    turn_blocks(turn_ps[n % 2], [probs_p[:, b * QT + qt, kt * P:(kt + 1) * P] for qt in range(QT)]).then_inc(p_turned, 1)

                def pv(g, n):
                    b, kt = n // 2, n % 2
                    pe.wait_ge(pT_lo, 4 * g + n + 1)
                    if n == 0:
                        pe.wait_ge(y_sb, 2 * YG * g)
                    for a, h in PASSES:
                        mm = pe.matmul(PV_BANKS[b][:, :], v_p[:, a, n, :], pT[:, n % 2, h, :],
                                       start=(kt == 0 and (a, h) == PASSES[0]), stop=(kt == 1 and (a, h) == PASSES[-1]))
                    mm.then_inc(pv_done, 1)

                def head(g, first, last):
                    for i in range(2 * YG):
                        t = i // 2
                        if not first and i < 12:
                            v_mms(g, range(2 * i, 2 * i + 2))
                        if i == 0:
                            pe.wait_ge(kq_lo, 3 * g + 3)
                            if first:
                                pe.wait_ge(start_lo, 24)
                        if i % 2 == 0:
                            if not first or t >= 2:
                                pe.wait_ge(score_sb, T * g + t - 1)
                            b = t // QT
                            split_product(score_half[t % 2][:, 0:QUARTER], lambda a, c: qT_p[:, a, t * P:(t + 1) * P],
                                          lambda h, c: kT_p[:, h, b * QUARTER:(b + 1) * QUARTER]).then_inc(score_done, 1)
                        if not first:
                            out_p(g - 1, i)
                    pe.wait_ge(vT_sb, g + 1)
                    pe.wait_ge(pT_lo, 4 * g)
                    turn_blocks(turn_ps[0], [vT[:, k * P:(k + 1) * P] for k in range(4)]).then_inc(v_turned, 1)

                    def fill(n):
                        if last:
                            for k in FILLS_PAIRED[n]:
                                turn(k)
                        else:
                            free = ((vT_sb, g + 1), (y_sb, 2 * YG * g), (kq_lo, 3 * g + 4))
                            for m in range(18 * n, 18 * n + 18):
                                kq(g + 1, m, free)

                    fill(0)
                    turn_p(g, 0)
                    turn_p(g, 1)
                    for n in range(4):
                        if n < 3:
                            fill(n + 1)
                        pv(g, n)
                        if n < 2:
                            turn_p(g, n + 2)

                for k in range(16):
                    start_group(k)
                free = (None, None, (vT_sb, 1))
                pe.wait_ge(start_lo, 16)
                for n in range(3 * NC):
                    kq(0, n, free)
                for n in range(3 * NC, 6 * NC):
                    kq(0, n, free)
                v_mms(0, range(3 * NC), True)
                for k in range(16, 24):
                    start_group(k)
                pe.wait_ge(start_lo, 24)
                for n in range(6 * NC, 9 * NC):
                    kq(0, n, free)
                run_paired(pe, head)

            pe.wait_ge(dve_step, INIT_STEPS)
            pe.wait_ge(seen_done, 4 * B)
            pe.matmul(out_ps[:, 0:4 * B], ones[:, :], seen[:, 0:4 * B], start=True, stop=True).then_inc(seen_ps, 1)
            pe.wait_ge(ident_done, 2)
            pe.wait_ge(plan_step, PLANNED)
            mode = pe.value_load(plan[0:1, MODE:MODE + 1], min_val=0, max_val=2)
            with pe.If(mode == PAIRED):
                follow(True)
                attend_paired()
                rest(True)
            with pe.Else():
                follow(False)
                with pe.If(mode == BOTH_HALVES):
                    attend(2)
                with pe.Else():
                    attend(1)
                rest(False)

        @block.scalar
        def _(act):
            A = nc.scalar
            count = [0]

            def step(ins, name):
                count[0] += 1
                ins.then_inc(act_step, 1)
                assert act_mark[name] == count[0], (name, count[0])

            def copy(dst, src, scale=1.0):
                return A.activation(dst, src, ACT.Copy, scale=scale)

            def weight(m, g, free):
                act.wait_ge(weight_in[m], DMA * g + DMA)
                act.wait_ge(*free)
                copy(w[m][:, HI, :], raw[:, WSLOT[m], :]).then_inc(weight_hi[m], 1)

            def take(k):
                act.wait_ge(turned, k + 1)
                if k == P1:
                    act.wait_ge(mix_ps, 1)
                if k == H1:
                    act.wait_ge(unit_ps, UT)
                    act.wait_ge(query_ps, 1)
                copy(F["order"][k][2](HI), f_source(k)).then_inc(turned_hi, 1)

            def std(half):
                act.wait_ge(dve_step, F["mark"][f"var{half}"])
                cols = slice(half * QT, half * QT + QT)
                step(A.activation(token[:, STD, cols], var_of(half), ACT.Sqrt, bias=scal[:, EPS_C:EPS_C + 1]), f"std{half}")

            def router(n):
                act.wait_ge(product_ps, n + 1)
                if n == 0:
                    step(copy(rkT[:, :], F_QUERY[0:RDIM, 0:NSLOT]), "rk")
                else:
                    act.wait_ge(weight_lo["o"], H if F["order"] is order_paired else ALL)
                    step(copy(slots[0:BOT, 0, :], F_QUERY[0:BOT, 0:NSLOT], float(RDIM) ** -0.5), "router")
                    step(copy(slots[0:BOT, 1, :], keysT[:, :], float(BOT) ** -0.5), "slots")

            def f_fill(i):
                for k in FILLS[i]:
                    take(k)
                if i in (3, 4):
                    router(i - 3)

            def query(half):
                act.wait_ge(query_ps, half + 1)
                if half:
                    act.wait_ge(slot_ps, QT)
                step(copy(queryT[0:BOT, :], F_QUERY[0:BOT, :]), f"query{half}")

            def slot_tiles(half):
                for t in range(QT):
                    act.wait_ge(slot_ps, half * QT + t + 1)
                    if half:
                        act.wait_ge(dve_step, F["mark"][f"attn{t}"])
                    copy(scores[:, t, :, :].rearrange("p a n -> p (a n)"), F_SCORES[t % 2][:, :]).then_inc(slot_sb, 1)

            def units(half, u):
                act.wait_ge(unit_ps, half * UT + u + 1)
                if half:
                    act.wait_ge(learned_ps, 1)
                A.activation(gelu[:, u, :], F_UNITS[u][:, :], ACT.Gelu_apprx_tanh, bias=bu[:, u:u + 1]).then_inc(gelu_done, 1)

            def weigh(half):
                for t in range(QT):
                    tile = half * QT + t
                    act.wait_ge(dve_step, F["mark"][f"attn{tile}"])
                    if half and t == 0:
                        act.wait_ge(turned, P1)
                    A.activation(prob[:, t, :], attn[:, t, :], ACT.Exp, bias=negmax_f[:, t:t + 1],
                                 accum_out=token[:, TOTAL, tile:tile + 1]).then_inc(prob_done, 1)

            def sig(half):
                act.wait_ge(learned_ps, half + 1)
                cols = slice(half * QT, half * QT + QT)
                step(A.activation(token[:, SIG, cols], F_MISC[:, P + half * QT:P + half * QT + QT], ACT.Tanh, scale=0.5,
                                  bias=scal[:, HALF_BU2:HALF_BU2 + 1]), f"sig{half}")

            def gate(half):
                act.wait_ge(dve_step, F["mark"][f"gate_in{half}"])
                cols = slice(half * QT, half * QT + QT)
                step(A.activation(token[:, GATE, cols], token[:, V2, cols], ACT.Tanh, scale=0.5), f"gate{half}")

            def mix(half):
                act.wait_ge(mix_ps, half + 1)
                copy(mixT[:, half, HI, :], F_QUERY[0:VB, :]).then_inc(mix_hi, 1)

            def rest(paired):
                arrived(act, "small")
                A.activation(scal[:, TG_F:TG_F + 1], scal[:, G_F:G_F + 1], ACT.Tanh).then_inc(gate_done, 1)
                copy(scal[:, HALF_BU2:HALF_BU2 + 1], scal[:, BU2:BU2 + 1], 0.5).then_inc(gate_done, 1)
                if paired:
                    std(0)
                    router(0)
                    router(1)
                    for k in range(F["H0"], H1):
                        take(k)

                def small_values():
                    act.wait_ge(product_ps, 3)
                    step(copy(values[:, :, :].rearrange("p s v -> p (s v)"), F_MISC[:, 0:ST * VB]), "values")

                def logvar():
                    act.wait_ge(dve_step, F["mark"]["var_h"])
                    step(A.activation(token[:, LOGVAR, :], token[:, U, :], ACT.Ln, bias=ones[:, 0:1]), "logvar")

                std(1)
                query(0)
                if paired:
                    small_values()
                    slot_tiles(0)
                    logvar()
                for u in range(UT):
                    units(0, u)
                if not paired:
                    slot_tiles(0)
                if not paired:
                    for k in range(FILLS[-1][-1] + 1, H1):
                        take(k)
                    small_values()
                    logvar()
                for k in range(H1, P0):
                    take(k)
                weigh(0)
                query(1)
                sig(0)
                slot_tiles(1)
                gate(0)
                units(1, 0)
                for k in range(P0, P1):
                    take(k)
                mix(0)
                weigh(1)
                units(1, 1)
                for k in range(P1, END):
                    take(k)
                sig(1)
                mix(1)
                gate(1)

            act.wait_ge(g_in, DMA)
            A.activation(scal[:, TG_X:TG_X + 1], scal[:, G_X:G_X + 1], ACT.Tanh).then_inc(gate_done, 1)
            def attend(halves):
                KT, W, GC, G, KQ = sizes(halves)
                count[0] = 0

                def kq(g, part_):
                    act.wait_ge(kq_ps, KQ * g + part_ + 1)
                    act.wait_ge(score_done, QT * g)
                    if part_ < halves:
                        ins = copy(kT[:, HI, part_ * BANK:(part_ + 1) * BANK], K_BANK[part_][:, :])
                    else:
                        ins = copy(qT[:, HI, :], Q_BANK[halves][:, :], SCALE)
                    ins.then_inc(kq_hi, 1)

                def start_group(b, k):
                    act.wait_ge(start_ps, G * b + k + 1)
                    if k == 0:
                        act.wait_ge(v_ps, halves * H * b)
                    if k == GC:
                        act.wait_ge(kq_ps, KQ * H * b)
                    tile, c = k // 2, 4 * (k % 2)
                    dst = (ctxT[:, HI, c:c + 4, tile * P:(tile + 1) * P] if tile < KT
                           else xnT[:, HI, c:c + 4, (tile - KT) * P:(tile - KT + 1) * P])
                    copy(dst, START_BANKS[start_bank(k, GC)].rearrange("p (c n) -> p c n", n=P)).then_inc(start_hi, 1)

                def start(b, g):
                    if b == 0:
                        weight("k", 0, (kq_ps, 0))
                        for k in range(GC):
                            start_group(b, k)
                        weight("v", 0, (v_ps, 0))
                        kq(g, 0)
                        weight("q", 0, (kq_ps, 0))
                    if b or halves == 2:
                        kq(g, halves - 1)
                    act.wait_ge(norm_step, STATS_STEPS + b * (STATS_STEPS + RSTD_STEPS))
                    A.activation(token[:, STD, 0:QT], var_of(0), ACT.Sqrt, bias=scal[:, EPS_C:EPS_C + 1]).then_inc(std_done, 1)
                    vT_half(g, 0)
                    for k in range(GC, G):
                        start_group(b, k)
                    kq(g, halves)

                def head_out(g):
                    act.wait_ge(pv_done, KT * g + KT)
                    act.wait_ge(y_ps, YG * g)
                    copy(oT[:, HI, :], head_ps[:, :]).then_inc(oT_hi, 1)

                def exp(g, qt):
                    act.wait_ge(score_sb, QT * g + qt + 1)
                    if qt == 0:
                        act.wait_ge(coef_step, 3 * g)
                    A.activation(probs[:, qt, 0:W], probs[:, qt, 0:W], ACT.Exp, bias=negmax[:, qt:qt + 1], scale=-1.0,
                                 accum_out=rowsum[:, qt:qt + 1]).then_inc(exp_done, 1)

                def vT_half(g, half):
                    act.wait_ge(v_ps, halves * g + half + 1)
                    act.wait_ge(v_turned, halves * g + half)
                    copy(vT[:, :], V_BANK[halves][half][:, :]).then_inc(vT_sb, 1)

                def v_half(g, half):
                    act.wait_ge(v_turned, halves * g + half + 1)
                    act.wait_ge(pv_done, KT * g)
                    copy(v[:, HI, 4 * half:4 * half + 4, :].rearrange("p t d -> p (t d)"), turn_ps[half][:, :]).then_inc(v_hi, 1)

                def pT_tile(g, kt):
                    act.wait_ge(p_turned, KT * g + kt + 1)
                    act.wait_ge(pv_done, KT * g + max(kt - 1, 0))
                    copy(pT[:, kt % 2, HI, :], turn_ps[kt % 2][:, :]).then_inc(pT_hi, 1)

                def head(g, first, last):
                    final = last and g == ALL - 1
                    if not first:
                        head_out(g - 1)
                    if not final:
                        weight("k", g + 1, (kq_ps, KQ * g + halves))
                    exp(g, 0)
                    if halves == 2 and not first:
                        vT_half(g, 0)
                    exp(g, 1)
                    if not final:
                        weight("q", g + 1, (kq_ps, KQ * g + KQ))
                    exp(g, 2)
                    if halves == 2:
                        v_half(g, 0)
                    elif not first:
                        vT_half(g, 0)
                    if final:
                        std(0)
                    if halves == 2:
                        vT_half(g, 1)
                    exp(g, 3)
                    v_half(g, halves - 1)

                    def fill(i):
                        if final:
                            for n in ((i,) if halves == 2 else (2 * i, 2 * i + 1)):
                                f_fill(n)
                        elif last:
                            start_group(1, 2 * i)
                            start_group(1, 2 * i + 1)

                    fill(0)
                    pT_tile(g, 0)
                    pT_tile(g, 1)
                    if not final:
                        weight("v", g + 1, (v_ps, halves * (g + 1)))
                    for kt in range(KT):
                        if kt + 1 < KT:
                            fill(kt + 1)
                        if kt + 2 < KT:
                            pT_tile(g, kt + 2)
                        if not last and kt in KQ_AT[halves]:
                            kq(g + 1, KQ_AT[halves][kt])
                        if kt == halves - 1:
                            weight("o", g, (y_ps, YG * g))
                    if last:
                        if not final and halves == 2:
                            kq(g + 1, 0)
                        head_out(g)

                run_heads(act, start, head)

            def attend_paired():
                count[0] = 0

                def kq(g, part_):
                    act.wait_ge(kq_ps, 3 * g + part_ + 1)
                    act.wait_ge(score_done, T * g)
                    if part_ == 0:
                        ins = copy(kT_p[:, HI, :], proj_ps[0][:, :])
                    else:
                        ins = copy(qT_p[:, HI, (part_ - 1) * S:part_ * S], proj_ps[part_ % 2][:, :], SCALE)
                    ins.then_inc(kq_hi, 1)

                def start_group(k):
                    act.wait_ge(start_ps, k + 1)
                    copy(start_dst(k)[:, HI], START_PAIRED[k % 4].rearrange("p (c n) -> p c n", n=P)).then_inc(start_hi, 1)

                def head_out(g, b):
                    act.wait_ge(pv_done, 4 * g + 2 * b + 2)
                    act.wait_ge(y_ps, 2 * YG * g)
                    copy(oT_p[b][:, HI, :], PV_BANKS[b][:, :]).then_inc(oT_hi, 1)

                def exp(g, t):
                    act.wait_ge(score_sb, T * g + t + 1)
                    if t == 0:
                        act.wait_ge(coef_step, 3 * g)
                    A.activation(probs_p[:, t, :], probs_p[:, t, :], ACT.Exp, bias=negmax_p[:, t:t + 1], scale=-1.0,
                                 accum_out=rowsum_p[:, t:t + 1]).then_inc(exp_done, 1)

                def vT_all(g):
                    act.wait_ge(v_ps, g + 1)
                    act.wait_ge(v_turned, g)
                    copy(vT[:, :], proj_ps[0][:, :]).then_inc(vT_sb, 1)

                def v_all(g):
                    act.wait_ge(v_turned, g + 1)
                    act.wait_ge(pv_done, 4 * g)
                    copy(v_p[:, HI, :, :].rearrange("p t d -> p (t d)"), turn_ps[0][:, :]).then_inc(v_hi, 1)

                def pT_tile(g, n):
                    act.wait_ge(p_turned, 4 * g + n + 1)
                    act.wait_ge(pv_done, 4 * g + max(n - 1, 0))
                    copy(pT[:, n % 2, HI, :], turn_ps[n % 2][:, :]).then_inc(pT_hi, 1)

                def head(g, first, last):
                    if not first:
                        head_out(g - 1, 1)
                    if not last:
                        weight("k", g + 1, (kq_ps, 3 * g + 1))
                    for t in range(T):
                        exp(g, t)
                        if t == 2 and not last:
                            weight("q", g + 1, (kq_ps, 3 * g + 3))
                        if t == 5 and not first:
                            vT_all(g)
                    v_all(g)

                    def fill(n):
                        if last:
                            for k in FILLS_PAIRED[n]:
                                take(k)

                    fill(0)
                    pT_tile(g, 0)
                    pT_tile(g, 1)
                    if not last:
                        weight("v", g + 1, (v_ps, g + 1))
                    for n in range(4):
                        if n < 3:
                            fill(n + 1)
                        if n < 2:
                            pT_tile(g, n + 2)
                        if not last and n in KQ_AT_PAIRED:
                            kq(g + 1, KQ_AT_PAIRED[n])
                        if n == 0:
                            weight("o", g, (y_ps, 2 * YG * g))
                        if n == 1:
                            head_out(g, 0)
                    if last:
                        head_out(g, 1)

                def std_of(b):
                    act.wait_ge(norm_step, STATS_STEPS + b * (STATS_STEPS + RSTD_STEPS))
                    A.activation(token[:, STD, b * QT:(b + 1) * QT], var_of(b), ACT.Sqrt, bias=scal[:, EPS_C:EPS_C + 1]).then_inc(std_done, 1)

                weight("k", 0, (kq_ps, 0))
                std_of(0)
                for k in range(16):
                    start_group(k)
                weight("q", 0, (kq_ps, 0))
                weight("v", 0, (v_ps, 0))
                kq(0, 0)
                std_of(1)
                kq(0, 1)
                vT_all(0)
                for k in range(16, 24):
                    start_group(k)
                kq(0, 2)
                run_paired(act, head)

            act.wait_ge(plan_step, PLANNED)
            mode = act.value_load(plan[0:1, MODE:MODE + 1], min_val=0, max_val=2)
            with act.If(mode == PAIRED):
                follow(True)
                attend_paired()
                rest(True)
            with act.Else():
                follow(False)
                with act.If(mode == BOTH_HALVES):
                    attend(2)
                with act.Else():
                    attend(1)
                rest(False)


_INS = ["x", "ctx_4096", "fside_Bx32xSxS2_0", "mask_BxSxS2_bk0", "g_xattn", "g_ffn",
        "L0_xattn_Wq", "L0_xattn_Wk", "L0_xattn_Wv", "L0_xattn_Wo", "L0_ffn_Wq", "L0_ffn_Wr",
        "L0_ffn_aux_keys", "L0_ffn_aux_values", "L0_ffn_Wvd", "L0_ffn_Wvu", "L0_ffn_Wu1", "L0_ffn_bu1",
        "L0_ffn_Wu2", "L0_ffn_bu2", "L0_ffn_gate_w1", "L0_ffn_gate_bias", "L0_ffn_log_rel"]


def kernel(**inputs):
    import numpy as _np
    import concourse.bacc as _bacc
    from concourse import mybir as _mybir
    from concourse.bass_utils import run_bass_kernel_spmd as _run

    nc = _bacc.Bacc("TRN2", target_bir_lowering=False, num_devices=1, dynamic_dma_scratch_size=1024)
    arrays, args = {}, []
    for name in _INS:
        a = _np.ascontiguousarray(inputs[name])
        a = a.reshape(a.shape or (1,))
        arrays[f"in_{name}_dram"] = a
        args.append(nc.dram_tensor(f"in_{name}_dram", a.shape, _mybir.dt.from_np(a.dtype), kind="ExternalInput").ap())
    shape = inputs["x"].shape
    args.append(nc.dram_tensor("out_0_dram", shape, _mybir.dt.float32, kind="ExternalOutput").ap())
    program(nc, *args)
    r = _run(nc, [arrays], core_ids=[0])
    return r.results[0]["out_0_dram"]
```
